# Optimizing a Trainium2 kernel written in Bass

```python
import numpy as np
import jax
import jax.numpy as jnp

def _softmax(x, axis=-1):
    return jax.nn.softmax(x, axis=axis)

def _gelu(x):
    return jax.nn.gelu(x, approximate=True)

def _silu(x):
    return jax.nn.silu(x)

def _sigmoid(x):
    return jax.nn.sigmoid(x)

def _layernorm(x, axis=-1, eps=1e-05):
    m = jnp.mean(x, axis=axis, keepdims=True)
    v = jnp.var(x, axis=axis, keepdims=True)
    return (x - m) / jnp.sqrt(v + eps)

def _scatter_add(tgt, idx, src, axis=0):
    return tgt.at[idx].add(src)

def _segment_sum(src, seg, n):
    return jax.ops.segment_sum(src, seg, n)
kernel_name = 'mk_decoder_preln_d2_seqx_r4_8ad909'

def setup_inputs(seed: int=0):
    np.random.seed(seed)
    _w = jnp.asarray

    def _rec_inputs():
        import jax
        import jax.numpy as jnp
        _rk = jax.random.key(seed)
        x = -0.0003929 + 0.9999 * jax.random.normal(jax.random.fold_in(_rk, 1), (16, 128, 256), jnp.float32)
        _lenS = 128 - jax.random.randint(jax.random.fold_in(_rk, 7), (16,), 0, max(1, 128 // 4) + 1, jnp.int32)
        _lenS2 = 128 - jax.random.randint(jax.random.fold_in(_rk, 8), (16,), 0, max(1, 128 // 4) + 1, jnp.int32)
        _ctx_1024P = jax.random.normal(jax.random.fold_in(_rk, 11), (16, 16, 256), jnp.float32)
        _ctx_1024c = jax.random.dirichlet(jax.random.fold_in(_rk, 511), 0.3 * jnp.ones((16,), jnp.float32), (16, 128))
        _ctx_1024t = jnp.einsum('bsk,bkd->bsd', _ctx_1024c, _ctx_1024P)
        _ctx_1024t = _ctx_1024t * jax.lax.rsqrt(jnp.mean(jnp.square(_ctx_1024t)) + 1e-12) * 0.953939
        ctx_1024 = 2.81802e-05 + 1.00001 * (_ctx_1024t + 0.3 * jax.random.normal(jax.random.fold_in(_rk, 611), (16, 128, 256), jnp.float32))
        _validS = jnp.arange(128)[None, :] < _lenS[:, None]
        _validS2 = jnp.arange(128)[None, :] < _lenS2[:, None]
        _causal = jnp.tril(jnp.ones((128, 128), dtype=bool))
        mask_S2_ff1 = jnp.where(jnp.ones((128,), dtype=bool), 1.0, 0.0).astype(jnp.float32)
        mask_BxS2_bk0 = jnp.logical_not(jnp.broadcast_to(_validS2[:, :], (16, 128)))
        return (x, ctx_1024, mask_S2_ff1, mask_BxS2_bk0)
    x, ctx_1024, mask_S2_ff1, mask_BxS2_bk0 = _rec_inputs()

    def _L0_attn_setup():
        import jax, jax.numpy as jnp
        import numpy as np
        NUM_HEADS = 16
        CLIP = 16
        key = jax.random.key(seed)
        ks = jax.random.split(key, 7)
        d = 256
        return {'x': jax.random.normal(ks[0], (2, 512, d), dtype=jnp.float32), 'Wq': jax.random.normal(ks[1], (d, d), dtype=jnp.float32) / np.sqrt(d), 'Wk': jax.random.normal(ks[2], (d, d), dtype=jnp.float32) / np.sqrt(d), 'Wv': jax.random.normal(ks[3], (d, d), dtype=jnp.float32) / np.sqrt(d), 'Wo': jax.random.normal(ks[4], (d, d), dtype=jnp.float32) / np.sqrt(d), 'bo': jax.random.normal(ks[5], (d,), dtype=jnp.float32) * 0.01, 'rel_emb': jax.random.normal(ks[6], (CLIP + 1,), dtype=jnp.float32)}
    _L0_attn_all = _L0_attn_setup()
    _L0_attn_in = {k: v for k, v in _L0_attn_all.items() if k in ('Wq', 'Wk', 'Wv', 'Wo', 'bo', 'rel_emb')}
    del _L0_attn_all

    def _L0_xattn_setup():
        import jax, jax.numpy as jnp
        import numpy as np
        N_HEADS = 16
        LEVELS = 3
        DS = 2
        WINDOW = 128
        B, L, E = (32, 128, 256)

        def _mha(q, k, v, Wq, bq, Wk, bk, Wv, bv, Wo, bo):
            b, lq, e = q.shape
            lk = k.shape[1]
            d = e // N_HEADS
            scale = 1.0 / np.sqrt(d)
            qh = (q @ Wq + bq).reshape(b, lq, N_HEADS, d)
            kh = (k @ Wk + bk).reshape(b, lk, N_HEADS, d)
            vh = (v @ Wv + bv).reshape(b, lk, N_HEADS, d)
            att = jax.nn.softmax(jnp.einsum('bqhd,bkhd->bhqk', qh, kh) * scale, axis=-1)
            out = jnp.einsum('bhqk,bkhd->bqhd', att, vh).reshape(b, lq, e)
            return out @ Wo + bo

        def _downsample(x):
            b, l, e = x.shape
            ln = l // DS
            return x[:, :ln * DS].reshape(b, ln, DS, e).mean(axis=2)
        key = jax.random.key(seed)
        ks = jax.random.split(key, 8)
        s = E ** (-0.5)
        return {'query': jax.random.normal(ks[0], (B, L, E), jnp.float32), 'key': jax.random.normal(ks[1], (B, L, E), jnp.float32), 'value': jax.random.normal(ks[2], (B, L, E), jnp.float32), 'Wq': jax.random.normal(ks[3], (E, E), jnp.float32) * s, 'bq': jnp.zeros((E,), jnp.float32), 'Wk': jax.random.normal(ks[4], (E, E), jnp.float32) * s, 'bk': jnp.zeros((E,), jnp.float32), 'Wv': jax.random.normal(ks[5], (E, E), jnp.float32) * s, 'bv': jnp.zeros((E,), jnp.float32), 'Wo': jax.random.normal(ks[6], (E, E), jnp.float32) * s, 'bo': jnp.zeros((E,), jnp.float32), 'soft_mask': jnp.ones((L,), jnp.float32)}
    _L0_xattn_all = _L0_xattn_setup()
    _L0_xattn_in = {k: v for k, v in _L0_xattn_all.items() if k in ('Wq', 'bq', 'Wk', 'bk', 'Wv', 'bv', 'Wo', 'bo')}
    del _L0_xattn_all

    def _L0_ffn_setup():
        import jax, jax.numpy as jnp
        import numpy as np
        HIDDEN = 256
        MOE_FF = 128
        SHARED_FF = 704
        NUM_EXPERTS = 16
        TOP_K = 2
        NORM_TOPK = True
        key = jax.random.key(seed)
        ks = jax.random.split(key, 8)
        s = 0.02
        return {'layer_input': jax.random.normal(ks[0], (1, 512, HIDDEN), dtype=jnp.float32), 'gate_w': jax.random.normal(ks[1], (NUM_EXPERTS, HIDDEN), dtype=jnp.float32) * s, 'w_gate_up': jax.random.normal(ks[2], (NUM_EXPERTS, HIDDEN, 2 * MOE_FF), dtype=jnp.float32) * s, 'w_down': jax.random.normal(ks[3], (NUM_EXPERTS, MOE_FF, HIDDEN), dtype=jnp.float32) * s, 'shared_w_gate': jax.random.normal(ks[4], (SHARED_FF, HIDDEN), dtype=jnp.float32) * s, 'shared_w_up': jax.random.normal(ks[5], (SHARED_FF, HIDDEN), dtype=jnp.float32) * s, 'shared_w_down': jax.random.normal(ks[6], (HIDDEN, SHARED_FF), dtype=jnp.float32) * s, 'shared_gate_w': jax.random.normal(ks[7], (1, HIDDEN), dtype=jnp.float32) * s}
    _L0_ffn_all = _L0_ffn_setup()
    _L0_ffn_in = {k: v for k, v in _L0_ffn_all.items() if k in ('gate_w', 'w_gate_up', 'w_down', 'shared_w_gate', 'shared_w_up', 'shared_w_down', 'shared_gate_w')}
    del _L0_ffn_all

    def _L1_attn_setup():
        import jax, jax.numpy as jnp
        import numpy as np
        D_MODEL = 256
        H = 4
        DK = 256
        DV = 512
        HQK = DK // H
        HV = DV // H
        LOW_RANK = 32
        CHUNK = 16
        GATE_NORM = 32.0
        GATE_MULT = 1.0
        EPS = 1e-05

        def gla_fused_chunk(q, k, v, g, chunk=CHUNK):
            B, Hh, N, Dk = q.shape
            Dv = v.shape[-1]
            q = q * Dk ** (-0.5)
            nc = N // chunk

            def to_chunks(t, d):
                return t.reshape(B, Hh, nc, chunk, d).transpose(2, 0, 1, 3, 4)
            qc, kc, vc, gc = (to_chunks(q, Dk), to_chunks(k, Dk), to_chunks(v, Dv), to_chunks(g, Dk))
            bc = jnp.cumsum(gc, axis=-2)
            causal = jnp.tril(jnp.ones((chunk, chunk), bool))

            def step(S, inp):
                qi, ki, vi, bi = inp
                o_inter = jnp.einsum('bhtd,bhde->bhte', qi * jnp.exp(bi), S)
                diff = bi[:, :, :, None, :] - bi[:, :, None, :, :]
                diff = jnp.where(causal[None, None, :, :, None], diff, -jnp.inf)
                A = jnp.einsum('bhtd,bhjd,bhtjd->bhtj', qi, ki, jnp.exp(diff))
                o_intra = jnp.einsum('bhtj,bhje->bhte', A, vi)
                blast = bi[:, :, -1:, :]
                kdec = ki * jnp.exp(blast - bi)
                S_new = jnp.exp(blast)[:, :, 0, :, None] * S + jnp.einsum('bhtd,bhte->bhde', kdec, vi)
                return (S_new, o_inter + o_intra)
            S0 = jnp.zeros((B, Hh, Dk, Dv), q.dtype)
            _, o = jax.lax.scan(step, S0, (qc, kc, vc, bc))
            return o.transpose(1, 2, 0, 3, 4).reshape(B, Hh, N, Dv)
        key = jax.random.key(seed)
        ks = jax.random.split(key, 10)
        B, N = (2, 1024)
        s = 0.02
        return {'x': jax.random.normal(ks[0], (B, N, D_MODEL), jnp.float32), 'Wq': jax.random.normal(ks[1], (DK, D_MODEL), jnp.float32) * s, 'Wk': jax.random.normal(ks[2], (DK, D_MODEL), jnp.float32) * s, 'Wv': jax.random.normal(ks[3], (DV, D_MODEL), jnp.float32) * s, 'Wg': jax.random.normal(ks[4], (DV, D_MODEL), jnp.float32) * s, 'Wgk1': jax.random.normal(ks[5], (LOW_RANK, D_MODEL), jnp.float32) * s, 'Wgk2': jax.random.normal(ks[6], (DK, LOW_RANK), jnp.float32) * s, 'bgk2': jax.random.normal(ks[7], (DK,), jnp.float32) * 0.1, 'Wout': jax.random.normal(ks[8], (D_MODEL, DV), jnp.float32) * s, 'rms_w': jnp.ones((HV,), jnp.float32)}
    _L1_attn_all = _L1_attn_setup()
    _L1_attn_in = {k: v for k, v in _L1_attn_all.items() if k in ('Wq', 'Wk', 'Wv', 'Wg', 'Wgk1', 'Wgk2', 'bgk2', 'Wout', 'rms_w')}
    del _L1_attn_all

    def _L1_xattn_setup():
        import jax, jax.numpy as jnp
        import numpy as np
        D_MODEL = 256
        N_HEADS = 1
        HEAD_DIM = D_MODEL // N_HEADS
        N, LEN_Q, LEN_IN = (8, 256, 1024)
        key = jax.random.key(seed)
        ks = jax.random.split(key, 7)
        s = 1.0 / np.sqrt(D_MODEL)
        return {'query': jax.random.normal(ks[0], (N, LEN_Q, D_MODEL), dtype=jnp.float32), 'input_flatten': jax.random.normal(ks[1], (N, LEN_IN, D_MODEL), dtype=jnp.float32), 'input_padding_mask': jax.random.randint(ks[2], (N, LEN_IN), 0, 2).astype(bool), 'Wq': jax.random.normal(ks[3], (D_MODEL, D_MODEL), dtype=jnp.float32) * s, 'bq': jnp.zeros((D_MODEL,), dtype=jnp.float32), 'Wk': jax.random.normal(ks[4], (D_MODEL, D_MODEL), dtype=jnp.float32) * s, 'bk': jnp.zeros((D_MODEL,), dtype=jnp.float32), 'Wo': jax.random.normal(ks[5], (D_MODEL, D_MODEL), dtype=jnp.float32) * s, 'bo': jnp.zeros((D_MODEL,), dtype=jnp.float32)}
    _L1_xattn_all = _L1_xattn_setup()
    _L1_xattn_in = {k: v for k, v in _L1_xattn_all.items() if k in ('Wq', 'bq', 'Wk', 'bk', 'Wo', 'bo')}
    del _L1_xattn_all

    def _L1_ffn_setup():
        import jax, jax.numpy as jnp
        import numpy as np
        THRESH_FACTOR = 0.7

        def ternary_quantize(w):
            delta = THRESH_FACTOR * jnp.mean(jnp.abs(w))
            return jnp.where(w > delta, 1.0, jnp.where(w < -delta, -1.0, 0.0)).astype(w.dtype)
        key = jax.random.key(seed)
        k1, k2, k3 = jax.random.split(key, 3)
        B, S, D_IN, D_OUT = (8, 1024, 256, 256)
        inp = {'input': jax.random.normal(k1, (B, S, D_IN), dtype=jnp.float32), 'weight': jax.random.normal(k2, (D_OUT, D_IN), dtype=jnp.float32) * (1.0 / np.sqrt(D_IN)), 'alpha': jnp.ones((1,), dtype=jnp.float32), 'bias': jax.random.normal(k3, (D_OUT,), dtype=jnp.float32) * (1.0 / np.sqrt(D_IN))}
        return inp
    _L1_ffn_all = _L1_ffn_setup()
    _L1_ffn_in = {k: v for k, v in _L1_ffn_all.items() if k in ('weight', 'alpha', 'bias')}
    del _L1_ffn_all
    return {'x': x, 'ctx_1024': ctx_1024, 'mask_S2_ff1': mask_S2_ff1, 'mask_BxS2_bk0': mask_BxS2_bk0, 'L0_attn_Wq': _L0_attn_in['Wq'], 'L0_attn_Wk': _L0_attn_in['Wk'], 'L0_attn_Wv': _L0_attn_in['Wv'], 'L0_attn_Wo': _L0_attn_in['Wo'], 'L0_attn_bo': _L0_attn_in['bo'], 'L0_attn_rel_emb': _L0_attn_in['rel_emb'], 'L0_xattn_Wq': _L0_xattn_in['Wq'], 'L0_xattn_bq': _L0_xattn_in['bq'], 'L0_xattn_Wk': _L0_xattn_in['Wk'], 'L0_xattn_bk': _L0_xattn_in['bk'], 'L0_xattn_Wv': _L0_xattn_in['Wv'], 'L0_xattn_bv': _L0_xattn_in['bv'], 'L0_xattn_Wo': _L0_xattn_in['Wo'], 'L0_xattn_bo': _L0_xattn_in['bo'], 'L0_ffn_gate_w': _L0_ffn_in['gate_w'], 'L0_ffn_w_gate_up': _L0_ffn_in['w_gate_up'], 'L0_ffn_w_down': _L0_ffn_in['w_down'], 'L0_ffn_shared_w_gate': _L0_ffn_in['shared_w_gate'], 'L0_ffn_shared_w_up': _L0_ffn_in['shared_w_up'], 'L0_ffn_shared_w_down': _L0_ffn_in['shared_w_down'], 'L0_ffn_shared_gate_w': _L0_ffn_in['shared_gate_w'], 'L1_attn_Wq': _L1_attn_in['Wq'], 'L1_attn_Wk': _L1_attn_in['Wk'], 'L1_attn_Wv': _L1_attn_in['Wv'], 'L1_attn_Wg': _L1_attn_in['Wg'], 'L1_attn_Wgk1': _L1_attn_in['Wgk1'], 'L1_attn_Wgk2': _L1_attn_in['Wgk2'], 'L1_attn_bgk2': _L1_attn_in['bgk2'], 'L1_attn_Wout': _L1_attn_in['Wout'], 'L1_attn_rms_w': _L1_attn_in['rms_w'], 'L1_xattn_Wq': _L1_xattn_in['Wq'], 'L1_xattn_bq': _L1_xattn_in['bq'], 'L1_xattn_Wk': _L1_xattn_in['Wk'], 'L1_xattn_bk': _L1_xattn_in['bk'], 'L1_xattn_Wo': _L1_xattn_in['Wo'], 'L1_xattn_bo': _L1_xattn_in['bo'], 'L1_ffn_weight': _L1_ffn_in['weight'], 'L1_ffn_alpha': _L1_ffn_in['alpha'], 'L1_ffn_bias': _L1_ffn_in['bias']}

def reference(x, ctx_1024, mask_S2_ff1, mask_BxS2_bk0, L0_attn_Wq, L0_attn_Wk, L0_attn_Wv, L0_attn_Wo, L0_attn_bo, L0_attn_rel_emb, L0_xattn_Wq, L0_xattn_bq, L0_xattn_Wk, L0_xattn_bk, L0_xattn_Wv, L0_xattn_bv, L0_xattn_Wo, L0_xattn_bo, L0_ffn_gate_w, L0_ffn_w_gate_up, L0_ffn_w_down, L0_ffn_shared_w_gate, L0_ffn_shared_w_up, L0_ffn_shared_w_down, L0_ffn_shared_gate_w, L1_attn_Wq, L1_attn_Wk, L1_attn_Wv, L1_attn_Wg, L1_attn_Wgk1, L1_attn_Wgk2, L1_attn_bgk2, L1_attn_Wout, L1_attn_rms_w, L1_xattn_Wq, L1_xattn_bq, L1_xattn_Wk, L1_xattn_bk, L1_xattn_Wo, L1_xattn_bo, L1_ffn_weight, L1_ffn_alpha, L1_ffn_bias):
    import jax
    import jax.numpy as jnp

    def _L0_attn_ref(x, Wq, Wk, Wv, Wo, bo, rel_emb):
        import jax, jax.numpy as jnp
        import numpy as np
        NUM_HEADS = 16
        CLIP = 16
        b, s, d_in = x.shape
        h, hd = (NUM_HEADS, x.shape[-1] // NUM_HEADS)
        q = (x @ Wq).reshape(b, s, h, hd).transpose(0, 2, 1, 3)
        k = (x @ Wk).reshape(b, s, h, hd).transpose(0, 2, 1, 3)
        v = (x @ Wv).reshape(b, s, h, hd).transpose(0, 2, 1, 3)
        r = jnp.arange(s)
        dist = jnp.clip(jnp.abs(r[None, :] - r[:, None]), 0, CLIP)
        a_k = rel_emb[dist]
        scores = jnp.einsum('bhqd,bhkd->bhqk', q, k) * a_k
        causal = jnp.triu(jnp.ones((s, s), dtype=bool), k=1)
        scores = jnp.where(causal, -jnp.inf, scores)
        attn = jax.nn.softmax(scores / np.sqrt(hd), axis=-1)
        ctx = jnp.einsum('bhqk,bhkd->bhqd', attn, v)
        ctx = ctx.transpose(0, 2, 1, 3).reshape(b, s, h * hd)
        return ctx @ Wo + bo

    def _L0_xattn_ref(query, key, value, Wq, bq, Wk, bk, Wv, bv, Wo, bo, soft_mask):
        import jax, jax.numpy as jnp
        import numpy as np
        N_HEADS = 16
        LEVELS = 3
        DS = 2
        WINDOW = 128
        B, L, E = (32, 128, 256)

        def _mha(q, k, v, Wq, bq, Wk, bk, Wv, bv, Wo, bo):
            b, lq, e = q.shape
            lk = k.shape[1]
            d = e // N_HEADS
            scale = 1.0 / np.sqrt(d)
            qh = (q @ Wq + bq).reshape(b, lq, N_HEADS, d)
            kh = (k @ Wk + bk).reshape(b, lk, N_HEADS, d)
            vh = (v @ Wv + bv).reshape(b, lk, N_HEADS, d)
            att = jax.nn.softmax(jnp.einsum('bqhd,bkhd->bhqk', qh, kh) * scale, axis=-1)
            out = jnp.einsum('bhqk,bkhd->bqhd', att, vh).reshape(b, lq, e)
            return out @ Wo + bo

        def _downsample(x):
            b, l, e = x.shape
            ln = l // DS
            return x[:, :ln * DS].reshape(b, ln, DS, e).mean(axis=2)
        params = (Wq, bq, Wk, bk, Wv, bv, Wo, bo)
        k, v = (key, value)
        acc = _mha(query, k, v, *params)
        for _ in range(LEVELS - 1):
            k = _downsample(k)
            v = _downsample(v)
            acc = acc + _mha(query, k, v, *params)
        hier = acc / LEVELS
        b, l, e = query.shape
        nw = l // WINDOW
        qw = query.reshape(b * nw, WINDOW, e)
        kw = key.reshape(b * nw, WINDOW, e)
        vw = value.reshape(b * nw, WINDOW, e)
        sw = _mha(qw, kw, vw, *params).reshape(b, l, e)
        sm = jax.nn.sigmoid(soft_mask[:l])
        return (hier + sw) * sm[None, :, None]

    def _L0_ffn_ref(layer_input, gate_w, w_gate_up, w_down, shared_w_gate, shared_w_up, shared_w_down, shared_gate_w):
        import jax, jax.numpy as jnp
        import numpy as np
        HIDDEN = 256
        MOE_FF = 128
        SHARED_FF = 704
        NUM_EXPERTS = 16
        TOP_K = 2
        NORM_TOPK = True
        B, S, D = layer_input.shape
        x = layer_input.reshape(-1, D)
        N = x.shape[0]
        shared = jax.nn.silu(x @ shared_w_gate.T) * (x @ shared_w_up.T) @ shared_w_down.T
        shared = shared * jax.nn.sigmoid(x @ shared_gate_w.T)
        logits = x @ gate_w.T
        probs = jax.nn.softmax(logits.astype(jnp.float32), axis=-1)
        rw, sel = jax.lax.top_k(probs, TOP_K)
        if NORM_TOPK:
            rw = rw / rw.sum(axis=-1, keepdims=True)
        rw = rw.astype(x.dtype)
        combine = jnp.zeros((N, NUM_EXPERTS), x.dtype).at[jnp.arange(N)[:, None], sel].set(rw)
        gu = jnp.einsum('nd,edf->nef', x, w_gate_up)
        g, h = jnp.split(gu, 2, axis=-1)
        h = jax.nn.silu(g) * h
        expert_out = jnp.einsum('nef,efd,ne->nd', h, w_down, combine)
        out = expert_out + shared
        return out.reshape(B, S, D)

    def _L1_attn_ref(x, Wq, Wk, Wv, Wg, Wgk1, Wgk2, bgk2, Wout, rms_w):
        import jax, jax.numpy as jnp
        import numpy as np
        D_MODEL = 256
        H = 4
        DK = 256
        DV = 512
        HQK = DK // H
        HV = DV // H
        LOW_RANK = 32
        CHUNK = 16
        GATE_NORM = 32.0
        GATE_MULT = 1.0
        EPS = 1e-05

        def gla_fused_chunk(q, k, v, g, chunk=CHUNK):
            B, Hh, N, Dk = q.shape
            Dv = v.shape[-1]
            q = q * Dk ** (-0.5)
            nc = N // chunk

            def to_chunks(t, d):
                return t.reshape(B, Hh, nc, chunk, d).transpose(2, 0, 1, 3, 4)
            qc, kc, vc, gc = (to_chunks(q, Dk), to_chunks(k, Dk), to_chunks(v, Dv), to_chunks(g, Dk))
            bc = jnp.cumsum(gc, axis=-2)
            causal = jnp.tril(jnp.ones((chunk, chunk), bool))

            def step(S, inp):
                qi, ki, vi, bi = inp
                o_inter = jnp.einsum('bhtd,bhde->bhte', qi * jnp.exp(bi), S)
                diff = bi[:, :, :, None, :] - bi[:, :, None, :, :]
                diff = jnp.where(causal[None, None, :, :, None], diff, -jnp.inf)
                A = jnp.einsum('bhtd,bhjd,bhtjd->bhtj', qi, ki, jnp.exp(diff))
                o_intra = jnp.einsum('bhtj,bhje->bhte', A, vi)
                blast = bi[:, :, -1:, :]
                kdec = ki * jnp.exp(blast - bi)
                S_new = jnp.exp(blast)[:, :, 0, :, None] * S + jnp.einsum('bhtd,bhte->bhde', kdec, vi)
                return (S_new, o_inter + o_intra)
            S0 = jnp.zeros((B, Hh, Dk, Dv), q.dtype)
            _, o = jax.lax.scan(step, S0, (qc, kc, vc, bc))
            return o.transpose(1, 2, 0, 3, 4).reshape(B, Hh, N, Dv)
        B, N, _ = x.shape
        split = lambda t, hd: t.reshape(B, N, H, hd).transpose(0, 2, 1, 3)
        q = split(x @ Wq.T, HQK)
        k = split(x @ Wk.T, HQK)
        v = split(x @ Wv.T, HV)
        g_logits = x @ Wgk1.T @ Wgk2.T + bgk2
        g = jax.nn.log_sigmoid(g_logits * GATE_MULT) / GATE_NORM
        g = split(g, HQK)
        o = gla_fused_chunk(q, k, v, g)
        o = o.transpose(0, 2, 1, 3)
        o = o * jax.lax.rsqrt(jnp.mean(o * o, axis=-1, keepdims=True) + EPS) * rms_w
        gate = jax.nn.silu(x @ Wg.T)
        return o.reshape(B, N, DV) * gate @ Wout.T

    def _L1_xattn_ref(query, input_flatten, input_padding_mask, Wq, bq, Wk, bk, Wo, bo):
        import jax, jax.numpy as jnp
        import numpy as np
        D_MODEL = 256
        N_HEADS = 1
        HEAD_DIM = D_MODEL // N_HEADS
        N, LEN_Q, LEN_IN = (8, 256, 1024)
        n, len_q, _ = query.shape
        len_in = input_flatten.shape[1]
        Q = (query @ Wq.T + bq).reshape(n, len_q, N_HEADS, HEAD_DIM).transpose(0, 2, 1, 3)
        K = (input_flatten @ Wk.T + bk).reshape(n, len_in, N_HEADS, HEAD_DIM).transpose(0, 2, 1, 3)
        scores = jnp.einsum('nhqd,nhkd->nhqk', Q, K)
        scores = jnp.where(input_padding_mask[:, None, None, :], -jnp.inf, scores)
        attn = jax.nn.softmax(scores, axis=-1)
        V = jnp.broadcast_to(input_flatten[:, None], (n, N_HEADS, len_in, D_MODEL))
        out = jnp.einsum('nhql,nhld->nhqd', attn, V)
        out = out.transpose(0, 2, 1, 3).reshape(n, len_q, D_MODEL)
        return out @ Wo.T + bo

    def _L1_ffn_ref(input, weight, alpha, bias):
        import jax, jax.numpy as jnp
        import numpy as np
        THRESH_FACTOR = 0.7

        def ternary_quantize(w):
            delta = THRESH_FACTOR * jnp.mean(jnp.abs(w))
            return jnp.where(w > delta, 1.0, jnp.where(w < -delta, -1.0, 0.0)).astype(w.dtype)
        w_ternary = ternary_quantize(weight)
        w_eff = w_ternary * alpha
        out = jnp.einsum('bsd,od->bso', input, w_eff) + bias
        return out
    x = x + _L0_attn_ref(_layernorm(x, axis=-1), L0_attn_Wq, L0_attn_Wk, L0_attn_Wv, L0_attn_Wo, L0_attn_bo, L0_attn_rel_emb)
    x = x + _L0_xattn_ref(_layernorm(x, axis=-1), ctx_1024, ctx_1024, L0_xattn_Wq, L0_xattn_bq, L0_xattn_Wk, L0_xattn_bk, L0_xattn_Wv, L0_xattn_bv, L0_xattn_Wo, L0_xattn_bo, mask_S2_ff1)
    x = x + _L0_ffn_ref(_layernorm(x, axis=-1), L0_ffn_gate_w, L0_ffn_w_gate_up, L0_ffn_w_down, L0_ffn_shared_w_gate, L0_ffn_shared_w_up, L0_ffn_shared_w_down, L0_ffn_shared_gate_w)
    x = x + _L1_attn_ref(_layernorm(x, axis=-1), L1_attn_Wq, L1_attn_Wk, L1_attn_Wv, L1_attn_Wg, L1_attn_Wgk1, L1_attn_Wgk2, L1_attn_bgk2, L1_attn_Wout, L1_attn_rms_w)
    x = x + _L1_xattn_ref(_layernorm(x, axis=-1), ctx_1024, mask_BxS2_bk0, L1_xattn_Wq, L1_xattn_bq, L1_xattn_Wk, L1_xattn_bk, L1_xattn_Wo, L1_xattn_bo)
    x = x + _L1_ffn_ref(_layernorm(x, axis=-1), L1_ffn_weight, L1_ffn_alpha, L1_ffn_bias)
    return x

_drawn_inputs = setup_inputs


def setup_inputs(seed=0):
    import zlib

    import numpy as np

    out = dict(_drawn_inputs(seed))
    spreads = {'mask_S2_ff1': (1.0, 0.2),
     'L0_xattn_bq': (0.0, 0.1),
     'L0_xattn_bk': (0.0, 0.8),
     'L0_xattn_bv': (0.0, 0.1),
     'L0_xattn_bo': (0.0, 0.1),
     'L1_attn_rms_w': (1.0, 0.6),
     'L1_xattn_bq': (0.0, 0.1),
     'L1_xattn_bk': (0.0, 0.8),
     'L1_xattn_bo': (0.0, 0.1)}
    factors = {'L0_attn_bo': 3.195,
     'L0_ffn_gate_w': 4.454,
     'L0_ffn_w_gate_up': 4.35,
     'L0_ffn_w_down': 4.387,
     'L0_ffn_shared_gate_w': 8.0,
     'L1_attn_Wgk1': 8.0,
     'L1_attn_Wgk2': 8.0,
     'L1_attn_bgk2': 7.725,
     'L1_ffn_bias': 8.0}
    for name, (base, spread) in spreads.items():
        noise = np.random.default_rng([zlib.crc32(name.encode()), seed]).standard_normal(out[name].shape)
        drawn = base * np.exp(spread * noise) if base else spread * noise
        out[name] = jnp.asarray(drawn.astype(out[name].dtype))
    for name, factor in factors.items():
        out[name] = (out[name] * factor).astype(out[name].dtype)
    return out
```

```python
from contextlib import ExitStack

import concourse.bass as bass
from concourse import mybir

F32 = mybir.dt.float32
U8 = mybir.dt.uint8
ALU = mybir.AluOpType
ACT = mybir.ActivationFunctionType
AX = mybir.AxisListType.X

P = 128
NSEQ = 16
D = 256
DC = D // P
H0 = 16
HD = D // H0
HC = P // HD
CLIP = 16
BIG = 1e30
EPS = 1e-5
LV = (P, P // 2, P // 4)
KEYS = sum(LV)
LOWK = KEYS - P
VW = HD + 1
NE = 16
FE = 128
FS = 704
NB = NE + -(-FS // FE)
GT = 4
NG = NSEQ // GT
H1 = 4
DV = 512
CB = 32
NCB = P // CB
GATE_NORM = 32.0
LR = 32

SEMS = """
ld_x ld_a ld_c
ident hmask causal dist rel_term rel_sum mhalf vones
ln_stats ln_aggr ln_var rstd xn xnT_ps xnT x_biased x_done
q_ps kv_ps kT q_heads v s_ps scaled maxed expd pt_ps pt o_ps o_inv ctx ctxT_ps ctxT out_ps
ld_b ld_e ld_w ld_m stored
x_cn x_bv x_bias_ps x_sig x_sigd x_bias x_bias2 vones2 vzero
cT mean_sum means k_ps kx qh v2_ps v2 s2_ps maxed2 shifted expd2 pt2_ps pt2 o2_ps o2_inv o2_part
turn_ps turned_a turned_v
r_ps logits top1 gt eqt beats rank shift_l exp_l sel selsum selinv cgate expg comb
g_ps h_ps sg hh d_ps acc tri
g_qk_ps g_qk g_gk_ps g_gk g_z_ps g_z g_v_ps g_v g_g_ps g_gate g_abs g_exp g_ln g_log g_cum g_dq g_dk g_eq g_ek
g_qx g_kx g_a_ps g_at g_o_ps g_ss g_ve g_rr g_g2 g_y g_yT_ps g_yT g_out_ps trim atz
m_add m_qk_ps m_qk m_s_ps m_s m_exp m_pT_ps m_pT m_o_ps m_inv m_o m_oT_ps m_oT m_out_ps f_out_ps
m_neg w_abs w_tot w_mean w_del w_neg w_pos w_tern cTm
""".split()
CREDITED = {"rstd": 1, "xn": 1, "xnT_ps": 1, "xnT": 1, "x_biased": 1, "x_done": 1, "q_ps": 1, "kv_ps": 1, "kT": 1,
            "q_heads": 1, "v": 1, "s_ps": 4, "expd": 4, "pt_ps": 4, "pt": 4, "o_ps": 1, "out_ps": 1,
            "cT": 1, "means": 2, "x_cn": 1, "k_ps": 1, "kx": 1, "qh": 1, "v2_ps": 1, "v2": 1, "s2_ps": 8, "shifted": 8,
            "expd2": 8, "pt2_ps": 8, "pt2": 8, "o2_ps": 1,
            "r_ps": 1, "comb": 1, "g_ps": NB, "h_ps": NB, "sg": NB, "hh": NB, "d_ps": NB, "acc": NB - 1,
            "g_qk": 1, "g_gk": 1, "g_z": 1, "g_v": 1, "g_gate": 1, "g_at": 1, "g_o_ps": 1, "g_a_ps": 1, "g_ss": 1,
            "g_qx": 1, "g_kx": 1, "g_y": 1, "g_yT": 1, "g_rr": 1, "g_g2": 1, "g_ln": 1, "g_log": 1,
            "m_qk": 1, "m_s": 1, "m_exp": 1, "m_pT": 1, "m_o": 1, "m_oT": 1, "cTm": 1}


def made(tile, part=0, parts=1):
    return (tile + 1) * parts + part + 1


def over(ap, at, n):
    ap = ap.unsqueeze(at)
    shape = list(ap.shape)
    shape[at] = n
    return ap.broadcast_to(shape)


def build(nc, A, out):
    with ExitStack() as ctx:
        def sb(name, shape, dt=F32):
            return ctx.enter_context(nc.sbuf_tensor(name, shape, dt))

        S = {n: ctx.enter_context(nc.semaphore(n)) for n in SEMS}
        PS = ctx.enter_context(nc.psum_tensor("PS", [P, 8, 512], F32))

        X = sb("X", [P, NSEQ, D])
        C = sb("C", [P, NSEQ, D])
        ident = sb("ident_sb", [P, P])
        hmask = sb("hmask_sb", [P, HC])
        mhalf = sb("mhalf_sb", [P, 1])
        half = sb("half", [P, 1])
        stats = sb("stats", [P, 6])
        mv = sb("mv", [P, 2])
        var = sb("var", [P, 1])
        rstd = sb("rstd_sb", [P, 1])
        xn = sb("xn_sb", [P, D])
        xnT = sb("xnT_sb", [P, DC, P])
        a_wq, a_wk, a_wv, a_wo = (sb(f"a_{n}", [P, DC, D]) for n in ("wq", "wk", "wv", "wo"))
        a_bo = sb("a_bo", [P, D])
        rel = sb("rel", [P, CLIP + 1])
        dist = sb("dist_sb", [P, P])
        relT = sb("relT", [P, P])
        csum = dist[:, :].rearrange("p (c t) -> p c t", c=DC)
        nA = sb("nA", [P, P])
        hide = sb("hide", [P, P])
        kT = sb("kT_sb", [P, DC, P])
        q_heads = sb("q_heads_sb", [P, H0, P])
        va = sb("va", [P, H0, HD + 1])
        low = sb("low", [P, H0])
        o_inv = sb("o_inv_sb", [P, H0])
        cx = sb("cx", [P, D])
        cxT = sb("cxT", [P, DC, P])

        x_wq, x_wk, x_wv, x_wo = (sb(f"x_{n}", [P, DC, D]) for n in ("wq", "wk", "wv", "wo"))
        x_bq, x_bk, x_bv = (sb(f"x_{n}", [P, DC]) for n in ("bq", "bk", "bv"))
        x_bo = sb("x_bo", [P, D])
        x_sm = sb("x_sm", [P, 1])
        x_bvb = sb("x_bvb", [P, DC, P])
        cT = sb("cT_sb", [P, DC, KEYS])
        kx = sb("kx_sb", [P, DC, KEYS])
        vx = sb("vx", [P, H0, VW])
        vlow = sb("vlow", [P, H0, 2 * VW])
        mx = sb("mx", [P, H0, 3])
        o2_inv = sb("o2_inv_sb", [P, 2, 8, 3])
        o2_part = sb("o2_part_sb", [P, 2, 8, 3, HD])
        s_g = sb("s_g", [P, DC, FS])
        s_u = sb("s_u", [P, DC, FS])
        s_dn = sb("s_dn", [P, NB - NE, D])
        gwT = sb("gwT", [P, DC, NE + 1])
        lg = sb("lg", [P, GT, NE + 1])
        l1 = sb("l1", [P, GT])
        tri16 = sb("tri16", [P, NE, NE])
        rank = sb("rank_sb", [P, GT, NE])
        wsum = sb("wsum", [P, GT])
        comb = sb("comb_sb", [P, GT, NE + 1])
        l_wq, l_wk = (sb(f"l_{n}", [P, DC, D]) for n in ("wq", "wk"))
        l_wv, l_wg = (sb(f"l_{n}", [P, DC, DV]) for n in ("wv", "wg"))
        l_gk1 = sb("l_gk1", [P, DC, LR])
        l_gk2 = sb("l_gk2", [LR, D])
        l_bgk = sb("l_bgk", [P, DC])
        l_wo = sb("l_wo", [P, DV // P, D])
        l_rms = sb("l_rms", [P, P])
        trim = sb("trim_sb", [P, P])
        ones = sb("ones", [P, P])
        m_wq, m_wk, m_wo, f_w = (sb(f"m_{n}", [P, DC, D]) for n in ("wq", "wk", "wo", "wf"))
        m_bq, m_bk = (sb(f"m_{n}", [P, DC]) for n in ("bq", "bk"))
        m_bo, f_b = (sb(f"m_{n}", [P, D]) for n in ("bo", "bf"))
        f_alpha = sb("f_alpha", [P, 1])
        f_stat = sb("f_stat", [P, 4])
        pad4 = sb("pad4", [P, NSEQ, P // 4], mybir.dt.int32)

        cn = sb("cn", [P, D])
        work = sb("work", [P, 7760])
        wide = sb("wide", [P, NE * (DC * 2 * FE + D)])

        def part(region, base, *shape):
            n = 1
            for x in shape:
                n *= x
            view = region[:, base:base + n]
            if len(shape) == 1:
                return view
            letters = "abcd"[:len(shape)]
            return view.rearrange(f"p ({' '.join(letters)}) -> p {' '.join(letters)}", **dict(zip(letters, shape)))

        sc = part(work, 0, H0, P)
        ex = part(work, 2048, H0, P)
        pT = part(work, 4096, H0, P)
        sc2 = part(work, 0, H0, KEYS)
        pT2 = part(work, 3584, 8, 512)
        sg = part(work, 0, 2, 512)
        hh = part(work, 1024, 2, 512)
        xT3 = part(work, 2048, DC, GT * P)
        cmp = part(work, 3072, GT, NE, NE)
        cmq = part(work, 4096, GT, NE, NE)
        g_zb = part(work, 2688, DC, P)
        g_t1 = part(work, 2944, DC, P)
        g_lg = part(work, 3200, DC, P)
        g_cum = part(work, 3456, DC, P)
        g_qk = part(work, 2048, 2 * DC, P)
        g_gk = part(work, 2560, P)
        g_qx = part(work, 3712, DC, P)
        g_kx = part(work, 3968, CB * NCB * (NCB + 1))
        g_v = part(work, 4608, DV)
        g_gate = part(work, 5120, DV)
        g_at = part(work, 5632, 2, 2, P)
        g_y = part(work, 6144, DV)
        g_yT = part(work, 6656, DV // P, P)
        g_ss = part(work, 7168, H1)
        g_rr = part(work, 7172, H1)
        g_sq = part(work, 7176, H1, P)
        m_qk = part(work, 0, 2 * DC, P)
        m_s = part(work, 512, P)
        m_e = part(work, 640, P)
        m_pT = part(work, 768, P)
        m_o = part(work, 896, D)
        m_oT = part(work, 1152, DC, P)
        m_low = part(work, 1408, 1)
        m_sum = part(work, 1409, 1)
        m_inv = part(work, 1410, 1)
        m_cT = part(work, 1412, DC, P)
        m_hide = part(work, 1668, P)

        e_gu = part(wide, 0, NE, DC, 2 * FE)
        e_dn = part(wide, NE * DC * 2 * FE, NE, D)
        SR = -(-FS // P)
        t_sg = part(wide, 0, SR, D)
        t_su = part(wide, 1536, SR, D)
        t_sd = part(wide, 3072, DC, FS)
        t_gw = part(wide, 4480, D)[0:NE + 1]
        t_lq = part(wide, 4736, DC, D)
        t_lk = part(wide, 5248, DC, D)
        t_lv = part(wide, 5760, DV // P, D)
        t_lg = part(wide, 6784, DV // P, D)
        t_g1 = part(wide, 7808, D)[0:LR]
        t_g2 = part(wide, 8064, DC, LR)
        t_lo = part(wide, 8128, DC, DV)
        t_mq = part(wide, 9152, DC, D)
        t_mk = part(wide, 9664, DC, D)
        t_mo = part(wide, 10176, DC, D)
        t_fw = part(wide, 10688, DC, D)
        t_fl = part(wide, 11200, DC, D)

        turns = []

        def turn(dst, blocks):
            turns.append((dst, blocks))

        def blocks_of(src, rows, c, width=P):
            return [(src[:, r, c * P:(c + 1) * P], n * width) for n, r in enumerate(rows)]

        for src, dst in ((t_sg, s_g), (t_su, s_u)):
            for c in range(DC):
                turn(dst[:, c, 0:4 * P], blocks_of(src, range(4), c))
                turn(dst[:, c, 4 * P:FS], [(src[:, 4, c * P:(c + 1) * P], 0),
                                           (src[0:FS - 5 * P, 5, c * P:(c + 1) * P], P)])
        for k in (0, 2):
            turn(s_dn[:, k:k + 2, :], [(t_sd[:, r, (k + j) * P:(k + j + 1) * P], j * D + r * P)
                                       for j in range(2) for r in range(DC)])
        turn(s_dn[:, 4, :], [(t_sd[:, r, 4 * P:5 * P], r * P) for r in range(DC)])
        turn(s_dn[0:FS - 5 * P, 5, :], [(t_sd[:, r, 5 * P:FS], r * P) for r in range(DC)])
        turn(gwT[:, :, :], [(t_gw[:, c * P:(c + 1) * P], c * (NE + 1)) for c in range(DC)])
        for src, dst in ((t_lq, l_wq), (t_lk, l_wk), (t_mq, m_wq), (t_mk, m_wk), (t_mo, m_wo)):
            turn(dst[:, :, :], [(src[:, r, c * P:(c + 1) * P], c * D + r * P) for c in range(DC) for r in range(DC)])
        for src, dst in ((t_lv, l_wv), (t_lg, l_wg)):
            for c in range(DC):
                turn(dst[:, c, :], blocks_of(src, range(4), c))
        turn(l_gk1[:, :, :], [(t_g1[:, c * P:(c + 1) * P], c * LR) for c in range(DC)])
        turn(l_gk2[:, :], [(t_g2[:, r, :], r * P) for r in range(DC)])
        for k in (0, 2):
            turn(l_wo[:, k:k + 2, :], [(t_lo[:, r, (k + j) * P:(k + j + 1) * P], j * D + r * P)
                                       for j in range(2) for r in range(DC)])
        turn(f_w[:, :, :], [(t_fw[:, r, c * P:(c + 1) * P], c * D + r * P) for c in range(DC) for r in range(DC)])

        def turned(n):
            dst, _ = turns[n]
            ps = PS[0:dst.shape[0], n % 4, 0:dst.free_size()]
            return ps if len(dst.shape) == 2 else ps.rearrange("p (a b) -> p a b", a=dst.shape[1])

        def tile(T, b):
            return T[:, bass.ds(b, 1), :].rearrange("p a d -> p (a d)")

        LD_A, LD_W, LD_C, LD_B, LD_M, LD_E = (16 * n for n in (6, 19, 1, 9, 7, 8))
        LAST = 4 * NSEQ
        block = ctx.enter_context(nc.Block())

        def piped(eng, front, body):
            front(0)
            with eng.Fori(0, NSEQ - 1) as b:
                body(b, True)
            body(NSEQ - 1, False)

        def k_block(n):
            w = CB * (n + 1)
            base = 3968 + DC * CB * (n * (n + 1) // 2)
            return part(work, base, DC, w)

        def F_OF(e):
            return min(FE, FS - (e - NE) * FE) if e >= NE else FE

        def w_in(ap):
            return ap.rearrange("(c p) n -> p c n", p=P)

        @block.sync
        def _(sp):
            xv = A["x"].rearrange("b t d -> t b d")

            def load(dst, src, done, slow=False):
                sp.dma_start(dst, src, allow_slow_non_contiguous=slow).then_inc(done, 16)

            def all_rows(name):
                return A[name].partition_broadcast(P)

            def column(name):
                return A[name].rearrange("(c p) -> p c", p=P)

            load(X[:, 0:4, :], xv[:, 0:4, :], S["ld_x"])
            for t, n in ((a_wq, "L0_attn_Wq"), (a_wk, "L0_attn_Wk"), (a_wv, "L0_attn_Wv"), (a_wo, "L0_attn_Wo")):
                load(t[:, :, :], w_in(A[n]), S["ld_a"])
            load(rel[:, :], all_rows("L0_attn_rel_emb"), S["ld_a"])
            load(a_bo[:, :], all_rows("L0_attn_bo"), S["ld_a"])
            for t, n in ((t_sg, "L0_ffn_shared_w_gate"), (t_su, "L0_ffn_shared_w_up")):
                load(t[:, 0:5, :], A[n][0:5 * P, :].rearrange("(r p) d -> p r d", p=P), S["ld_w"])
                load(t[0:FS - 5 * P, 5, :], A[n][5 * P:FS, :], S["ld_w"])
            load(t_gw[0:NE, :], A["L0_ffn_gate_w"], S["ld_w"])
            load(t_gw[NE:NE + 1, :], A["L0_ffn_shared_gate_w"], S["ld_w"])
            load(t_g1[:, :], A["L1_attn_Wgk1"], S["ld_w"])
            for t, n in ((t_sd, "L0_ffn_shared_w_down"), (t_lq, "L1_attn_Wq"), (t_lk, "L1_attn_Wk"),
                         (t_lv, "L1_attn_Wv"), (t_lg, "L1_attn_Wg"), (t_g2, "L1_attn_Wgk2"),
                         (t_lo, "L1_attn_Wout"), (t_mq, "L1_xattn_Wq"), (t_mk, "L1_xattn_Wk"),
                         (t_mo, "L1_xattn_Wo"), (t_fw, "L1_ffn_weight")):
                load(t[:, :, :], A[n].rearrange("(r p) d -> p r d", p=P), S["ld_w"])
            load(f_alpha[:, :], all_rows("L1_ffn_alpha"), S["ld_w"])
            load(X[:, 4:NSEQ, :], xv[:, 4:NSEQ, :], S["ld_x"])
            load(C[:, :, :], A["ctx_1024"].rearrange("b t d -> t b d"), S["ld_c"])
            for t, n in ((x_wq, "Wq"), (x_wk, "Wk"), (x_wv, "Wv"), (x_wo, "Wo")):
                load(t[:, :, :], w_in(A["L0_xattn_" + n]), S["ld_b"])
            for t, n in ((x_bq, "bq"), (x_bk, "bk"), (x_bv, "bv")):
                load(t[:, :], column("L0_xattn_" + n), S["ld_b"], slow=True)
            load(x_bo[:, :], all_rows("L0_xattn_bo"), S["ld_b"])
            load(x_sm[:, :], A["mask_S2_ff1"].rearrange("(p a) -> p a", a=1), S["ld_b"], slow=True)
            load(l_bgk[:, :], column("L1_attn_bgk2"), S["ld_m"], slow=True)
            load(l_rms[:, :], all_rows("L1_attn_rms_w"), S["ld_m"])
            for t, n in ((m_bq, "L1_xattn_bq"), (m_bk, "L1_xattn_bk")):
                load(t[:, :], column(n), S["ld_m"], slow=True)
            load(m_bo[:, :], all_rows("L1_xattn_bo"), S["ld_m"])
            load(f_b[:, :], all_rows("L1_ffn_bias"), S["ld_m"])
            load(pad4.rearrange("p b t -> p (b t)"), A["mask_BxS2_bk0"].rearrange("b t -> (b t)").partition_broadcast(P), S["ld_m"])
            sp.wait_ge(S["turn_ps"], len(turns))
            for e in range(0, NE, 4):
                load(e_gu[:, e:e + 4, :, :].rearrange("p e c n -> p (e c) n"),
                     A["L0_ffn_w_gate_up"][e:e + 4].rearrange("e (c p) n -> p (e c) n", p=P), S["ld_e"])
                load(e_dn[:, e:e + 4, :], A["L0_ffn_w_down"][e:e + 4].rearrange("e f n -> f e n"), S["ld_e"])
            for done, n in ((S["ld_c"], LD_C), (S["ld_b"], LD_B), (S["ld_m"], LD_M), (S["ld_w"], LD_W), (S["ld_e"], LD_E)):
                sp.wait_ge(done, n)
            with sp.Fori(0, NSEQ) as b:
                sp.wait_ge(S["x_done"], made(LAST + 2 * b + 1))
                load(out[bass.ds(b, 1)].rearrange("b t d -> t (b d)"), tile(X, b), S["stored"])
            sp.wait_ge(S["stored"], 16 * NSEQ)

        @block.gpsimd
        def _(gp):
            for name, n in CREDITED.items():
                gp.sem_inc(S[name], n)
            gp.memset(mhalf[:, :], -0.5).then_inc(S["mhalf"], 1)
            gp.memset(half[:, :], 0.5).then_inc(S["mhalf"], 1)
            gp.memset(ident[:, :], 0.0).then_inc(S["ident"], 1)
            gp.memset(hmask[:, :], 1.0).then_inc(S["hmask"], 1)
            gp.memset(hide[:, :], 0.0).then_inc(S["causal"], 1)
            gp.memset(va[:, :, HD:VW], 1.0).then_inc(S["vones"], 1)
            gp.memset(vx[:, :, HD:VW], 0.75).then_inc(S["vones2"], 1)
            gp.memset(vlow[:, :, :], 0.0).then_inc(S["vzero"], 1)
            gp.wait_ge(S["vzero"], 1)
            gp.memset(vlow[0:LV[1], :, HD:VW], 3.0).then_inc(S["vones2"], 1)
            gp.wait_ge(S["vones2"], 2)
            gp.memset(vlow[LV[1]:LOWK, :, VW + HD:2 * VW], 3.0).then_inc(S["vones2"], 1)
            gp.wait_ge(S["vones2"], 3)
            gp.memset(tri16[:, :, :], 1.0).then_inc(S["tri"], 1)
            gp.memset(trim[:, :], 1.0).then_inc(S["trim"], 1)
            gp.memset(ones[:, :], 1.0).then_inc(S["w_abs"], 1)
            gp.wait_ge(S["tri"], 1)
            gp.affine_select(out=tri16[:, :, :], in_=tri16[:, :, :], compare_op=ALU.is_gt, fill=0.0, base=0,
                             pattern=[[1, NE], [-1, NE]], channel_multiplier=0).then_inc(S["tri"], 1)
            gp.wait_ge(S["trim"], 1)
            gp.affine_select(out=trim[:, :], in_=trim[:, :], compare_op=ALU.is_ge, fill=0.0, base=0,
                             pattern=[[1, P]], channel_multiplier=-1).then_inc(S["trim"], 1)
            gp.wait_ge(S["ident"], 1)
            gp.affine_select(out=ident[:, :], in_=ident[:, :], compare_op=ALU.not_equal, fill=1.0,
                             base=0, pattern=[[-1, P]], channel_multiplier=1).then_inc(S["ident"], 1)
            gp.wait_ge(S["hmask"], 1)
            gp.affine_select(out=hmask[:, :], in_=hmask[:, :], compare_op=ALU.is_ge, fill=0.0,
                             base=0, pattern=[[-HD, HC]], channel_multiplier=1).then_inc(S["hmask"], 1)
            gp.wait_ge(S["hmask"], 2)
            gp.affine_select(out=hmask[:, :], in_=hmask[:, :], compare_op=ALU.is_ge, fill=0.0,
                             base=HD - 1, pattern=[[HD, HC]], channel_multiplier=-1).then_inc(S["hmask"], 1)
            gp.wait_ge(S["causal"], 1)
            gp.affine_select(out=hide[:, :], in_=hide[:, :], compare_op=ALU.is_ge, fill=BIG,
                             base=0, pattern=[[-1, P]], channel_multiplier=1).then_inc(S["causal"], 1)
            gp.iota(dist[:, :], pattern=[[-1, P]], base=0, channel_multiplier=1,
                    allow_small_or_imprecise_dtypes=True).then_inc(S["dist"], 1)

            def ln(i):
                gp.wait_ge(S["ln_var"], i + 1)
                gp.wait_ge(S["xn"], made(i - 1))
                gp.tensor_tensor(rstd[:, :], var[:, :], mhalf[:, :], ALU.pow).then_inc(S["rstd"], 1)

            def bias_x(i, b, bias):
                gp.wait_ge(S["xn"], made(i))
                gp.tensor_tensor(tile(X, b), tile(X, b), bias[:, :], ALU.add).then_inc(S["x_biased"], 1)

            gp.wait_ge(S["mhalf"], 2)
            gp.wait_ge(S["ld_a"], LD_A)

            def front(b):
                ln(b)
                bias_x(b, b, a_bo)

            piped(gp, front, lambda b, more: front(b + 1) if more else None)

            def x_front(b):
                i = NSEQ + b
                ln(i)
                bias_x(i, b, x_bo)
                at0, n = 0, P
                for lv in range(2):
                    if lv == 0:
                        gp.wait_ge(S["cT"], made(b))
                    else:
                        gp.wait_ge(S["means"], made(b, 0, 2))
                    pair = cT[:, :, at0:at0 + n].rearrange("p c (t a) -> p c t a", a=2)
                    gp.tensor_tensor(csum[:, :, 0:n // 2], pair[:, :, :, 0], pair[:, :, :, 1], ALU.add)\
                        .then_inc(S["mean_sum"], 1)
                    gp.wait_ge(S["mean_sum"], 2 * b + lv + 1)
                    gp.tensor_tensor(cT[:, :, at0 + n:at0 + n + n // 2], csum[:, :, 0:n // 2],
                                     half[:, 0:1].unsqueeze(2).broadcast_to([P, DC, n // 2]), ALU.mult)\
                        .then_inc(S["means"], 1)
                    at0, n = at0 + n, n // 2

            gp.wait_ge(S["x_done"], made(NSEQ - 1))
            gp.wait_ge(S["x_bias"], 1)
            piped(gp, x_front, lambda b, more: x_front(b + 1) if more else None)
            gp.wait_ge(S["x_done"], made(2 * NSEQ - 1))
            with gp.Fori(0, NG) as g:
                for t in range(GT):
                    ln(2 * NSEQ + g * GT + t)
            gp.wait_ge(S["x_done"], made(3 * NSEQ - 1))
            gp.memset(part(work, 5632, 2 * 2 * P), 0.0).then_inc(S["atz"], 1)
            gp.wait_ge(S["ld_m"], LD_M)
            with gp.Fori(0, NSEQ) as b:
                ln(3 * NSEQ + b)
                gp.wait_ge(S["g_gate"], made(b))
                gp.wait_ge(S["g_y"], made(b - 1))
                gp.tensor_tensor(g_gate.rearrange("p (h e) -> p h e", h=H1),
                                 g_gate.rearrange("p (h e) -> p h e", h=H1), over(l_rms[:, :], 1, H1), ALU.mult)\
                    .then_inc(S["g_g2"], 1)
                gp.wait_ge(S["g_ve"], b + 1)
                gp.tensor_tensor(g_rr, g_ss, mhalf[:, 0:1].broadcast_to([P, H1]), ALU.pow).then_inc(S["g_rr"], 1)
            gp.wait_ge(S["x_done"], made(4 * NSEQ - 1))
            with gp.Fori(0, NSEQ) as b:
                ln(LAST + 2 * b)
                gp.wait_ge(S["xn"], made(LAST + 2 * b))
                gp.tensor_tensor(tile(X, b), tile(X, b), m_bo[:, :], ALU.add).then_inc(S["x_biased"], 1)
                ln(LAST + 2 * b + 1)

        @block.scalar
        def _(act):
            def ln_xnT(i):
                act.wait_ge(S["xnT_ps"], made(i))
                act.activation(xnT[:, :, :], PS[:, 4, 0:D].rearrange("p (c t) -> p c t", c=DC),
                               ACT.Copy).then_inc(S["xnT"], 1)

            def front_k(b):
                act.wait_ge(S["kv_ps"], made(b))
                act.activation(kT[:, :, :], PS[:, 6, 0:D].rearrange("p (c t) -> p c t", c=DC),
                               ACT.Copy).then_inc(S["kT"], 1)

            def front_v(b):
                act.wait_ge(S["o_ps"], made(b - 1))
                act.activation(va[:, :, 0:HD], PS[:, 6, D:2 * D].rearrange("p (h d) -> p h d", h=H0),
                               ACT.Copy).then_inc(S["v"], 1)

            def exps(b, g):
                act.wait_ge(S["maxed"], b * 4 + g + 1)
                act.wait_ge(S["pt_ps"], made(b - 1, g, 4))
                for h in range(4 * g, 4 * g + 4):
                    i = act.activation(ex[:, h, :], sc[:, h, :], ACT.Exp, bias=low[:, h:h + 1], scale=-1.0)
                i.then_inc(S["expd"], 1)

            def pts(b, g):
                act.wait_ge(S["pt_ps"], made(b, g, 4))
                act.wait_ge(S["o_ps"], made(b - 1))
                act.activation(pT[:, 4 * g:4 * g + 4, :], PS[:, g, :].rearrange("p (h t) -> p h t", h=4),
                               ACT.Copy).then_inc(S["pt"], 1)

            def ctxT(b):
                act.wait_ge(S["ctxT_ps"], b + 1)
                act.activation(cxT[:, :, :], PS[:, 7, 0:D].rearrange("p (c t) -> p c t", c=DC),
                               ACT.Copy).then_inc(S["ctxT"], 1)

            def front(b):
                ln_xnT(b)
                front_k(b)
                front_v(b)

            def body(b, more):
                exps(b, 0)
                if more:
                    ln_xnT(b + 1)
                exps(b, 1)
                pts(b, 0)
                exps(b, 2)
                pts(b, 1)
                exps(b, 3)
                pts(b, 2)
                pts(b, 3)
                if more:
                    front_k(b + 1)
                    front_v(b + 1)
                ctxT(b)

            for n in range(0, len(turns), 2):
                act.wait_ge(S["turn_ps"], n + 1)
                act.activation(turns[n][0], turned(n), ACT.Copy).then_inc(S["turned_a"], 1)

            act.wait_ge(S["vones"], 1)
            piped(act, front, body)

            def two(ap):
                return ap.rearrange("p (c t) -> p c t", c=DC)

            def x_T(b):
                act.wait_ge(S["xnT_ps"], made(NSEQ + b))
                act.activation(xnT[:, :, :], two(PS[:, 4, 0:D]), ACT.Copy).then_inc(S["xnT"], 1)
                act.activation(cT[:, :, 0:P], two(PS[:, 4, D:2 * D]), ACT.Copy).then_inc(S["cT"], 1)

            def x_k(b):
                act.wait_ge(S["k_ps"], made(b))
                for c in range(DC):
                    i = act.activation(kx[:, c, :], PS[:, 4, c * KEYS:(c + 1) * KEYS], ACT.Identity,
                                       bias=x_bk[:, c:c + 1], scale=1.0)
                i.then_inc(S["kx"], 1)

            def x_v(b):
                act.wait_ge(S["v2_ps"], made(b))
                act.wait_ge(S["o2_ps"], made(b - 1))
                heads = PS[:, 4, :].rearrange("p (a h d) -> p a h d", a=2, h=H0)
                act.activation(vx[:, :, 0:HD], heads[:, 0], ACT.Copy)
                act.activation(vlow[0:LV[1], :, 0:HD], heads[0:LV[1], 1], ACT.Copy)
                act.activation(vlow[LV[1]:LOWK, :, VW:VW + HD], heads[LV[1]:LOWK, 1], ACT.Copy).then_inc(S["v2"], 1)

            def x_exp(b, g):
                act.wait_ge(S["shifted"], made(b, g, 8))
                act.activation(sc2[:, 2 * g:2 * g + 2, :], sc2[:, 2 * g:2 * g + 2, :], ACT.Exp,
                               scale=float(HD) ** -0.5).then_inc(S["expd2"], 1)

            def x_pT(b, g):
                act.wait_ge(S["pt2_ps"], made(b, g, 8))
                act.wait_ge(S["o2_ps"], made(b - 1))
                act.activation(pT2[:, g, :], PS[:, 2 + g % 2, :], ACT.Copy).then_inc(S["pt2"], 1)

            def x_ctxT(b):
                act.wait_ge(S["ctxT_ps"], NSEQ + b + 1)
                act.activation(cxT[:, :, :], two(PS[:, 7, 0:D]), ACT.Copy).then_inc(S["ctxT"], 1)

            def x_front(b):
                x_T(b)
                x_k(b)
                x_v(b)

            def x_body(b, more):
                for g in range(8):
                    x_exp(b, g)
                    if g:
                        x_pT(b, g - 1)
                    if g == 2 and more:
                        x_T(b + 1)
                x_pT(b, 7)
                if more:
                    x_k(b + 1)
                    x_v(b + 1)
                x_ctxT(b)

            act.wait_ge(S["ld_b"], LD_B)
            act.activation(x_sm[:, :], x_sm[:, :], ACT.Exp, scale=-1.0).then_inc(S["x_sig"], 1)
            act.wait_ge(S["vones2"], 3)
            act.wait_ge(S["x_done"], made(NSEQ - 1))
            piped(act, x_front, x_body)

            def e_silu(g, e):
                rows = F_OF(e)
                act.wait_ge(S["g_ps"], made(g, e, NB))
                act.wait_ge(S["hh"], made(g, e - 2, NB))
                act.activation(sg[0:rows, e % 2, :], PS[0:rows, e % 2, :], ACT.Silu).then_inc(S["sg"], 1)

            act.wait_ge(S["x_done"], made(2 * NSEQ - 1))
            with act.Fori(0, NG) as g:
                for t in range(GT):
                    act.wait_ge(S["xnT_ps"], made(2 * NSEQ + g * GT + t))
                    act.activation(xT3[:, :, t * P:(t + 1) * P], two(PS[:, 4 + t, 0:D]), ACT.Copy)\
                        .then_inc(S["xnT"], 1)
                act.wait_ge(S["shift_l"], g + 1)
                act.activation(lg[:, :, 0:NE], lg[:, :, 0:NE], ACT.Exp).then_inc(S["exp_l"], 1)
                act.activation(comb[:, :, NE:NE + 1], lg[:, :, NE:NE + 1], ACT.Exp, scale=-1.0)\
                    .then_inc(S["expg"], 1)
                for e in range(NB):
                    e_silu(g, e)

            act.wait_ge(S["x_done"], made(3 * NSEQ - 1))
            act.wait_ge(S["ld_m"], LD_M)
            with act.Fori(0, NSEQ) as b:
                act.wait_ge(S["xnT_ps"], made(3 * NSEQ + b))
                act.activation(xnT[:, :, :], two(PS[:, 0, 0:D]), ACT.Copy).then_inc(S["xnT"], 1)
                act.wait_ge(S["g_gk_ps"], b + 1)
                act.activation(g_gk[0:LR, :], PS[0:LR, 2, 0:P], ACT.Copy).then_inc(S["g_gk"], 1)
                act.wait_ge(S["g_qk_ps"], b + 1)
                act.wait_ge(S["g_kx"], made(b - 1))
                act.wait_ge(S["g_qx"], made(b - 1))
                act.activation(g_qk, PS[:, 1, :].rearrange("p (c t) -> p c t", c=2 * DC), ACT.Copy)\
                    .then_inc(S["g_qk"], 1)
                act.wait_ge(S["g_z_ps"], b + 1)
                act.wait_ge(S["g_log"], made(b - 1))
                for c in range(DC):
                    i = act.activation(g_zb[:, c, :], PS[:, 2, P + c * P:2 * P + c * P], ACT.Identity,
                                       bias=l_bgk[:, c:c + 1], scale=1.0)
                i.then_inc(S["g_z"], 1)
                act.wait_ge(S["g_z"], made(b))
                act.activation(g_t1, g_zb, ACT.Abs).then_inc(S["g_abs"], 1)
                act.wait_ge(S["g_abs"], b + 1)
                act.activation(g_t1, g_t1, ACT.Exp, scale=-1.0).then_inc(S["g_exp"], 1)
                act.wait_ge(S["g_exp"], b + 1)
                act.activation(g_t1, g_t1, ACT.Ln, bias=1.0).then_inc(S["g_ln"], 1)
                act.wait_ge(S["g_v_ps"], b + 1)
                act.wait_ge(S["g_o_ps"], made(b - 1))
                act.activation(g_v, PS[:, 3, :], ACT.Copy).then_inc(S["g_v"], 1)
                act.wait_ge(S["g_dq"], b + 1)
                act.activation(g_qx, g_qx, ACT.Exp, scale=1.0 / GATE_NORM).then_inc(S["g_eq"], 1)
                act.wait_ge(S["g_dk"], b + 1)
                act.activation(g_kx, g_kx, ACT.Exp, scale=1.0 / GATE_NORM).then_inc(S["g_ek"], 1)
                act.wait_ge(S["g_g_ps"], b + 1)
                act.wait_ge(S["g_y"], made(b - 1))
                act.activation(g_gate, PS[:, 4, :], ACT.Silu).then_inc(S["g_gate"], 1)
                act.wait_ge(S["g_o_ps"], made(b))
                act.wait_ge(S["g_rr"], made(b - 1))
                for h in range(H1):
                    i = act.activation(g_sq[:, h, :], PS[:, 7, h * P:(h + 1) * P], ACT.Square, accum_out=g_ss[:, h:h + 1])
                i.then_inc(S["g_ss"], 1)
                act.wait_ge(S["g_yT_ps"], b + 1)
                act.activation(g_yT, PS[:, 5, :].rearrange("p (h t) -> p h t", h=H1), ACT.Copy).then_inc(S["g_yT"], 1)

            act.wait_ge(S["x_done"], made(4 * NSEQ - 1))
            with act.Fori(0, NSEQ) as b:
                act.wait_ge(S["xnT_ps"], made(LAST + 2 * b))
                act.activation(xnT[:, :, :], two(PS[:, 0, 0:D]), ACT.Copy).then_inc(S["xnT"], 1)
                act.activation(m_cT, two(PS[:, 0, D:2 * D]), ACT.Copy).then_inc(S["cTm"], 1)
                act.wait_ge(S["m_qk_ps"], b + 1)
                for c in range(DC):
                    act.activation(m_qk[:, c, :], PS[:, 1, c * P:(c + 1) * P], ACT.Identity,
                                   bias=m_bq[:, c:c + 1], scale=1.0)
                    i = act.activation(m_qk[:, DC + c, :], PS[:, 1, D + c * P:D + (c + 1) * P], ACT.Identity,
                                       bias=m_bk[:, c:c + 1], scale=1.0)
                i.then_inc(S["m_qk"], 1)
                act.wait_ge(S["m_s"], made(b))
                act.activation(m_e, m_s, ACT.Exp, bias=m_low, scale=-1.0, accum_out=m_sum).then_inc(S["m_exp"], 1)
                act.wait_ge(S["m_pT_ps"], b + 1)
                act.activation(m_pT, PS[:, 3, 0:P], ACT.Copy).then_inc(S["m_pT"], 1)
                act.wait_ge(S["m_oT_ps"], b + 1)
                act.activation(m_oT, two(PS[:, 5, 0:D]), ACT.Copy).then_inc(S["m_oT"], 1)
                act.wait_ge(S["xnT_ps"], made(LAST + 2 * b + 1))
                act.activation(xnT[:, :, :], two(PS[:, 7, 0:D]), ACT.Copy).then_inc(S["xnT"], 1)

        @block.tensor
        def _(pe):
            def ln_T(i):
                pe.wait_ge(S["xn"], made(i))
                pe.wait_ge(S["xnT"], made(i - 1))
                for c in range(DC):
                    m = pe.transpose(PS[:, 4, c * P:(c + 1) * P], xn[:, c * P:(c + 1) * P], ident[:, :])
                m.then_inc(S["xnT_ps"], 1)

            def qkv(b):
                pe.wait_ge(S["xnT"], made(b))
                for w, bank, done in ((a_wq, 5, S["q_ps"]), (a_wk, 6, None)):
                    for oc in range(DC):
                        for c in range(DC):
                            m = pe.matmul(PS[:, bank, oc * P:(oc + 1) * P], w[:, c, oc * P:(oc + 1) * P],
                                          xnT[:, c, :], start=(c == 0), stop=(c == DC - 1))
                    if done:
                        m.then_inc(done, 1)
                for c in range(DC):
                    m = pe.matmul(PS[:, 6, D:2 * D], xnT[:, c, :], a_wv[:, c, :], start=(c == 0), stop=(c == DC - 1))
                m.then_inc(S["kv_ps"], 1)

            def scores(b):
                pe.wait_ge(S["q_heads"], made(b))
                pe.wait_ge(S["kT"], made(b))
                pe.wait_ge(S["pt"], made(b - 1, 3, 4))
                for g in range(4):
                    for h in range(4 * g, 4 * g + 4):
                        m = pe.matmul(PS[:, g, (h % 4) * P:(h % 4 + 1) * P], q_heads[:, h, :], kT[:, h // HC, :],
                                      start=True, stop=True)
                    m.then_inc(S["s_ps"], 1)

            def p_T(b, g):
                pe.wait_ge(S["expd"], made(b, g, 4))
                for h in range(4 * g, 4 * g + 4):
                    m = pe.transpose(PS[:, g, (h % 4) * P:(h % 4 + 1) * P], ex[:, h, :], ident[:, :])
                m.then_inc(S["pt_ps"], 1)

            def av(b, g):
                if g == 0:
                    pe.wait_ge(S["v"], made(b))
                    pe.wait_ge(S["x_done"], made(b - 1))
                pe.wait_ge(S["pt"], made(b, g, 4))
                for h in range(4 * g, 4 * g + 4):
                    m = pe.matmul(PS[:, 7, h * (HD + 1):(h + 1) * (HD + 1)], pT[:, h, :], va[:, h, :],
                                  start=True, stop=True)
                if g == 3:
                    m.then_inc(S["o_ps"], 1)

            def ctx_out(b):
                pe.wait_ge(S["ctx"], b + 1)
                for c in range(DC):
                    m = pe.transpose(PS[:, 7, c * P:(c + 1) * P], cx[:, c * P:(c + 1) * P], ident[:, :])
                m.then_inc(S["ctxT_ps"], 1)
                pe.wait_ge(S["ctxT"], b + 1)
                for c in range(DC):
                    m = pe.matmul(PS[:, 7, D:2 * D], cxT[:, c, :], a_wo[:, c, :], start=(c == 0), stop=(c == DC - 1))
                m.then_inc(S["out_ps"], 1)

            def front(b):
                ln_T(b)
                qkv(b)

            def body(b, more):
                scores(b)
                if more:
                    ln_T(b + 1)
                p_T(b, 0)
                p_T(b, 1)
                av(b, 0)
                p_T(b, 2)
                av(b, 1)
                p_T(b, 3)
                av(b, 2)
                if more:
                    qkv(b + 1)
                av(b, 3)
                ctx_out(b)

            pe.wait_ge(S["ident"], 2)
            pe.wait_ge(S["w_tot"], 1)
            pe.matmul(PS[:, 0, 0:1], ones[:, :], f_stat[:, 0:1], start=True, stop=True).then_inc(S["w_mean"], 1)
            pe.wait_ge(S["ld_w"], LD_W)
            pe.wait_ge(S["w_tern"], 1)
            for n, (dst, blocks) in enumerate(turns):
                if n >= 4:
                    if n % 2:
                        pe.wait_ge(S["turned_v"], (n - 3) // 2)
                    else:
                        pe.wait_ge(S["turned_a"], (n - 2) // 2)
                for src, col in blocks:
                    m = pe.transpose(PS[0:src.shape[1], n % 4, col:col + src.shape[0]], src,
                                     ident[0:src.shape[0], 0:src.shape[0]])
                m.then_inc(S["turn_ps"], 1)
            pe.wait_ge(S["ld_a"], LD_A)
            pe.wait_ge(S["turned_a"], (len(turns) + 1) // 2)
            pe.wait_ge(S["turned_v"], len(turns) // 2)
            piped(pe, front, body)

            def product(ps, lhsT, rhs, chunks=DC):
                for c in range(chunks):
                    m = pe.matmul(ps, lhsT(c), rhs(c), start=(c == 0), stop=(c == chunks - 1))
                return m

            def x_T(b):
                pe.wait_ge(S["xn"], made(NSEQ + b))
                pe.wait_ge(S["v2"], made(b - 1))
                for c in range(DC):
                    pe.transpose(PS[:, 4, c * P:(c + 1) * P], xn[:, c * P:(c + 1) * P], ident[:, :])
                copy_wait(b)
                for c in range(DC):
                    m = pe.transpose(PS[:, 4, D + c * P:D + (c + 1) * P], cn[:, c * P:(c + 1) * P], ident[:, :])
                m.then_inc(S["xnT_ps"], 1)

            def copy_wait(b):
                pe.wait_ge(S["x_cn"], made(b))

            def x_q(b):
                pe.wait_ge(S["xnT"], made(NSEQ + b))
                for oc in range(DC):
                    m = product(PS[:, 5, oc * P:(oc + 1) * P], lambda c: x_wq[:, c, oc * P:(oc + 1) * P],
                                lambda c: xnT[:, c, :])
                m.then_inc(S["q_ps"], 1)

            def x_k(b):
                pe.wait_ge(S["means"], made(b, 1, 2))
                for oc in range(DC):
                    m = product(PS[:, 4, oc * KEYS:(oc + 1) * KEYS], lambda c: x_wk[:, c, oc * P:(oc + 1) * P],
                                lambda c: cT[:, c, :])
                m.then_inc(S["k_ps"], 1)

            def x_v(b):
                pe.wait_ge(S["kx"], made(b))
                product(PS[:, 4, 0:D], lambda c: cT[:, c, 0:P], lambda c: x_wv[:, c, :])
                product(PS[0:LOWK, 4, D:2 * D], lambda c: cT[:, c, P:KEYS], lambda c: x_wv[:, c, :])\
                    .then_inc(S["v2_ps"], 1)

            def x_scores(b, g):
                pe.wait_ge(S["shifted"], made(b, g - 2, 8))
                for j in range(2):
                    h = 2 * g + j
                    m = pe.matmul(PS[:, g % 2, j * KEYS:(j + 1) * KEYS], q_heads[:, h, :], kx[:, h // HC, :],
                                  start=True, stop=True)
                m.then_inc(S["s2_ps"], 1)

            def x_pT(b, g):
                pe.wait_ge(S["expd2"], made(b, g, 8))
                pe.wait_ge(S["pt2"], made(b, g - 2, 8))
                for j in range(2):
                    h = 2 * g + j
                    pe.transpose(PS[:, 2 + g % 2, j * P:(j + 1) * P], sc2[:, h, 0:P], ident[:, :])
                    m = pe.transpose(PS[0:LOWK, 2 + g % 2, D + j * P:D + (j + 1) * P], sc2[:, h, P:KEYS], ident[:, :])
                m.then_inc(S["pt2_ps"], 1)

            def x_av(b, g):
                if g == 0:
                    pe.wait_ge(S["v2"], made(b))
                    pe.wait_ge(S["x_done"], made(NSEQ + b - 1))
                pe.wait_ge(S["pt2"], made(b, g, 8))
                for j in range(2):
                    h = 2 * g + j
                    o = 3 * VW * (h % 8)
                    pe.matmul(PS[:, 6 + g // 4, o:o + VW], pT2[:, g, j * P:(j + 1) * P], vx[:, h, :],
                              start=True, stop=True)
                    m = pe.matmul(PS[:, 6 + g // 4, o + VW:o + 3 * VW], pT2[0:LOWK, g, D + j * P:D + (j + 1) * P],
                                  vlow[0:LOWK, h, :], start=True, stop=True)
                if g == 7:
                    m.then_inc(S["o2_ps"], 1)

            def x_out(b):
                i = NSEQ + b
                pe.wait_ge(S["ctx"], i + 1)
                for c in range(DC):
                    m = pe.transpose(PS[:, 7, c * P:(c + 1) * P], cx[:, c * P:(c + 1) * P], ident[:, :])
                m.then_inc(S["ctxT_ps"], 1)
                pe.wait_ge(S["ctxT"], i + 1)
                product(PS[:, 6, 0:D], lambda c: cxT[:, c, :], lambda c: x_wo[:, c, :]).then_inc(S["out_ps"], 1)

            def x_front(b):
                x_T(b)
                x_q(b)
                x_k(b)
                x_v(b)

            def x_body(b, more):
                pe.wait_ge(S["qh"], made(b))
                pe.wait_ge(S["kx"], made(b))
                x_scores(b, 0)
                x_scores(b, 1)
                for g in range(8):
                    if g + 2 < 8:
                        x_scores(b, g + 2)
                    x_pT(b, g)
                    if g:
                        x_av(b, g - 1)
                    if g == 1 and more:
                        x_T(b + 1)
                    if g == 6 and more:
                        x_q(b + 1)
                        x_k(b + 1)
                x_av(b, 7)
                if more:
                    x_v(b + 1)
                x_out(b)

            pe.wait_ge(S["ld_c"], LD_C)
            pe.wait_ge(S["ld_b"], LD_B)
            pe.wait_ge(S["x_done"], made(NSEQ - 1))
            pe.wait_ge(S["x_bv"], DC)
            product(PS[:, 7, 0:D], lambda c: x_bvb[:, c, :], lambda c: x_wo[:, c, :]).then_inc(S["x_bias_ps"], 1)
            piped(pe, x_front, x_body)

            def e_up(g, e):
                rows = F_OF(e)
                if e < NE:
                    wg, wu = (lambda c: e_gu[:, e, c, 0:FE]), (lambda c: e_gu[:, e, c, FE:2 * FE])
                else:
                    o = (e - NE) * FE
                    wg, wu = (lambda c: s_g[:, c, o:o + rows]), (lambda c: s_u[:, c, o:o + rows])
                pe.wait_ge(S["sg"], made(g, e - 2, NB))
                product(PS[0:rows, e % 2, :], wg, lambda c: xT3[:, c, :]).then_inc(S["g_ps"], 1)
                pe.wait_ge(S["hh"], made(g, e - 2, NB))
                product(PS[0:rows, 2 + e % 2, :], wu, lambda c: xT3[:, c, :]).then_inc(S["h_ps"], 1)

            def e_down(g, e):
                rows, r = F_OF(e), e % 2
                w = e_dn[:, e, :] if e < NE else s_dn[0:rows, e - NE, :]
                pe.wait_ge(S["hh"], made(g, e, NB))
                if e >= 2:
                    pe.wait_ge(S["acc"], made(g, e - 2, NB - 1))
                for t in range(GT):
                    m = pe.matmul(PS[:, 4 + 2 * r + t // 2, (t % 2) * D:(t % 2 + 1) * D],
                                  hh[0:rows, r, t * P:(t + 1) * P], w, start=True, stop=True)
                m.then_inc(S["d_ps"], 1)

            pe.wait_ge(S["ld_e"], LD_E)
            pe.wait_ge(S["x_done"], made(2 * NSEQ - 1))
            with pe.Fori(0, NG) as g:
                pe.wait_ge(S["x_done"], made(2 * NSEQ + g * GT - 1))
                for t in range(GT):
                    pe.wait_ge(S["xn"], made(2 * NSEQ + g * GT + t))
                    for c in range(DC):
                        m = pe.transpose(PS[:, 4 + t, c * P:(c + 1) * P], xn[:, c * P:(c + 1) * P], ident[:, :])
                    m.then_inc(S["xnT_ps"], 1)
                pe.wait_ge(S["xnT"], made(2 * NSEQ + g * GT + GT - 1))
                pe.wait_ge(S["sg"], made(g - 1, NB - 1, NB))
                for t in range(GT):
                    m = product(PS[:, 0, t * (NE + 1):(t + 1) * (NE + 1)],
                                lambda c: xT3[:, c, t * P:(t + 1) * P], lambda c: gwT[:, c, :])
                m.then_inc(S["r_ps"], 1)
                pe.wait_ge(S["logits"], g + 1)
                e_up(g, 0)
                for e in range(NB):
                    if e + 1 < NB:
                        e_up(g, e + 1)
                    e_down(g, e)

            pe.wait_ge(S["x_done"], made(3 * NSEQ - 1))
            pe.wait_ge(S["trim"], 2)
            with pe.Fori(0, NSEQ) as b:
                pe.wait_ge(S["xn"], made(3 * NSEQ + b))
                for c in range(DC):
                    m = pe.transpose(PS[:, 0, c * P:(c + 1) * P], xn[:, c * P:(c + 1) * P], ident[:, :])
                m.then_inc(S["xnT_ps"], 1)
                pe.wait_ge(S["xnT"], made(3 * NSEQ + b))
                product(PS[0:LR, 2, 0:P], lambda c: l_gk1[:, c, :], lambda c: xnT[:, c, :]).then_inc(S["g_gk_ps"], 1)
                pe.wait_ge(S["g_qk"], made(b - 1))
                for n, w in enumerate((l_wq, l_wk)):
                    for oc in range(DC):
                        m = product(PS[:, 1, n * D + oc * P:n * D + (oc + 1) * P],
                                    lambda c: w[:, c, oc * P:(oc + 1) * P], lambda c: xnT[:, c, :])
                m.then_inc(S["g_qk_ps"], 1)
                pe.wait_ge(S["g_gk"], made(b))
                for oc in range(DC):
                    m = pe.matmul(PS[:, 2, P + oc * P:2 * P + oc * P], l_gk2[:, oc * P:(oc + 1) * P],
                                  g_gk[0:LR, :], start=True, stop=True)
                m.then_inc(S["g_z_ps"], 1)
                pe.wait_ge(S["g_v"], made(b - 1))
                product(PS[:, 3, :], lambda c: xnT[:, c, :], lambda c: l_wv[:, c, :]).then_inc(S["g_v_ps"], 1)
                pe.wait_ge(S["g_gate"], made(b - 1))
                pe.wait_ge(S["x_done"], made(3 * NSEQ + b - 1))
                product(PS[:, 4, :], lambda c: xnT[:, c, :], lambda c: l_wg[:, c, :]).then_inc(S["g_g_ps"], 1)
                pe.wait_ge(S["trim"], 2)
                pe.wait_ge(S["g_yT"], made(b - 1))
                pe.wait_ge(S["g_kx"], made(b))
                pe.wait_ge(S["g_qx"], made(b))
                for n in range(NCB):
                    w = CB * (n + 1)
                    for h in range(H1):
                        lo, c = (P // 2) * (h % 2), h // 2
                        m = pe.matmul(PS[0:w, 5 + h % 2, c * P + CB * n:c * P + CB * (n + 1)],
                                      k_block(n)[lo:lo + P // 2, c, :],
                                      g_qx[lo:lo + P // 2, c, CB * n:CB * (n + 1)], start=True, stop=True)
                m.then_inc(S["g_a_ps"], 1)
                pe.wait_ge(S["g_at"], made(b))
                pe.wait_ge(S["g_v"], made(b))
                pe.wait_ge(S["g_y"], made(b - 1))
                for h in range(H1):
                    m = pe.matmul(PS[:, 7, h * P:(h + 1) * P], g_at[:, h % 2, h // 2, :],
                                  g_v[:, h * P:(h + 1) * P], start=True, stop=True)
                m.then_inc(S["g_o_ps"], 1)
                pe.wait_ge(S["g_y"], made(b))
                for h in range(H1):
                    m = pe.transpose(PS[:, 5, h * P:(h + 1) * P], g_y[:, h * P:(h + 1) * P], ident[:, :])
                m.then_inc(S["g_yT_ps"], 1)
                pe.wait_ge(S["g_yT"], made(b))
                product(PS[:, 6, 0:D], lambda c: g_yT[:, c, :], lambda c: l_wo[:, c, :], DV // P)\
                    .then_inc(S["g_out_ps"], 1)

            pe.wait_ge(S["x_done"], made(4 * NSEQ - 1))
            with pe.Fori(0, NSEQ) as b:
                i = LAST + 2 * b
                pe.wait_ge(S["xn"], made(i))
                pe.wait_ge(S["cTm"], made(b - 1))
                pe.wait_ge(S["m_add"], 3 * b + 2)
                for n, src in enumerate((xn, cn)):
                    for c in range(DC):
                        m = pe.transpose(PS[:, 0, n * D + c * P:n * D + (c + 1) * P], src[:, c * P:(c + 1) * P],
                                         ident[:, :])
                m.then_inc(S["xnT_ps"], 1)
                pe.wait_ge(S["xnT"], made(i))
                pe.wait_ge(S["cTm"], made(b))
                for n, (w, src) in enumerate(((m_wq, xnT), (m_wk, m_cT))):
                    for oc in range(DC):
                        m = product(PS[:, 1, n * D + oc * P:n * D + (oc + 1) * P],
                                    lambda c: w[:, c, oc * P:(oc + 1) * P], lambda c: src[:, c, :])
                m.then_inc(S["m_qk_ps"], 1)
                pe.wait_ge(S["m_qk"], made(b))
                pe.wait_ge(S["m_s"], made(b - 1))
                product(PS[:, 2, 0:P], lambda c: m_qk[:, c, :], lambda c: m_qk[:, DC + c, :]).then_inc(S["m_s_ps"], 1)
                pe.wait_ge(S["m_exp"], made(b))
                pe.transpose(PS[:, 3, 0:P], m_e, ident[:, :]).then_inc(S["m_pT_ps"], 1)
                pe.wait_ge(S["m_pT"], made(b))
                pe.wait_ge(S["m_o"], made(b - 1))
                pe.matmul(PS[:, 4, 0:D], m_pT, cn[:, :], start=True, stop=True).then_inc(S["m_o_ps"], 1)
                pe.wait_ge(S["m_o"], made(b))
                for c in range(DC):
                    m = pe.transpose(PS[:, 5, c * P:(c + 1) * P], m_o[:, c * P:(c + 1) * P], ident[:, :])
                m.then_inc(S["m_oT_ps"], 1)
                pe.wait_ge(S["m_oT"], made(b))
                product(PS[:, 6, 0:D], lambda c: m_oT[:, c, :], lambda c: m_wo[:, c, :]).then_inc(S["m_out_ps"], 1)
                pe.wait_ge(S["xn"], made(i + 1))
                for c in range(DC):
                    m = pe.transpose(PS[:, 7, c * P:(c + 1) * P], xn[:, c * P:(c + 1) * P], ident[:, :])
                m.then_inc(S["xnT_ps"], 1)
                pe.wait_ge(S["xnT"], made(i + 1))
                product(PS[:, 7, D:2 * D], lambda c: xnT[:, c, :], lambda c: f_w[:, c, :]).then_inc(S["f_out_ps"], 1)

        @block.vector
        def _(dv):
            def ln(i, b):
                dv.wait_ge(S["rstd"], made(i - 1))
                dv.bn_stats(stats[:, :], tile(X, b)).then_inc(S["ln_stats"], 1)
                dv.wait_ge(S["hmask"], 3)
                dv.wait_ge(S["ln_stats"], i + 1)
                dv.bn_aggr(mv[:, :], stats[:, :]).then_inc(S["ln_aggr"], 1)
                dv.wait_ge(S["ln_aggr"], i + 1)
                dv.tensor_scalar(var[:, :], mv[:, 1:2], EPS, None, ALU.add).then_inc(S["ln_var"], 1)

            def ln_apply(i, b):
                dv.wait_ge(S["rstd"], made(i))
                dv.wait_ge(S["xnT_ps"], made(i - 1))
                dv.tensor_scalar(xn[:, :], tile(X, b), mv[:, 0:1], rstd[:, 0:1], ALU.subtract,
                                 ALU.mult).then_inc(S["xn"], 1)

            def q_split(b):
                dv.wait_ge(S["q_ps"], made(b))
                for c in range(DC):
                    i = dv.tensor_tensor(q_heads[:, c * HC:(c + 1) * HC, :],
                                         over(PS[:, 5, c * P:(c + 1) * P], 1, HC), over(hmask[:, :], 2, P), ALU.mult)
                i.then_inc(S["q_heads"], 1)

            def scale(b, g):
                dv.wait_ge(S["s_ps"], made(b, g, 4))
                dv.wait_ge(S["expd"], made(b - 1, g, 4))
                dv.tensor_tensor(sc[:, 4 * g:4 * g + 4, :], PS[:, g, :].rearrange("p (h t) -> p h t", h=4),
                                 over(nA[:, :], 1, 4), ALU.mult).then_inc(S["scaled"], 1)

            def hide_max(b, g):
                dv.wait_ge(S["hmask"], 3)
                dv.wait_ge(S["scaled"], b * 4 + g + 1)
                for h in range(4 * g, 4 * g + 4):
                    i = dv.tensor_tensor_reduce(sc[:, h, :], sc[:, h, :], hide[:, :], 1.0, BIG, ALU.add, ALU.min,
                                                low[:, h:h + 1])
                i.then_inc(S["maxed"], 1)

            def norm(b):
                dv.wait_ge(S["o_ps"], made(b))
                o = PS[:, 7, 0:H0 * (HD + 1)].rearrange("p (h d) -> p h d", h=H0)
                dv.reciprocal(o_inv[:, :].unsqueeze(2), o[:, :, HD:HD + 1]).then_inc(S["o_inv"], 1)
                dv.wait_ge(S["o_inv"], b + 1)
                dv.tensor_tensor(cx[:, :].rearrange("p (h d) -> p h d", h=H0), o[:, :, 0:HD],
                                 over(o_inv[:, :], 2, HD), ALU.mult).then_inc(S["ctx"], 1)

            def add_x(b):
                dv.wait_ge(S["out_ps"], made(b))
                dv.wait_ge(S["x_biased"], made(b))
                dv.tensor_tensor(tile(X, b), PS[:, 7, D:2 * D], tile(X, b), ALU.add).then_inc(S["x_done"], 1)

            dv.wait_ge(S["dist"], 1)
            dv.wait_ge(S["ld_a"], LD_A)
            dv.tensor_scalar(dist[:, :], dist[:, :], float(CLIP), None, ALU.min).then_inc(S["dist"], 1)
            dv.tensor_scalar(rel[:, :], rel[:, :], -float(HD) ** -0.5, None, ALU.mult).then_inc(S["dist"], 1)
            dv.memset(nA[:, :], 0.0).then_inc(S["rel_sum"], 1)
            dv.wait_ge(S["dist"], 3)
            for d in range(CLIP + 1):
                dv.wait_ge(S["rel_sum"], d + 1)
                dv.tensor_scalar(relT[:, :], dist[:, :], float(d), rel[:, d:d + 1], ALU.is_equal,
                                 ALU.mult).then_inc(S["rel_term"], 1)
                dv.wait_ge(S["rel_term"], d + 1)
                dv.tensor_tensor(nA[:, :], nA[:, :], relT[:, :], ALU.add).then_inc(S["rel_sum"], 1)
            dv.wait_ge(S["rel_sum"], CLIP + 2)
            dv.wait_ge(S["hmask"], 3)
            dv.wait_ge(S["causal"], 2)
            dv.wait_ge(S["ld_x"], 32)

            def front(b):
                ln(b, b)
                ln_apply(b, b)
                q_split(b)

            def body(b, more):
                if more:
                    ln(b + 1, b + 1)
                scale(b, 0)
                if more:
                    ln_apply(b + 1, b + 1)
                scale(b, 1)
                hide_max(b, 0)
                scale(b, 2)
                hide_max(b, 1)
                scale(b, 3)
                hide_max(b, 2)
                hide_max(b, 3)
                if more:
                    q_split(b + 1)
                norm(b)
                add_x(b)

            dv.wait_ge(S["ld_w"], LD_W)
            dv.wait_ge(S["w_abs"], 1)
            fw = t_fw.rearrange("p a b -> p (a b)")
            fl = t_fl.rearrange("p a b -> p (a b)")
            dv.tensor_reduce(f_stat[:, 0:1], fw, AX, ALU.add, apply_absolute_value=True).then_inc(S["w_tot"], 1)
            dv.wait_ge(S["w_mean"], 1)
            dv.tensor_scalar(f_stat[:, 1:2], PS[:, 0, 0:1], 1.0 / (D * D), 0.7, ALU.mult, ALU.mult)\
                .then_inc(S["w_del"], 1)
            dv.wait_ge(S["w_del"], 1)
            dv.tensor_scalar(f_stat[:, 2:3], f_stat[:, 1:2], -1.0, None, ALU.mult).then_inc(S["w_del"], 1)
            dv.wait_ge(S["w_del"], 2)
            dv.tensor_scalar(fl, fw, f_stat[:, 2:3], None, ALU.is_lt).then_inc(S["w_neg"], 1)
            dv.wait_ge(S["w_neg"], 1)
            dv.scalar_tensor_tensor(out=fw, in0=fw, scalar=f_stat[:, 1:2], in1=fl, op0=ALU.is_gt,
                                    op1=ALU.subtract).then_inc(S["w_pos"], 1)
            dv.wait_ge(S["w_pos"], 1)
            dv.tensor_scalar(fw, fw, f_alpha[:, 0:1], None, ALU.mult).then_inc(S["w_tern"], 1)
            for n in range(1, len(turns), 2):
                dv.wait_ge(S["turn_ps"], n + 1)
                dv.tensor_copy(turns[n][0], turned(n)).then_inc(S["turned_v"], 1)

            piped(dv, front, body)

            def x_ln(b):
                ln(NSEQ + b, b)
                dv.wait_ge(S["cT"], made(b - 1))
                dv.tensor_copy(cn[:, :], tile(C, b)).then_inc(S["x_cn"], 1)

            def x_q(b):
                dv.wait_ge(S["q_ps"], made(NSEQ + b))
                dv.wait_ge(S["s2_ps"], made(b - 1, 7, 8))
                for c in range(DC):
                    i = dv.scalar_tensor_tensor(out=q_heads[:, c * HC:(c + 1) * HC, :],
                                                in0=over(PS[:, 5, c * P:(c + 1) * P], 1, HC), scalar=x_bq[:, c:c + 1],
                                                in1=over(hmask[:, :], 2, P), op0=ALU.add, op1=ALU.mult)
                i.then_inc(S["qh"], 1)

            def levels(b, g):
                o = 0
                for lv, n in enumerate(LV):
                    yield (PS[:, g % 2, 0:2 * KEYS].rearrange("p (h k) -> p h k", h=2)[:, :, o:o + n],
                           sc2[:, 2 * g:2 * g + 2, o:o + n], mx[:, 2 * g:2 * g + 2, lv], n)
                    o += n

            def x_max(b, g):
                dv.wait_ge(S["s2_ps"], made(b, g, 8))
                for s_in, _, m, _ in levels(b, g):
                    i = dv.tensor_reduce(m, s_in, AX, ALU.max)
                i.then_inc(S["maxed2"], 1)

            def x_shift(b, g):
                dv.wait_ge(S["maxed2"], b * 8 + g + 1)
                dv.wait_ge(S["pt2_ps"], made(b - 1, g, 8))
                for s_in, s_out, m, n in levels(b, g):
                    i = dv.tensor_tensor(s_out, s_in, over(m, 2, n), ALU.subtract)
                i.then_inc(S["shifted"], 1)

            def x_norm(b):
                dv.wait_ge(S["o2_ps"], made(b))
                dv.wait_ge(S["ctx"], NSEQ + b)
                outs = [PS[:, 6 + half, 0:8 * 3 * VW].rearrange("p (h l d) -> p h l d", h=8, l=3)
                        for half in range(2)]
                for half in range(2):
                    dv.reciprocal(o2_inv[:, half, :, :].unsqueeze(3), outs[half][:, :, :, HD:VW]).then_inc(S["o2_inv"], 1)
                for half in range(2):
                    dv.wait_ge(S["o2_inv"], b * 2 + half + 1)
                    dv.tensor_tensor(o2_part[:, half], outs[half][:, :, :, 0:HD], over(o2_inv[:, half], 3, HD),
                                     ALU.mult).then_inc(S["o2_part"], 1)
                for half in range(2):
                    dv.wait_ge(S["o2_part"], b * 2 + half + 1)
                    i = dv.tensor_reduce(cx[:, half * P:(half + 1) * P].rearrange("p (h d) -> p h d", h=8),
                                         o2_part[:, half].rearrange("p h l d -> p h d l"), AX, ALU.add)
                i.then_inc(S["ctx"], 1)

            def x_add(b):
                dv.wait_ge(S["out_ps"], made(NSEQ + b))
                dv.wait_ge(S["x_biased"], made(NSEQ + b))
                dv.scalar_tensor_tensor(out=tile(X, b), in0=PS[:, 6, 0:D], scalar=x_sm[:, 0:1], in1=tile(X, b),
                                        op0=ALU.mult, op1=ALU.add).then_inc(S["x_done"], 1)

            def x_front(b):
                x_ln(b)
                ln_apply(NSEQ + b, b)
                x_q(b)

            def x_body(b, more):
                if more:
                    x_ln(b + 1)
                x_max(b, 0)
                for g in range(8):
                    if g < 7:
                        x_max(b, g + 1)
                    x_shift(b, g)
                    if g == 1 and more:
                        ln_apply(NSEQ + b + 1, b + 1)
                if more:
                    x_q(b + 1)
                x_norm(b)
                x_add(b)

            dv.wait_ge(S["ld_b"], LD_B)
            dv.wait_ge(S["ld_c"], LD_C)
            dv.wait_ge(S["x_done"], made(NSEQ - 1))
            for c in range(DC):
                dv.tensor_scalar(x_bvb[:, c, :], ones[:, :], x_bv[:, c:c + 1], None, ALU.mult).then_inc(S["x_bv"], 1)
            dv.wait_ge(S["x_sig"], 1)
            dv.tensor_scalar(x_sm[:, :], x_sm[:, :], 1.0, None, ALU.add).then_inc(S["x_sigd"], 1)
            dv.wait_ge(S["x_sigd"], 1)
            dv.reciprocal(x_sm[:, :], x_sm[:, :]).then_inc(S["x_sigd"], 1)
            dv.wait_ge(S["x_bias_ps"], 1)
            dv.tensor_tensor(x_bo[:, :], x_bo[:, :], PS[:, 7, 0:D], ALU.add).then_inc(S["x_bias2"], 1)
            dv.wait_ge(S["x_bias2"], 1)
            dv.wait_ge(S["x_sigd"], 2)
            dv.tensor_scalar(x_bo[:, :], x_bo[:, :], 2.0, x_sm[:, 0:1], ALU.mult, ALU.mult).then_inc(S["x_bias"], 1)
            piped(dv, x_front, x_body)

            def router(g):
                dv.wait_ge(S["r_ps"], made(g))
                dv.wait_ge(S["comb"], made(g - 1))
                dv.tensor_copy(lg[:, :, :], PS[:, 0, 0:GT * (NE + 1)].rearrange("p (t e) -> p t e", t=GT))\
                    .then_inc(S["logits"], 1)
                dv.wait_ge(S["logits"], g + 1)
                dv.tensor_reduce(l1[:, :], lg[:, :, 0:NE], AX, ALU.max).then_inc(S["top1"], 1)
                for t in range(GT):
                    li, lj = over(lg[:, t, 0:NE], 2, NE), over(lg[:, t, 0:NE], 1, NE)
                    dv.tensor_tensor(cmp[:, t], lj, li, ALU.is_gt)
                    i = dv.tensor_tensor(cmq[:, t], lj, li, ALU.is_equal)
                i.then_inc(S["gt"], 1)
                dv.wait_ge(S["top1"], g + 1)
                dv.wait_ge(S["gt"], g + 1)
                dv.tensor_tensor(lg[:, :, 0:NE], lg[:, :, 0:NE], over(l1[:, :], 2, NE), ALU.subtract)\
                    .then_inc(S["shift_l"], 1)
                for t in range(GT):
                    i = dv.tensor_tensor(cmq[:, t], cmq[:, t], tri16[:, :, :], ALU.mult)
                i.then_inc(S["eqt"], 1)
                dv.wait_ge(S["eqt"], g + 1)
                dv.tensor_tensor(cmp.rearrange("p a b c -> p (a b c)"), cmp.rearrange("p a b c -> p (a b c)"),
                                 cmq.rearrange("p a b c -> p (a b c)"), ALU.add).then_inc(S["beats"], 1)
                dv.wait_ge(S["beats"], g + 1)
                dv.tensor_reduce(rank[:, :, :], cmp, AX, ALU.add).then_inc(S["rank"], 1)
                dv.wait_ge(S["rank"], g + 1)
                dv.wait_ge(S["exp_l"], g + 1)
                dv.scalar_tensor_tensor(out=comb[:, :, 0:NE], in0=rank[:, :, :], scalar=2.0, in1=lg[:, :, 0:NE],
                                        op0=ALU.is_lt, op1=ALU.mult).then_inc(S["sel"], 1)
                dv.wait_ge(S["sel"], g + 1)
                dv.tensor_reduce(wsum[:, :], comb[:, :, 0:NE], AX, ALU.add).then_inc(S["selsum"], 1)
                dv.wait_ge(S["selsum"], g + 1)
                dv.reciprocal(wsum[:, :], wsum[:, :]).then_inc(S["selinv"], 1)
                dv.wait_ge(S["selinv"], g + 1)
                dv.tensor_tensor(comb[:, :, 0:NE], comb[:, :, 0:NE], over(wsum[:, :], 2, NE), ALU.mult)
                dv.wait_ge(S["expg"], g + 1)
                dv.tensor_scalar(comb[:, :, NE:NE + 1], comb[:, :, NE:NE + 1], 1.0, None, ALU.add).then_inc(S["cgate"], 1)
                dv.wait_ge(S["cgate"], g + 1)
                dv.reciprocal(comb[:, :, NE:NE + 1], comb[:, :, NE:NE + 1]).then_inc(S["comb"], 1)

            def e_hidden(g, e):
                rows = F_OF(e)
                dv.wait_ge(S["sg"], made(g, e, NB))
                dv.wait_ge(S["h_ps"], made(g, e, NB))
                dv.wait_ge(S["d_ps"], made(g, e - 2, NB))
                dv.tensor_tensor(hh[0:rows, e % 2, :], PS[0:rows, 2 + e % 2, :], sg[0:rows, e % 2, :], ALU.mult)\
                    .then_inc(S["hh"], 1)

            def e_acc(g, e):
                r = e % 2
                dv.wait_ge(S["d_ps"], made(g, e, NB))
                dv.wait_ge(S["comb"], made(g))
                if e:
                    dv.wait_ge(S["acc"], made(g, e - 1, NB - 1))
                for t in range(GT):
                    x = tile(X, g * GT + t)
                    w = min(e, NE)
                    i = dv.scalar_tensor_tensor(out=x, in0=PS[:, 4 + 2 * r + t // 2, (t % 2) * D:(t % 2 + 1) * D],
                                                scalar=comb[:, t, w:w + 1], in1=x, op0=ALU.mult, op1=ALU.add)
                    if e == NB - 1:
                        i.then_inc(S["x_done"], 1)
                if e < NB - 1:
                    i.then_inc(S["acc"], 1)

            dv.wait_ge(S["tri"], 2)
            with dv.Fori(0, NG) as g:
                for t in range(GT):
                    i = 2 * NSEQ + g * GT + t
                    ln(i, g * GT + t)
                    ln_apply(i, g * GT + t)
                router(g)
                e_hidden(g, 0)
                for e in range(NB):
                    if e + 1 < NB:
                        e_hidden(g, e + 1)
                    e_acc(g, e)

            dv.wait_ge(S["atz"], 1)
            dv.wait_ge(S["trim"], 2)
            with dv.Fori(0, NSEQ) as b:
                i = 3 * NSEQ + b
                ln(i, b)
                ln_apply(i, b)
                dv.wait_ge(S["g_z"], made(b))
                dv.wait_ge(S["g_ln"], made(b))
                dv.scalar_tensor_tensor(out=g_lg, in0=g_zb, scalar=0.0, in1=g_t1, op0=ALU.min,
                                        op1=ALU.subtract).then_inc(S["g_log"], 1)
                dv.wait_ge(S["g_log"], made(b))
                for c in range(DC):
                    k = dv.tensor_tensor_scan(g_cum[:, c, :], ones[:, :], g_lg[:, c, :], 0.0, ALU.mult, ALU.add)
                k.then_inc(S["g_cum"], 1)
                mid = g_cum.rearrange("p c (n t) -> p c n t", n=NCB)[:, :, :, CB // 2 - 1]
                dv.wait_ge(S["g_cum"], b + 1)
                dv.wait_ge(S["g_a_ps"], made(b - 1))
                dv.tensor_tensor(g_qx.rearrange("p c (n t) -> p c n t", n=NCB),
                                 g_cum.rearrange("p c (n t) -> p c n t", n=NCB), over(mid, 3, CB), ALU.subtract)\
                    .then_inc(S["g_dq"], 1)
                for n in range(NCB):
                    w = CB * (n + 1)
                    k = dv.tensor_tensor(k_block(n), over(mid[:, :, n], 2, w), g_cum[:, :, 0:w], ALU.subtract)
                k.then_inc(S["g_dk"], 1)
                dv.wait_ge(S["g_eq"], b + 1)
                dv.wait_ge(S["g_qk"], made(b))
                dv.scalar_tensor_tensor(out=g_qx, in0=g_qk[:, 0:DC, :], scalar=float(D // H1) ** -0.5, in1=g_qx,
                                        op0=ALU.mult, op1=ALU.mult).then_inc(S["g_qx"], 1)
                dv.wait_ge(S["g_ek"], b + 1)
                for n in range(NCB):
                    k = dv.tensor_tensor(k_block(n), k_block(n), g_qk[:, DC:2 * DC, 0:CB * (n + 1)], ALU.mult)
                k.then_inc(S["g_kx"], 1)
                dv.wait_ge(S["trim"], 2)
                dv.wait_ge(S["g_a_ps"], made(b))
                dv.wait_ge(S["g_o_ps"], made(b - 1))
                for n in range(NCB):
                    w, t0 = CB * (n + 1), CB * n
                    for par in range(2):
                        k = dv.copy_predicated(
                            g_at[0:w, par, :, t0:t0 + CB],
                            over(trim[0:w, t0:t0 + CB], 1, DC).bitcast(mybir.dt.int32),
                            PS[0:w, 5 + par, 0:D].rearrange("p (c t) -> p c t", c=DC)[:, :, t0:t0 + CB])
                k.then_inc(S["g_at"], 1)
                dv.wait_ge(S["g_ss"], made(b))
                dv.tensor_scalar(g_ss, g_ss, 1.0 / P, EPS, ALU.mult, ALU.add).then_inc(S["g_ve"], 1)
                dv.wait_ge(S["g_rr"], made(b))
                dv.wait_ge(S["g_g2"], made(b))
                for h in range(H1):
                    k = dv.scalar_tensor_tensor(out=g_y[:, h * P:(h + 1) * P], in0=PS[:, 7, h * P:(h + 1) * P],
                                                scalar=g_rr[:, h:h + 1], in1=g_gate[:, h * P:(h + 1) * P],
                                                op0=ALU.mult, op1=ALU.mult)
                k.then_inc(S["g_y"], 1)
                dv.wait_ge(S["g_out_ps"], b + 1)
                dv.tensor_tensor(tile(X, b), PS[:, 6, 0:D], tile(X, b), ALU.add).then_inc(S["x_done"], 1)

            dv.wait_ge(S["x_done"], made(4 * NSEQ - 1))
            with dv.Fori(0, NSEQ) as b:
                i = LAST + 2 * b
                ln(i, b)
                dv.wait_ge(S["m_o"], made(b - 1))
                dv.tensor_copy(cn[:, :], tile(C, b)).then_inc(S["m_add"], 1)
                dv.tensor_scalar(m_hide, tile(pad4, b).bitcast(U8), -BIG, None, ALU.mult).then_inc(S["m_add"], 1)
                ln_apply(i, b)
                dv.wait_ge(S["m_add"], 3 * b + 2)
                dv.wait_ge(S["m_s_ps"], b + 1)
                dv.tensor_tensor(m_s, PS[:, 2, 0:P], m_hide, ALU.add).then_inc(S["m_add"], 1)
                dv.wait_ge(S["m_add"], 3 * b + 3)
                dv.tensor_scalar(m_s, m_s, -1.0, None, ALU.mult).then_inc(S["m_neg"], 1)
                dv.wait_ge(S["m_neg"], b + 1)
                dv.tensor_reduce(m_low, m_s, AX, ALU.min).then_inc(S["m_s"], 1)
                dv.wait_ge(S["m_exp"], made(b))
                dv.reciprocal(m_inv, m_sum).then_inc(S["m_inv"], 1)
                dv.wait_ge(S["m_inv"], b + 1)
                dv.wait_ge(S["m_o_ps"], b + 1)
                dv.tensor_scalar(m_o, PS[:, 4, 0:D], m_inv, None, ALU.mult).then_inc(S["m_o"], 1)
                dv.wait_ge(S["m_out_ps"], b + 1)
                dv.wait_ge(S["x_biased"], made(2 * NSEQ + 2 * b))
                dv.tensor_tensor(tile(X, b), PS[:, 6, 0:D], tile(X, b), ALU.add).then_inc(S["x_done"], 1)
                dv.wait_ge(S["hmask"], 3)
                dv.wait_ge(S["x_done"], made(i))
                ln(i + 1, b)
                ln_apply(i + 1, b)
                dv.tensor_tensor(tile(X, b), tile(X, b), f_b[:, :], ALU.add).then_inc(S["x_biased"], 1)
                dv.wait_ge(S["f_out_ps"], b + 1)
                dv.wait_ge(S["x_biased"], made(2 * NSEQ + 2 * b + 1))
                dv.tensor_tensor(tile(X, b), PS[:, 7, D:2 * D], tile(X, b), ALU.add).then_inc(S["x_done"], 1)


_INS = ["x", "ctx_1024", "mask_S2_ff1", "mask_BxS2_bk0",
        "L0_attn_Wq", "L0_attn_Wk", "L0_attn_Wv", "L0_attn_Wo", "L0_attn_bo", "L0_attn_rel_emb",
        "L0_xattn_Wq", "L0_xattn_bq", "L0_xattn_Wk", "L0_xattn_bk", "L0_xattn_Wv", "L0_xattn_bv", "L0_xattn_Wo",
        "L0_xattn_bo",
        "L0_ffn_gate_w", "L0_ffn_w_gate_up", "L0_ffn_w_down", "L0_ffn_shared_w_gate", "L0_ffn_shared_w_up",
        "L0_ffn_shared_w_down", "L0_ffn_shared_gate_w",
        "L1_attn_Wq", "L1_attn_Wk", "L1_attn_Wv", "L1_attn_Wg", "L1_attn_Wgk1", "L1_attn_Wgk2", "L1_attn_bgk2",
        "L1_attn_Wout", "L1_attn_rms_w",
        "L1_xattn_Wq", "L1_xattn_bq", "L1_xattn_Wk", "L1_xattn_bk", "L1_xattn_Wo", "L1_xattn_bo",
        "L1_ffn_weight", "L1_ffn_alpha", "L1_ffn_bias"]


def kernel(**inputs):
    import numpy as _np
    import concourse.bacc as _bacc
    from concourse import mybir as _mybir
    from concourse.bass_utils import run_bass_kernel_spmd as _run

    nc = _bacc.Bacc("TRN2", target_bir_lowering=False, num_devices=1)
    arrays, aps = {}, {}
    for name in _INS:
        a = _np.ascontiguousarray(inputs[name])
        if a.dtype == _np.bool_:
            a = a.view(_np.int32)
        arrays[f"in_{name}"] = a
        aps[name] = nc.dram_tensor(f"in_{name}", a.shape, _mybir.dt.from_np(a.dtype), kind="ExternalInput").ap()
    out = nc.dram_tensor("out_0", (NSEQ, P, D), _mybir.dt.from_np(_np.dtype("float32")), kind="ExternalOutput").ap()
    build(nc, aps, out)
    r = _run(nc, [arrays], core_ids=[0])
    return r.results[0]["out_0"]
```

```python
from contextlib import ExitStack

import concourse.bass as bass
from concourse import mybir

F32 = mybir.dt.float32
U8 = mybir.dt.uint8
ALU = mybir.AluOpType
ACT = mybir.ActivationFunctionType
AX = mybir.AxisListType.X

P = 128
NSEQ = 16
D = 256
DC = D // P
H0 = 16
HD = D // H0
HC = P // HD
CLIP = 16
BIG = 1e30
EPS = 1e-5
LV = (P, P // 2, P // 4)
KEYS = sum(LV)
LOWK = KEYS - P
VW = HD + 1
NE = 16
FE = 128
FS = 704
NB = NE + -(-FS // FE)
GT = 4
STEP = 14
NG = NSEQ // GT
H1 = 4
DV = 512
CB = 32
NCB = P // CB
GATE_NORM = 32.0
LR = 32

SEMS = """
ld_x ld_x_rest ld_rel ld_a ld_c
consts dist rel_term rel_sum
ln_stats ln_aggr ln_var rstd xn xnT_ps xnT x_biased x_done
q_ps kv_ps kT q_heads v s_ps scaled maxed expd pt_ps pt o_ps o_inv ctx ctxT_ps ctxT out_ps
ld_b ld_e ld_w ld_m stored
x_cn x_bv x_bias_ps x_sig x_sigd x_bias
cT mean_sum means k_ps kx qh v2_ps v2 s2_ps maxed2 shifted expd2 pt2_ps pt2 o2_ps o2_inv o2_part
turn_ps turned_a turned_v w_tot w_mean w_step
gl_stats gl_aggr gl_var gl_rstd
r_ps logits top1 gt eqt beats rank shift_l exp_l sel selsum cgate expg comb xT_in comb_in
g_ps h_ps sg hh d_ps acc
g_qk_ps g_qk g_gk_ps g_gk g_z_ps g_z g_v_ps g_v g_g_ps g_gate g_abs g_exp g_ln g_log g_cum g_dq g_dk g_eq g_ek
g_qx g_kx g_a_ps g_at g_o_ps g_ss g_ve g_rr g_g2 g_y g_yT_ps g_yT g_out_ps atz
m_cn m_hide m_cT m_qk_ps m_qk m_s_ps m_masked m_neg m_low m_exp m_pT_ps m_pT m_o_ps m_inv m_o m_oT_ps m_oT m_out_ps
m_biased m_done f_stats f_aggr f_var f_rstd f_xn f_xnT_ps f_xnT f_biased f_out_ps
""".split()
CREDITED = {"rstd": 1, "xn": 1, "xnT_ps": 1, "xnT": 1, "x_biased": 1, "x_done": 1, "q_ps": 1, "kv_ps": 1, "kT": 1,
            "q_heads": 1, "v": 1, "s_ps": 4, "expd": 4, "pt_ps": 4, "pt": 4, "o_ps": 1, "out_ps": 1,
            "cT": 1, "means": 2, "x_cn": 1, "k_ps": 1, "kx": 1, "qh": 1, "v2_ps": 1, "v2": 1, "s2_ps": 8, "shifted": 8,
            "expd2": 8, "pt2_ps": 8, "pt2": 8, "o2_ps": 1,
            "r_ps": 1, "comb": 1, "g_ps": NB, "h_ps": NB, "sg": NB, "hh": NB, "d_ps": NB, "acc": NB - 1,
            "gl_rstd": 1}


def made(tile, part=0, parts=1):
    return (tile + 1) * parts + part + 1


def over(ap, at, n):
    ap = ap.unsqueeze(at)
    shape = list(ap.shape)
    shape[at] = n
    return ap.broadcast_to(shape)


def build(nc, A, out):
    with ExitStack() as ctx:
        def sb(name, shape, dt=F32):
            return ctx.enter_context(nc.sbuf_tensor(name, shape, dt))

        S = {n: ctx.enter_context(nc.semaphore(n)) for n in SEMS}
        PS = ctx.enter_context(nc.psum_tensor("PS", [P, 8, 512], F32))

        X = sb("X", [P, NSEQ, D])
        C = sb("C", [P, NSEQ, D])
        ident = sb("ident_sb", [P, P])
        hmask = sb("hmask_sb", [P, HC])
        mhalf = sb("mhalf_sb", [P, 1])
        half = sb("half", [P, 1])
        stats = sb("stats", [P, 6])
        mv = sb("mv", [P, 2])
        var = sb("var", [P, 1])
        rstd = sb("rstd_sb", [P, 1])
        xn = sb("xn_sb", [P, D])
        xnT = sb("xnT_sb", [P, DC, P])
        a_wq, a_wk, a_wv, a_wo = (sb(f"a_{n}", [P, DC, D]) for n in ("wq", "wk", "wv", "wo"))
        a_bo = sb("a_bo", [P, D])
        rel = sb("rel", [P, CLIP + 1])
        dist = sb("dist_sb", [P, P])
        relT = sb("relT", [P, P])
        csum = dist[:, :].rearrange("p (c t) -> p c t", c=DC)
        nA = sb("nA", [P, P])
        hide = sb("hide", [P, P])
        kT = sb("kT_sb", [P, DC, P])
        q_heads = sb("q_heads_sb", [P, H0, P])
        va = sb("va", [P, H0, HD + 1])
        low = sb("low", [P, H0])
        o_inv = sb("o_inv_sb", [P, H0])
        cx = sb("cx", [P, D])
        cxT = sb("cxT", [P, DC, P])

        x_wq, x_wk, x_wv, x_wo = (sb(f"x_{n}", [P, DC, D]) for n in ("wq", "wk", "wv", "wo"))
        x_bq, x_bk, x_bv = (sb(f"x_{n}", [P, DC]) for n in ("bq", "bk", "bv"))
        x_bo = sb("x_bo", [P, D])
        x_sm = sb("x_sm", [P, 1])
        x_bvb = sb("x_bvb", [P, DC, P])
        cT = sb("cT_sb", [P, DC, KEYS])
        kx = sb("kx_sb", [P, DC, KEYS])
        vx = sb("vx", [P, H0, VW])
        vlow = sb("vlow", [P, H0, 2 * VW])
        mx = sb("mx", [P, H0, 3])
        o2_inv = sb("o2_inv_sb", [P, 2, 8, 3])
        o2_part = sb("o2_part_sb", [P, 2, 8, 3, HD])
        s_g = sb("s_g", [P, DC, FS])
        s_u = sb("s_u", [P, DC, FS])
        s_dn = sb("s_dn", [P, NB - NE, D])
        gwT = sb("gwT", [P, DC, NE + 1])
        lg = sb("lg", [P, GT, NE + 1])
        l1 = sb("l1", [P, GT])
        tri16 = sb("tri16", [P, NE, NE])
        rank = sb("rank_sb", [P, GT, NE])
        wsum = sb("wsum", [P, GT])
        comb = sb("comb_sb", [P, GT, NE + 1])
        l_wq, l_wk = (sb(f"l_{n}", [P, DC, D]) for n in ("wq", "wk"))
        l_wv, l_wg = (sb(f"l_{n}", [P, DC, DV]) for n in ("wv", "wg"))
        l_gk1 = sb("l_gk1", [P, DC, LR])
        l_gk2 = sb("l_gk2", [LR, D])
        l_bgk = sb("l_bgk", [P, DC])
        l_wo = sb("l_wo", [P, DV // P, D])
        l_rms = sb("l_rms", [P, P])
        trim = sb("trim_sb", [P, P])
        ones = sb("ones", [P, P])
        m_wq, m_wk, m_wo, f_w = (sb(f"m_{n}", [P, DC, D]) for n in ("wq", "wk", "wo", "wf"))
        m_bq, m_bk = (sb(f"m_{n}", [P, DC]) for n in ("bq", "bk"))
        m_bo, f_b = (sb(f"m_{n}", [P, D]) for n in ("bo", "bf"))
        f_alpha = sb("f_alpha", [P, 1])
        f_stat = sb("f_stat", [P, 4])
        pad4 = sb("pad4", [P, NSEQ, P // 4], mybir.dt.int32)

        cn = sb("cn", [P, D])
        work = sb("work", [P, 7760])
        wide = sb("wide", [P, NE * (DC * 2 * FE + D)])

        def part(region, base, *shape):
            n = 1
            for x in shape:
                n *= x
            view = region[:, base:base + n]
            if len(shape) == 1:
                return view
            letters = "abcd"[:len(shape)]
            return view.rearrange(f"p ({' '.join(letters)}) -> p {' '.join(letters)}", **dict(zip(letters, shape)))

        sc = part(work, 0, H0, P)
        ex = part(work, 2048, H0, P)
        pT = part(work, 4096, H0, P)
        sc2 = part(work, 0, H0, KEYS)
        pT2 = part(work, 3584, 8, 512)
        sg = part(work, 0, 2, 512)
        hh = part(work, 1024, 2, 512)
        xT3 = part(work, 2048, DC, GT * P)
        cmp = part(work, 3072, GT, NE, NE)
        cmq = part(work, 4096, GT, NE, NE)
        xTn = part(work, 6144, DC, GT * P)
        combn = part(work, 7168, GT, NE + 1)
        gl_stats, gl_mv = sb("gl_stats_sb", [P, GT, 6]), sb("gl_mv", [P, GT, 2])
        gl_var, gl_rstd = sb("gl_var_sb", [P, GT]), sb("gl_rstd_sb", [P, GT])
        f_stats, f_mv = sb("f_stats_sb", [P, GT, 6]), sb("f_mv", [P, GT, 2])
        f_var, f_rstd = sb("f_var_sb", [P, GT]), sb("f_rstd_sb", [P, GT])
        xn4 = part(work, 5120, GT, D)
        xnT4 = part(work, 6656, GT, DC, P)
        def slots(base, *shape):
            return [part(wide, t * 3072 + base, *shape) for t in range(GT)]

        g_qk = slots(0, 2 * DC, P)
        g_zb = slots(512, DC, P)
        g_t1 = slots(768, DC, P)
        g_v = slots(1024, DV)
        g_gate = slots(1536, DV)
        g_at = slots(2048, 2, 2, P)
        g_yT = slots(2560, DV // P, P)
        g_sq = slots(2560, H1, P)
        KX = CB * NCB * (NCB + 1)
        g_qx = [part(work, t * 2 * D, DC, NCB, 2, CB) for t in range(GT)]
        g_kx = [part(work, GT * 2 * D + t * KX, KX) for t in range(GT)]
        g_gk = [part(work, 6144 + t * P, P) for t in range(GT)]
        g_ss = part(work, 7680, GT, H1)
        g_rr = part(work, 7680 + GT * H1, GT, H1)
        m_qk = slots(0, 2 * DC, P)
        m_s = slots(512, P)
        m_e = slots(640, P)
        m_pT = slots(768, P)
        m_o = slots(896, D)
        m_oT = slots(1152, DC, P)
        m_cT = slots(1408, DC, P)
        m_hide = slots(1664, P)
        cn4 = slots(1792, D)
        f_xn = slots(2048, D)
        f_xnT = slots(2304, DC, P)
        m_low = slots(2560, 1)
        m_sum = slots(2561, 1)
        m_inv = slots(2562, 1)

        e_gu = part(wide, 0, NE, DC, 2 * FE)
        e_dn = part(wide, NE * DC * 2 * FE, NE, D)
        SR = -(-FS // P)
        t_sg = part(wide, 0, SR, D)
        t_su = part(wide, 1536, SR, D)
        t_sd = part(wide, 3072, DC, FS)
        t_gw = part(wide, 4480, D)[0:NE + 1]
        t_lq = part(wide, 4736, DC, D)
        t_lk = part(wide, 5248, DC, D)
        t_lv = part(wide, 5760, DV // P, D)
        t_lg = part(wide, 6784, DV // P, D)
        t_g1 = part(wide, 7808, D)[0:LR]
        t_g2 = part(wide, 8064, DC, LR)
        t_lo = part(wide, 8128, DC, DV)
        t_mq = part(wide, 9152, DC, D)
        t_mk = part(wide, 9664, DC, D)
        t_mo = part(wide, 10176, DC, D)
        t_fw = part(wide, 10688, DC, D)
        t_fl = part(wide, 11200, DC, D)

        turns = []

        def turn(dst, blocks):
            turns.append((dst, blocks))

        def blocks_of(src, rows, c, width=P):
            return [(src[:, r, c * P:(c + 1) * P], n * width) for n, r in enumerate(rows)]

        for src, dst in ((t_sg, s_g), (t_su, s_u)):
            for c in range(DC):
                turn(dst[:, c, 0:4 * P], blocks_of(src, range(4), c))
                turn(dst[:, c, 4 * P:FS], [(src[:, 4, c * P:(c + 1) * P], 0),
                                           (src[0:FS - 5 * P, 5, c * P:(c + 1) * P], P)])
        for k in (0, 2):
            turn(s_dn[:, k:k + 2, :], [(t_sd[:, r, (k + j) * P:(k + j + 1) * P], j * D + r * P)
                                       for j in range(2) for r in range(DC)])
        turn(s_dn[:, 4, :], [(t_sd[:, r, 4 * P:5 * P], r * P) for r in range(DC)])
        turn(s_dn[0:FS - 5 * P, 5, :], [(t_sd[:, r, 5 * P:FS], r * P) for r in range(DC)])
        turn(gwT[:, :, :], [(t_gw[:, c * P:(c + 1) * P], c * (NE + 1)) for c in range(DC)])
        for src, dst in ((t_lq, l_wq), (t_lk, l_wk), (t_mq, m_wq), (t_mk, m_wk), (t_mo, m_wo)):
            turn(dst[:, :, :], [(src[:, r, c * P:(c + 1) * P], c * D + r * P) for c in range(DC) for r in range(DC)])
        for src, dst in ((t_lv, l_wv), (t_lg, l_wg)):
            for c in range(DC):
                turn(dst[:, c, :], blocks_of(src, range(4), c))
        turn(l_gk1[:, :, :], [(t_g1[:, c * P:(c + 1) * P], c * LR) for c in range(DC)])
        turn(l_gk2[:, :], [(t_g2[:, r, :], r * P) for r in range(DC)])
        for k in (0, 2):
            turn(l_wo[:, k:k + 2, :], [(t_lo[:, r, (k + j) * P:(k + j + 1) * P], j * D + r * P)
                                       for j in range(2) for r in range(DC)])
        turn(f_w[:, :, :], [(t_fw[:, r, c * P:(c + 1) * P], c * D + r * P) for c in range(DC) for r in range(DC)])

        def turned(n):
            dst, _ = turns[n]
            ps = PS[0:dst.shape[0], n % 4, 0:dst.free_size()]
            return ps if len(dst.shape) == 2 else ps.rearrange("p (a b) -> p a b", a=dst.shape[1])

        def tile(T, b):
            return T[:, bass.ds(b, 1), :].rearrange("p a d -> p (a d)")

        CONSTS = 19
        LD_A, LD_W, LD_C, LD_B, LD_M, LD_E = (16 * n for n in (5, 19, 1, 9, 7, 8))
        LAST = 4 * NSEQ
        block = ctx.enter_context(nc.Block())

        def piped(eng, front, body):
            front(0)
            with eng.Fori(0, NSEQ - 1) as b:
                body(b, True)
            body(NSEQ - 1, False)

        def k_block(t, n):
            w = CB * (n + 1)
            base = GT * 2 * D + t * KX + DC * CB * (n * (n + 1) // 2)
            return part(work, base, DC, w)

        def tiles(T, g):
            return T[:, bass.ds(g * GT, GT), :]

        def grouped(eng, front, body):
            front(0)
            with eng.Fori(0, NG - 1) as g:
                body(g, True)
            body(NG - 1, False)

        def F_OF(e):
            return min(FE, FS - (e - NE) * FE) if e >= NE else FE

        def w_in(ap):
            return ap.rearrange("(c p) n -> p c n", p=P)

        @block.sync
        def _(sp):
            xv = A["x"].rearrange("b t d -> t b d")

            def load(dst, src, done, slow=False):
                sp.dma_start(dst, src, allow_slow_non_contiguous=slow).then_inc(done, 16)

            def all_rows(name):
                return A[name].partition_broadcast(P)

            def column(name):
                return A[name].rearrange("(c p) -> p c", p=P)

            load(rel[:, :], all_rows("L0_attn_rel_emb"), S["ld_rel"])
            load(X[:, 0:4, :], xv[:, 0:4, :], S["ld_x"])
            for t, n in ((a_wq, "L0_attn_Wq"), (a_wk, "L0_attn_Wk"), (a_wv, "L0_attn_Wv"), (a_wo, "L0_attn_Wo")):
                load(t[:, :, :], w_in(A[n]), S["ld_a"])
            load(a_bo[:, :], all_rows("L0_attn_bo"), S["ld_a"])
            load(X[:, 4:NSEQ, :], xv[:, 4:NSEQ, :], S["ld_x_rest"])
            for t, n in ((t_sg, "L0_ffn_shared_w_gate"), (t_su, "L0_ffn_shared_w_up")):
                load(t[:, 0:5, :], A[n][0:5 * P, :].rearrange("(r p) d -> p r d", p=P), S["ld_w"])
                load(t[0:FS - 5 * P, 5, :], A[n][5 * P:FS, :], S["ld_w"])
            load(t_gw[0:NE, :], A["L0_ffn_gate_w"], S["ld_w"])
            load(t_gw[NE:NE + 1, :], A["L0_ffn_shared_gate_w"], S["ld_w"])
            load(t_g1[:, :], A["L1_attn_Wgk1"], S["ld_w"])
            for t, n in ((t_sd, "L0_ffn_shared_w_down"), (t_lq, "L1_attn_Wq"), (t_lk, "L1_attn_Wk"),
                         (t_lv, "L1_attn_Wv"), (t_lg, "L1_attn_Wg"), (t_g2, "L1_attn_Wgk2"),
                         (t_lo, "L1_attn_Wout"), (t_mq, "L1_xattn_Wq"), (t_mk, "L1_xattn_Wk"),
                         (t_mo, "L1_xattn_Wo"), (t_fw, "L1_ffn_weight")):
                load(t[:, :, :], A[n].rearrange("(r p) d -> p r d", p=P), S["ld_w"])
            load(f_alpha[:, :], all_rows("L1_ffn_alpha"), S["ld_w"])
            load(C[:, :, :], A["ctx_1024"].rearrange("b t d -> t b d"), S["ld_c"])
            for t, n in ((x_wq, "Wq"), (x_wk, "Wk"), (x_wv, "Wv"), (x_wo, "Wo")):
                load(t[:, :, :], w_in(A["L0_xattn_" + n]), S["ld_b"])
            for t, n in ((x_bq, "bq"), (x_bk, "bk"), (x_bv, "bv")):
                load(t[:, :], column("L0_xattn_" + n), S["ld_b"], slow=True)
            load(x_bo[:, :], all_rows("L0_xattn_bo"), S["ld_b"])
            load(x_sm[:, :], A["mask_S2_ff1"].rearrange("(p a) -> p a", a=1), S["ld_b"], slow=True)
            load(l_bgk[:, :], column("L1_attn_bgk2"), S["ld_m"], slow=True)
            load(l_rms[:, :], all_rows("L1_attn_rms_w"), S["ld_m"])
            for t, n in ((m_bq, "L1_xattn_bq"), (m_bk, "L1_xattn_bk")):
                load(t[:, :], column(n), S["ld_m"], slow=True)
            load(m_bo[:, :], all_rows("L1_xattn_bo"), S["ld_m"])
            load(f_b[:, :], all_rows("L1_ffn_bias"), S["ld_m"])
            load(pad4.rearrange("p b t -> p (b t)"), A["mask_BxS2_bk0"].rearrange("b t -> (b t)").partition_broadcast(P), S["ld_m"])
            sp.wait_ge(S["turn_ps"], len(turns))
            for e in range(0, NE, 4):
                load(e_gu[:, e:e + 4, :, :].rearrange("p e c n -> p (e c) n"),
                     A["L0_ffn_w_gate_up"][e:e + 4].rearrange("e (c p) n -> p (e c) n", p=P), S["ld_e"])
                load(e_dn[:, e:e + 4, :], A["L0_ffn_w_down"][e:e + 4].rearrange("e f n -> f e n"), S["ld_e"])
            for done, n in ((S["ld_c"], LD_C), (S["ld_b"], LD_B), (S["ld_m"], LD_M), (S["ld_w"], LD_W), (S["ld_e"], LD_E)):
                sp.wait_ge(done, n)
            with sp.Fori(0, NSEQ) as b:
                sp.wait_ge(S["x_done"], made(LAST + b))
                load(out[bass.ds(b, 1)].rearrange("b t d -> t (b d)"), tile(X, b), S["stored"])
            sp.wait_ge(S["stored"], 16 * NSEQ)

        @block.gpsimd
        def _(gp):
            for name, n in CREDITED.items():
                gp.sem_inc(S[name], n)
            for buf, value in ((mhalf[:, :], -0.5), (half[:, :], 0.5), (ident[:, :], 0.0), (hmask[:, :], 1.0),
                               (hide[:, :], 0.0), (va[:, :, HD:VW], 1.0), (tri16[:, :, :], 1.0), (trim[:, :], 1.0),
                               (ones[:, :], 1.0), (vlow[:, :, :], 0.0),
                               (vx[:, :, HD:VW], 0.75)):
                gp.memset(buf, value).then_inc(S["consts"], 1)
            gp.wait_ge(S["consts"], 11)
            gp.memset(vlow[0:LV[1], :, HD:VW], 3.0).then_inc(S["consts"], 1)
            gp.wait_ge(S["consts"], 12)
            gp.memset(vlow[LV[1]:LOWK, :, VW + HD:2 * VW], 3.0).then_inc(S["consts"], 1)
            gp.wait_ge(S["consts"], 13)
            gp.affine_select(out=tri16[:, :, :], in_=tri16[:, :, :], compare_op=ALU.is_gt, fill=0.0, base=0,
                             pattern=[[1, NE], [-1, NE]], channel_multiplier=0).then_inc(S["consts"], 1)
            gp.affine_select(out=trim[:, :], in_=trim[:, :], compare_op=ALU.is_ge, fill=0.0, base=0,
                             pattern=[[1, P]], channel_multiplier=-1).then_inc(S["consts"], 1)
            gp.affine_select(out=ident[:, :], in_=ident[:, :], compare_op=ALU.not_equal, fill=1.0,
                             base=0, pattern=[[-1, P]], channel_multiplier=1).then_inc(S["consts"], 1)
            gp.affine_select(out=hide[:, :], in_=hide[:, :], compare_op=ALU.is_ge, fill=BIG,
                             base=0, pattern=[[-1, P]], channel_multiplier=1).then_inc(S["consts"], 1)
            gp.affine_select(out=hmask[:, :], in_=hmask[:, :], compare_op=ALU.is_ge, fill=0.0,
                             base=0, pattern=[[-HD, HC]], channel_multiplier=1).then_inc(S["consts"], 1)
            gp.wait_ge(S["consts"], 18)
            gp.affine_select(out=hmask[:, :], in_=hmask[:, :], compare_op=ALU.is_ge, fill=0.0,
                             base=HD - 1, pattern=[[HD, HC]], channel_multiplier=-1).then_inc(S["consts"], 1)
            gp.iota(dist[:, :], pattern=[[-1, P]], base=0, channel_multiplier=1,
                    allow_small_or_imprecise_dtypes=True).then_inc(S["dist"], 1)

            def ln(i):
                gp.wait_ge(S["ln_var"], i + 1)
                gp.wait_ge(S["xn"], made(i - 1))
                gp.tensor_tensor(rstd[:, :], var[:, :], mhalf[:, :], ALU.pow).then_inc(S["rstd"], 1)

            def bias_x(i, b, bias):
                gp.wait_ge(S["xn"], made(i))
                gp.tensor_tensor(tile(X, b), tile(X, b), bias[:, :], ALU.add).then_inc(S["x_biased"], 1)

            gp.wait_ge(S["consts"], CONSTS)
            gp.wait_ge(S["ld_a"], LD_A)

            def front(b):
                ln(b)
                bias_x(b, b, a_bo)

            piped(gp, front, lambda b, more: front(b + 1) if more else None)

            def x_front(b):
                i = NSEQ + b
                ln(i)
                bias_x(i, b, x_bo)
                for lv, (src, dst, n) in enumerate(((LOWK, 0, P), (0, LV[1], LV[1]))):
                    if lv == 0:
                        gp.wait_ge(S["cT"], made(b))
                    else:
                        gp.wait_ge(S["means"], made(b, 0, 2))
                    pair = cT[:, :, src:src + n].rearrange("p c (t a) -> p c t a", a=2)
                    gp.tensor_tensor(csum[:, :, 0:n // 2], pair[:, :, :, 0], pair[:, :, :, 1], ALU.add)\
                        .then_inc(S["mean_sum"], 1)
                    gp.wait_ge(S["mean_sum"], 2 * b + lv + 1)
                    gp.tensor_tensor(cT[:, :, dst:dst + n // 2], csum[:, :, 0:n // 2],
                                     half[:, 0:1].unsqueeze(2).broadcast_to([P, DC, n // 2]), ALU.mult)\
                        .then_inc(S["means"], 1)

            gp.wait_ge(S["x_done"], made(NSEQ - 1))
            gp.wait_ge(S["x_bias"], 1)
            piped(gp, x_front, lambda b, more: x_front(b + 1) if more else None)
            def group_ln(n, i):
                gp.wait_ge(S["gl_var"], n + 1)
                gp.wait_ge(S["xn"], made(i - 1))
                gp.tensor_tensor(gl_rstd[:, :], gl_var[:, :], mhalf[:, 0:1].broadcast_to([P, GT]), ALU.pow)\
                    .then_inc(S["gl_rstd"], 1)

            gp.wait_ge(S["x_done"], made(2 * NSEQ - 1))
            with gp.Fori(0, NG) as g:
                group_ln(g, 2 * NSEQ + g * GT)

            def l_front(g):
                group_ln(NG + g, 3 * NSEQ + g * GT)

            def l_body(g, more):
                for t in range(GT):
                    gp.wait_ge(S["g_gate"], g * GT + t + 1)
                    gate = g_gate[t].rearrange("p (h e) -> p h e", h=H1)
                    gp.tensor_tensor(gate, gate, over(l_rms[:, :], 1, H1), ALU.mult).then_inc(S["g_g2"], 1)
                if more:
                    l_front(g + 1)
                gp.wait_ge(S["g_ve"], g + 1)
                gp.tensor_tensor(g_rr, g_ss, mhalf[:, 0:1].unsqueeze(2).broadcast_to([P, GT, H1]), ALU.pow)\
                    .then_inc(S["g_rr"], 1)

            gp.wait_ge(S["x_done"], made(3 * NSEQ - 1))
            for t in range(GT):
                gp.memset(part(wide, t * 3072 + 2048, 2 * 2 * P), 0.0).then_inc(S["atz"], 1)
            gp.memset(part(work, 0, GT * 2 * D), 0.0).then_inc(S["atz"], 1)
            gp.wait_ge(S["ld_m"], LD_M)
            grouped(gp, l_front, l_body)

            def m_front(g):
                group_ln(2 * NG + g, LAST + g * GT)

            def m_body(g, more):
                if more:
                    m_front(g + 1)
                gp.wait_ge(S["f_var"], g + 1)
                gp.tensor_tensor(f_rstd[:, :], f_var[:, :], mhalf[:, 0:1].broadcast_to([P, GT]), ALU.pow)\
                    .then_inc(S["f_rstd"], 1)

            gp.wait_ge(S["x_done"], made(4 * NSEQ - 1))
            grouped(gp, m_front, m_body)

        @block.scalar
        def _(act):
            def ln_xnT(i):
                act.wait_ge(S["xnT_ps"], made(i))
                act.activation(xnT[:, :, :], PS[:, 4, 0:D].rearrange("p (c t) -> p c t", c=DC),
                               ACT.Copy).then_inc(S["xnT"], 1)

            def front_k(b):
                act.wait_ge(S["kv_ps"], made(b))
                act.activation(kT[:, :, :], PS[:, 6, 0:D].rearrange("p (c t) -> p c t", c=DC),
                               ACT.Copy).then_inc(S["kT"], 1)

            def front_v(b):
                act.wait_ge(S["o_ps"], made(b - 1))
                act.activation(va[:, :, 0:HD], PS[:, 6, D:2 * D].rearrange("p (h d) -> p h d", h=H0),
                               ACT.Copy).then_inc(S["v"], 1)

            def exps(b, g):
                act.wait_ge(S["maxed"], b * 4 + g + 1)
                act.wait_ge(S["pt_ps"], made(b - 1, g, 4))
                for h in range(4 * g, 4 * g + 4):
                    i = act.activation(ex[:, h, :], sc[:, h, :], ACT.Exp, bias=low[:, h:h + 1], scale=-1.0)
                i.then_inc(S["expd"], 1)

            def pts(b, g):
                act.wait_ge(S["pt_ps"], made(b, g, 4))
                act.wait_ge(S["o_ps"], made(b - 1))
                act.activation(pT[:, 4 * g:4 * g + 4, :], PS[:, g, :].rearrange("p (h t) -> p h t", h=4),
                               ACT.Copy).then_inc(S["pt"], 1)

            def ctxT(b):
                act.wait_ge(S["ctxT_ps"], b + 1)
                act.activation(cxT[:, :, :], PS[:, 7, 0:D].rearrange("p (c t) -> p c t", c=DC),
                               ACT.Copy).then_inc(S["ctxT"], 1)

            def front(b):
                ln_xnT(b)
                front_k(b)
                front_v(b)
                exps(b, 0)
                exps(b, 1)
                exps(b, 2)

            def body(b, more):
                pts(b, 0)
                pts(b, 1)
                if more:
                    ln_xnT(b + 1)
                exps(b, 3)
                pts(b, 2)
                pts(b, 3)
                if more:
                    front_k(b + 1)
                    front_v(b + 1)
                ctxT(b)
                if more:
                    exps(b + 1, 0)
                    exps(b + 1, 1)
                    exps(b + 1, 2)

            act.wait_ge(S["consts"], CONSTS)
            piped(act, front, body)

            def two(ap):
                return ap.rearrange("p (c t) -> p c t", c=DC)

            def x_T(b):
                act.wait_ge(S["xnT_ps"], made(NSEQ + b))
                act.activation(xnT[:, :, :], two(PS[:, 4, 0:D]), ACT.Copy).then_inc(S["xnT"], 1)
                act.activation(cT[:, :, LOWK:KEYS], two(PS[:, 4, D:2 * D]), ACT.Copy).then_inc(S["cT"], 1)

            def x_k(b):
                act.wait_ge(S["k_ps"], made(b))
                for c in range(DC):
                    i = act.activation(kx[:, c, :], PS[:, 4, c * KEYS:(c + 1) * KEYS], ACT.Identity,
                                       bias=x_bk[:, c:c + 1], scale=1.0)
                i.then_inc(S["kx"], 1)

            def x_v(b):
                act.wait_ge(S["v2_ps"], made(b))
                act.wait_ge(S["o2_ps"], made(b - 1))
                heads = PS[:, 4, :].rearrange("p (a h d) -> p a h d", a=2, h=H0)
                act.activation(vx[:, :, 0:HD], heads[:, 0], ACT.Copy)
                act.activation(vlow[0:LV[1], :, 0:HD], heads[0:LV[1], 1], ACT.Copy)
                act.activation(vlow[LV[1]:LOWK, :, VW:VW + HD], heads[LV[1]:LOWK, 1], ACT.Copy).then_inc(S["v2"], 1)

            def x_exp(b, g):
                act.wait_ge(S["shifted"], made(b, g, 8))
                act.activation(sc2[:, 2 * g:2 * g + 2, :], sc2[:, 2 * g:2 * g + 2, :], ACT.Exp,
                               scale=float(HD) ** -0.5).then_inc(S["expd2"], 1)

            def x_pT(b, g):
                act.wait_ge(S["pt2_ps"], made(b, g, 8))
                act.wait_ge(S["o2_ps"], made(b - 1))
                act.activation(pT2[:, g, :], PS[:, 2 + g % 2, :], ACT.Copy).then_inc(S["pt2"], 1)

            def x_ctxT(b):
                act.wait_ge(S["ctxT_ps"], NSEQ + b + 1)
                act.activation(cxT[:, :, :], two(PS[:, 7, 0:D]), ACT.Copy).then_inc(S["ctxT"], 1)

            def turn_weights():
                for n in range(0, len(turns), 2):
                    act.wait_ge(S["turn_ps"], n + 1)
                    act.activation(turns[n][0], turned(n), ACT.Copy).then_inc(S["turned_a"], 1)



            def x_front(b):
                x_T(b)
                x_k(b)
                x_v(b)
                turn_weights()
                x_exp(b, 0)

            def x_body(b, more):
                for g in range(8):
                    if g:
                        x_exp(b, g)
                        x_pT(b, g - 1)
                    if g == 4 and more:
                        x_T(b + 1)
                    if g == 7 and more:
                        x_k(b + 1)
                x_pT(b, 7)
                if more:
                    x_v(b + 1)
                x_ctxT(b)
                if more:
                    x_exp(b + 1, 0)

            act.wait_ge(S["ld_b"], LD_B)
            act.activation(x_sm[:, :], x_sm[:, :], ACT.Exp, scale=-1.0).then_inc(S["x_sig"], 1)
            act.wait_ge(S["consts"], CONSTS)
            act.wait_ge(S["x_done"], made(NSEQ - 1))
            piped(act, x_front, x_body)

            def e_silu(g, e):
                rows = F_OF(e)
                act.wait_ge(S["g_ps"], made(g, e, NB))
                act.wait_ge(S["hh"], made(g, e - 2, NB))
                act.activation(sg[0:rows, e % 2, :], PS[0:rows, e % 2, :], ACT.Silu).then_inc(S["sg"], 1)

            act.wait_ge(S["x_done"], made(2 * NSEQ - 1))

            def e_xT(g):
                for t in range(GT):
                    act.wait_ge(S["xnT_ps"], made(2 * NSEQ + g * GT + (t | 1)))
                    act.activation(xTn[:, :, t * P:(t + 1) * P], two(PS[:, 4 + t // 2, (t % 2) * D:(t % 2 + 1) * D]),
                                   ACT.Copy).then_inc(S["xnT"], 1)

            def e_exps(g):
                act.wait_ge(S["shift_l"], g + 1)
                act.activation(lg[:, :, 0:NE], lg[:, :, 0:NE], ACT.Exp).then_inc(S["exp_l"], 1)
                act.activation(combn[:, :, NE:NE + 1], lg[:, :, NE:NE + 1], ACT.Exp, scale=-1.0)\
                    .then_inc(S["expg"], 1)

            def e_front(g):
                e_xT(g)
                e_exps(g)

            def e_body(g, more):
                act.wait_ge(S["h_ps"], made(g - 1, NB - 1, NB))
                act.wait_ge(S["xnT"], made(2 * NSEQ + g * GT + GT - 1))
                act.activation(xT3, xTn, ACT.Copy).then_inc(S["xT_in"], 1)
                for e in range(NB):
                    e_silu(g, e)
                    if e == STEP and more:
                        e_xT(g + 1)
                    if e == STEP + 2 and more:
                        e_exps(g + 1)

            grouped(act, e_front, e_body)

            def l_front(g):
                for t in range(GT):
                    act.wait_ge(S["xnT_ps"], made(3 * NSEQ + g * GT + t))
                    act.activation(xnT4[:, t], two(PS[:, t, 0:D]), ACT.Copy).then_inc(S["xnT"], 1)

            def l_body(g, more):
                for t in range(GT):
                    act.wait_ge(S["g_gk_ps"], g * GT + t + 1)
                    act.activation(g_gk[t][0:LR, :], PS[0:LR, t, D:D + P], ACT.Copy).then_inc(S["g_gk"], 1)
                for t in range(GT):
                    act.wait_ge(S["g_qk_ps"], g * GT + t + 1)
                    act.activation(g_qk[t], PS[:, 4 + t, :].rearrange("p (c t) -> p c t", c=2 * DC), ACT.Copy)\
                        .then_inc(S["g_qk"], 1)
                for t in range(GT):
                    act.wait_ge(S["g_z_ps"], g * GT + t + 1)
                    for c in range(DC):
                        i = act.activation(g_zb[t][:, c, :], PS[:, t, c * P:(c + 1) * P], ACT.Identity,
                                           bias=l_bgk[:, c:c + 1], scale=1.0)
                    i.then_inc(S["g_z"], 1)
                for t in range(GT):
                    act.wait_ge(S["g_z"], g * GT + t + 1)
                    act.activation(g_t1[t], g_zb[t], ACT.Abs).then_inc(S["g_abs"], 1)
                for t in range(GT):
                    act.wait_ge(S["g_abs"], g * GT + t + 1)
                    act.activation(g_t1[t], g_t1[t], ACT.Exp, scale=-1.0).then_inc(S["g_exp"], 1)
                for t in range(GT):
                    act.wait_ge(S["g_exp"], g * GT + t + 1)
                    act.activation(g_t1[t], g_t1[t], ACT.Ln, bias=1.0).then_inc(S["g_ln"], 1)
                for t in range(GT):
                    act.wait_ge(S["g_v_ps"], g * GT + t + 1)
                    act.activation(g_v[t], PS[:, t, :], ACT.Copy).then_inc(S["g_v"], 1)
                for t in range(GT):
                    act.wait_ge(S["g_dq"], g * GT + t + 1)
                    act.activation(g_zb[t], g_zb[t], ACT.Exp, scale=1.0 / GATE_NORM).then_inc(S["g_eq"], 1)
                    act.wait_ge(S["g_dk"], g * GT + t + 1)
                    act.activation(g_kx[t], g_kx[t], ACT.Exp, scale=1.0 / GATE_NORM).then_inc(S["g_ek"], 1)
                for t in range(GT):
                    act.wait_ge(S["g_g_ps"], g * GT + t + 1)
                    act.activation(g_gate[t], PS[:, 4 + t, :], ACT.Silu).then_inc(S["g_gate"], 1)
                for t in range(GT):
                    act.wait_ge(S["g_o_ps"], g * GT + t + 1)
                    for h in range(H1):
                        i = act.activation(g_sq[t][:, h, :], PS[:, 4 + t, h * P:(h + 1) * P], ACT.Square,
                                           accum_out=g_ss[:, t, h:h + 1])
                    i.then_inc(S["g_ss"], 1)
                if more:
                    l_front(g + 1)
                for t in range(GT):
                    act.wait_ge(S["g_yT_ps"], g * GT + t + 1)
                    act.activation(g_yT[t], PS[:, t, :].rearrange("p (h t) -> p h t", h=H1), ACT.Copy)\
                        .then_inc(S["g_yT"], 1)

            act.wait_ge(S["x_done"], made(3 * NSEQ - 1))
            act.wait_ge(S["ld_m"], LD_M)
            grouped(act, l_front, l_body)

            def m_front(g):
                for t in range(GT):
                    act.wait_ge(S["xnT_ps"], made(LAST + g * GT + t))
                    act.activation(xnT4[:, t], two(PS[:, t, 0:D]), ACT.Copy).then_inc(S["xnT"], 1)
                    act.activation(m_cT[t], two(PS[:, t, D:2 * D]), ACT.Copy).then_inc(S["m_cT"], 1)

            def m_body(g, more):
                for t in range(GT):
                    act.wait_ge(S["m_qk_ps"], g * GT + t + 1)
                    for c in range(DC):
                        act.activation(m_qk[t][:, c, :], PS[:, 4 + t, c * P:(c + 1) * P], ACT.Identity,
                                       bias=m_bq[:, c:c + 1], scale=1.0)
                        i = act.activation(m_qk[t][:, DC + c, :], PS[:, 4 + t, D + c * P:D + (c + 1) * P],
                                           ACT.Identity, bias=m_bk[:, c:c + 1], scale=1.0)
                    i.then_inc(S["m_qk"], 1)
                for t in range(GT):
                    act.wait_ge(S["m_low"], g * GT + t + 1)
                    act.activation(m_e[t], m_s[t], ACT.Exp, bias=m_low[t], scale=-1.0, accum_out=m_sum[t])\
                        .then_inc(S["m_exp"], 1)
                for t in range(GT):
                    act.wait_ge(S["m_pT_ps"], g * GT + t + 1)
                    act.activation(m_pT[t], PS[:, t, P:2 * P], ACT.Copy).then_inc(S["m_pT"], 1)
                for t in range(GT):
                    act.wait_ge(S["m_oT_ps"], g * GT + t + 1)
                    act.activation(m_oT[t], two(PS[:, 4 + t, 0:D]), ACT.Copy).then_inc(S["m_oT"], 1)
                if more:
                    m_front(g + 1)
                for t in range(GT):
                    act.wait_ge(S["f_xnT_ps"], g * GT + t + 1)
                    act.activation(f_xnT[t], two(PS[:, 4 + t, 0:D]), ACT.Copy).then_inc(S["f_xnT"], 1)

            act.wait_ge(S["x_done"], made(4 * NSEQ - 1))
            grouped(act, m_front, m_body)

        @block.tensor
        def _(pe):
            def ln_T(i):
                pe.wait_ge(S["xn"], made(i))
                pe.wait_ge(S["xnT"], made(i - 1))
                for c in range(DC):
                    m = pe.transpose(PS[:, 4, c * P:(c + 1) * P], xn[:, c * P:(c + 1) * P], ident[:, :])
                m.then_inc(S["xnT_ps"], 1)

            def q_or_k(b, w, bank):
                for oc in range(DC):
                    for c in range(DC):
                        m = pe.matmul(PS[:, bank, oc * P:(oc + 1) * P], w[:, c, oc * P:(oc + 1) * P],
                                      xnT[:, c, :], start=(c == 0), stop=(c == DC - 1))
                return m

            def qs(b, first=False):
                pe.wait_ge(S["xnT"], made(b))
                if not first:
                    pe.wait_ge(S["x_done"], made(b - 2))
                q_or_k(b, a_wq, 5).then_inc(S["q_ps"], 1)

            def ks(b):
                q_or_k(b, a_wk, 6)

            def vs(b):
                for c in range(DC):
                    m = pe.matmul(PS[:, 6, D:2 * D], xnT[:, c, :], a_wv[:, c, :], start=(c == 0), stop=(c == DC - 1))
                m.then_inc(S["kv_ps"], 1)

            def scores(b):
                pe.wait_ge(S["q_heads"], made(b))
                pe.wait_ge(S["kT"], made(b))
                pe.wait_ge(S["pt"], made(b - 1, 3, 4))
                for g in range(4):
                    for h in range(4 * g, 4 * g + 4):
                        m = pe.matmul(PS[:, g, (h % 4) * P:(h % 4 + 1) * P], q_heads[:, h, :], kT[:, h // HC, :],
                                      start=True, stop=True)
                    m.then_inc(S["s_ps"], 1)

            def p_T(b, g):
                pe.wait_ge(S["expd"], made(b, g, 4))
                for h in range(4 * g, 4 * g + 4):
                    m = pe.transpose(PS[:, g, (h % 4) * P:(h % 4 + 1) * P], ex[:, h, :], ident[:, :])
                m.then_inc(S["pt_ps"], 1)

            def av(b, g):
                if g == 0:
                    pe.wait_ge(S["v"], made(b))
                pe.wait_ge(S["pt"], made(b, g, 4))
                for h in range(4 * g, 4 * g + 4):
                    m = pe.matmul(PS[:, 7, h * (HD + 1):(h + 1) * (HD + 1)], pT[:, h, :], va[:, h, :],
                                  start=True, stop=True)
                if g == 3:
                    m.then_inc(S["o_ps"], 1)

            def ctx_out(b):
                pe.wait_ge(S["ctx"], b + 1)
                for c in range(DC):
                    m = pe.transpose(PS[:, 7, c * P:(c + 1) * P], cx[:, c * P:(c + 1) * P], ident[:, :])
                m.then_inc(S["ctxT_ps"], 1)
                pe.wait_ge(S["ctxT"], b + 1)
                for c in range(DC):
                    m = pe.matmul(PS[:, 5, D:2 * D], cxT[:, c, :], a_wo[:, c, :], start=(c == 0), stop=(c == DC - 1))
                m.then_inc(S["out_ps"], 1)

            def front(b):
                ln_T(b)
                qs(b, first=True)
                ks(b)
                vs(b)
                scores(b)

            def body(b, more):
                p_T(b, 0)
                p_T(b, 1)
                p_T(b, 2)
                av(b, 0)
                if more:
                    ln_T(b + 1)
                av(b, 1)
                if more:
                    qs(b + 1)
                    ks(b + 1)
                p_T(b, 3)
                if more:
                    vs(b + 1)
                av(b, 2)
                av(b, 3)
                if more:
                    scores(b + 1)
                ctx_out(b)

            pe.wait_ge(S["consts"], CONSTS)
            pe.wait_ge(S["ld_a"], LD_A)
            piped(pe, front, body)

            def product(ps, lhsT, rhs, chunks=DC):
                for c in range(chunks):
                    m = pe.matmul(ps, lhsT(c), rhs(c), start=(c == 0), stop=(c == chunks - 1))
                return m

            def x_T(b):
                pe.wait_ge(S["xn"], made(NSEQ + b))
                pe.wait_ge(S["v2"], made(b - 1))
                for c in range(DC):
                    pe.transpose(PS[:, 4, c * P:(c + 1) * P], xn[:, c * P:(c + 1) * P], ident[:, :])
                copy_wait(b)
                for c in range(DC):
                    m = pe.transpose(PS[:, 4, D + c * P:D + (c + 1) * P], cn[:, c * P:(c + 1) * P], ident[:, :])
                m.then_inc(S["xnT_ps"], 1)

            def copy_wait(b):
                pe.wait_ge(S["x_cn"], made(b))

            def x_q(b):
                pe.wait_ge(S["xnT"], made(NSEQ + b))
                for oc in range(DC):
                    m = product(PS[:, 5, oc * P:(oc + 1) * P], lambda c: x_wq[:, c, oc * P:(oc + 1) * P],
                                lambda c: xnT[:, c, :])
                m.then_inc(S["q_ps"], 1)

            def x_k(b):
                pe.wait_ge(S["means"], made(b, 1, 2))
                for oc in range(DC):
                    m = product(PS[:, 4, oc * KEYS:(oc + 1) * KEYS], lambda c: x_wk[:, c, oc * P:(oc + 1) * P],
                                lambda c: cT[:, c, :])
                m.then_inc(S["k_ps"], 1)

            def x_v(b):
                pe.wait_ge(S["kx"], made(b))
                product(PS[:, 4, 0:D], lambda c: cT[:, c, LOWK:KEYS], lambda c: x_wv[:, c, :])
                product(PS[:, 4, D:2 * D], lambda c: cT[:, c, 0:P], lambda c: x_wv[:, c, :])\
                    .then_inc(S["v2_ps"], 1)

            def x_scores(b, g):
                if g == 0:
                    pe.wait_ge(S["qh"], made(b))
                    pe.wait_ge(S["kx"], made(b))
                pe.wait_ge(S["shifted"], made(b, g - 2, 8))
                for j in range(2):
                    h = 2 * g + j
                    m = pe.matmul(PS[:, g % 2, j * KEYS:(j + 1) * KEYS], q_heads[:, h, :], kx[:, h // HC, :],
                                  start=True, stop=True)
                m.then_inc(S["s2_ps"], 1)

            def x_pT(b, g):
                pe.wait_ge(S["expd2"], made(b, g, 8))
                pe.wait_ge(S["pt2"], made(b, g - 2, 8))
                for j in range(2):
                    h = 2 * g + j
                    pe.transpose(PS[:, 2 + g % 2, j * P:(j + 1) * P], sc2[:, h, LOWK:KEYS], ident[:, :])
                    m = pe.transpose(PS[:, 2 + g % 2, D + j * P:D + (j + 1) * P], sc2[:, h, 0:P], ident[:, :])
                m.then_inc(S["pt2_ps"], 1)

            def x_av(b, g):
                if g == 0:
                    pe.wait_ge(S["v2"], made(b))
                    pe.wait_ge(S["x_done"], made(NSEQ + b - 1))
                pe.wait_ge(S["pt2"], made(b, g, 8))
                for j in range(2):
                    h = 2 * g + j
                    o = 3 * VW * (h % 8)
                    pe.matmul(PS[:, 6 + g // 4, o:o + VW], pT2[:, g, j * P:(j + 1) * P], vx[:, h, :],
                              start=True, stop=True)
                    m = pe.matmul(PS[:, 6 + g // 4, o + VW:o + 3 * VW], pT2[:, g, D + j * P:D + (j + 1) * P],
                                  vlow[:, h, :], start=True, stop=True)
                if g == 7:
                    m.then_inc(S["o2_ps"], 1)

            def x_out(b):
                i = NSEQ + b
                pe.wait_ge(S["ctx"], i + 1)
                for c in range(DC):
                    m = pe.transpose(PS[:, 7, c * P:(c + 1) * P], cx[:, c * P:(c + 1) * P], ident[:, :])
                m.then_inc(S["ctxT_ps"], 1)
                pe.wait_ge(S["ctxT"], i + 1)
                product(PS[:, 6, 0:D], lambda c: cxT[:, c, :], lambda c: x_wo[:, c, :]).then_inc(S["out_ps"], 1)

            def turn_weights():
                pe.wait_ge(S["ld_w"], LD_W)
                for n, (dst, blocks) in enumerate(turns):
                    if n == len(turns) - 1:
                        pe.wait_ge(S["w_step"], 5)
                    if n >= 4:
                        if n % 2:
                            pe.wait_ge(S["turned_v"], (n - 3) // 2)
                        else:
                            pe.wait_ge(S["turned_a"], (n - 2) // 2)
                    for src, col in blocks:
                        m = pe.transpose(PS[0:src.shape[1], n % 4, col:col + src.shape[0]], src,
                                         ident[0:src.shape[0], 0:src.shape[0]])
                    m.then_inc(S["turn_ps"], 1)
                pe.wait_ge(S["turned_a"], (len(turns) + 1) // 2)
                pe.wait_ge(S["turned_v"], len(turns) // 2)


            def x_front(b):
                x_T(b)
                x_q(b)
                x_k(b)
                x_v(b)
                turn_weights()
                x_scores(b, 0)
                x_scores(b, 1)

            def x_body(b, more):
                for g in range(8):
                    if g + 2 < 8:
                        x_scores(b, g + 2)
                    x_pT(b, g)
                    if g:
                        x_av(b, g - 1)
                    if g == 3 and more:
                        x_T(b + 1)
                    if g == 4 and more:
                        x_q(b + 1)
                    if g == 6 and more:
                        x_k(b + 1)
                    if g == 7 and more:
                        x_v(b + 1)
                x_av(b, 7)
                if more:
                    x_scores(b + 1, 0)
                    x_scores(b + 1, 1)
                x_out(b)

            pe.wait_ge(S["ld_c"], LD_C)
            pe.wait_ge(S["ld_b"], LD_B)
            pe.wait_ge(S["x_done"], made(NSEQ - 1))
            pe.wait_ge(S["w_tot"], 1)
            pe.matmul(PS[:, 6, 0:1], ones[:, :], f_stat[:, 0:1], start=True, stop=True).then_inc(S["w_mean"], 1)
            pe.wait_ge(S["x_bv"], DC)
            product(PS[:, 7, 0:D], lambda c: x_bvb[:, c, :], lambda c: x_wo[:, c, :]).then_inc(S["x_bias_ps"], 1)
            piped(pe, x_front, x_body)

            def e_up(g, e):
                rows = F_OF(e)
                if e < NE:
                    wg, wu = (lambda c: e_gu[:, e, c, 0:FE]), (lambda c: e_gu[:, e, c, FE:2 * FE])
                else:
                    o = (e - NE) * FE
                    wg, wu = (lambda c: s_g[:, c, o:o + rows]), (lambda c: s_u[:, c, o:o + rows])
                if e == 0:
                    pe.wait_ge(S["xT_in"], g + 1)
                pe.wait_ge(S["sg"], made(g, e - 2, NB))
                product(PS[0:rows, e % 2, :], wg, lambda c: xT3[:, c, :]).then_inc(S["g_ps"], 1)
                pe.wait_ge(S["hh"], made(g, e - 2, NB))
                product(PS[0:rows, 2 + e % 2, :], wu, lambda c: xT3[:, c, :]).then_inc(S["h_ps"], 1)

            def e_down(g, e):
                rows, r = F_OF(e), e % 2
                w = e_dn[:, e, :] if e < NE else s_dn[0:rows, e - NE, :]
                pe.wait_ge(S["hh"], made(g, e, NB))
                if e == 0:
                    pe.wait_ge(S["acc"], made(g - 1, NB - 2, NB - 1))
                elif e == 1:
                    pe.wait_ge(S["x_done"], made(2 * NSEQ + g * GT - 1))
                else:
                    pe.wait_ge(S["acc"], made(g, e - 2, NB - 1))
                for t in range(GT):
                    m = pe.matmul(PS[:, 4 + 2 * r + t // 2, (t % 2) * D:(t % 2 + 1) * D],
                                  hh[0:rows, r, t * P:(t + 1) * P], w, start=True, stop=True)
                m.then_inc(S["d_ps"], 1)

            pe.wait_ge(S["ld_e"], LD_E)
            pe.wait_ge(S["x_done"], made(2 * NSEQ - 1))

            def e_T(g):
                for t in range(GT):
                    pe.wait_ge(S["xn"], made(2 * NSEQ + g * GT + t))
                    for c in range(DC):
                        o = (t % 2) * D + c * P
                        m = pe.transpose(PS[:, 4 + t // 2, o:o + P], xn4[:, t, c * P:(c + 1) * P], ident[:, :])
                    m.then_inc(S["xnT_ps"], 1)

            def e_router(g):
                pe.wait_ge(S["xnT"], made(2 * NSEQ + g * GT + GT - 1))
                for t in range(GT):
                    m = product(PS[:, 4, t * (NE + 1):(t + 1) * (NE + 1)],
                                lambda c: xTn[:, c, t * P:(t + 1) * P], lambda c: gwT[:, c, :])
                m.then_inc(S["r_ps"], 1)

            def e_body(g, more):
                e_up(g, 0)
                for e in range(NB):
                    if e + 1 < NB:
                        e_up(g, e + 1)
                    if e == STEP and more:
                        e_router(g + 1)
                        pe.wait_ge(S["logits"], g + 2)
                    e_down(g, e)
                    if e == STEP - 1 and more:
                        pe.wait_ge(S["acc"], made(g, STEP - 2, NB - 1))
                        e_T(g + 1)

            def e_front(g):
                e_T(g)
                e_router(g)
                pe.wait_ge(S["logits"], g + 1)

            grouped(pe, e_front, e_body)

            def l_front(g):
                for t in range(GT):
                    pe.wait_ge(S["xn"], made(3 * NSEQ + g * GT + t))
                    for c in range(DC):
                        m = pe.transpose(PS[:, t, c * P:(c + 1) * P], xn4[:, t, c * P:(c + 1) * P], ident[:, :])
                    m.then_inc(S["xnT_ps"], 1)

            def l_body(g, more):
                for t in range(GT):
                    pe.wait_ge(S["xnT"], made(3 * NSEQ + g * GT + t))
                    product(PS[0:LR, t, D:D + P], lambda c: l_gk1[:, c, :], lambda c: xnT4[:, t, c, :])\
                        .then_inc(S["g_gk_ps"], 1)
                pe.wait_ge(S["x_done"], made(3 * NSEQ + g * GT - 1))
                for t in range(GT):
                    for n, w in enumerate((l_wq, l_wk)):
                        for oc in range(DC):
                            m = product(PS[:, 4 + t, n * D + oc * P:n * D + (oc + 1) * P],
                                        lambda c: w[:, c, oc * P:(oc + 1) * P], lambda c: xnT4[:, t, c, :])
                    m.then_inc(S["g_qk_ps"], 1)
                for t in range(GT):
                    pe.wait_ge(S["g_gk"], g * GT + t + 1)
                    for oc in range(DC):
                        m = pe.matmul(PS[:, t, oc * P:(oc + 1) * P], l_gk2[:, oc * P:(oc + 1) * P],
                                      g_gk[t][0:LR, :], start=True, stop=True)
                    m.then_inc(S["g_z_ps"], 1)
                for t in range(GT):
                    pe.wait_ge(S["g_z"], g * GT + t + 1)
                    product(PS[:, t, :], lambda c: xnT4[:, t, c, :], lambda c: l_wv[:, c, :]).then_inc(S["g_v_ps"], 1)
                for t in range(GT):
                    pe.wait_ge(S["g_qk"], g * GT + t + 1)
                    product(PS[:, 4 + t, :], lambda c: xnT4[:, t, c, :], lambda c: l_wg[:, c, :])\
                        .then_inc(S["g_g_ps"], 1)
                for t in range(GT):
                    pe.wait_ge(S["consts"], CONSTS)
                    pe.wait_ge(S["g_v"], g * GT + t + 1)
                    pe.wait_ge(S["g_kx"], g * GT + t + 1)
                    pe.wait_ge(S["g_qx"], g * GT + t + 1)
                    for n in range(NCB):
                        w = CB * (n + 1)
                        for c in range(DC):
                            o = (c * NCB + n) * 2 * CB
                            m = pe.matmul(PS[0:w, t, o:o + 2 * CB], k_block(t, n)[:, c, :],
                                          g_qx[t][:, c, n].rearrange("p r t -> p (r t)"), start=True, stop=True)
                    m.then_inc(S["g_a_ps"], 1)
                for t in range(GT):
                    pe.wait_ge(S["g_gate"], g * GT + t + 1)
                    pe.wait_ge(S["g_at"], g * GT + t + 1)
                    for h in range(H1):
                        m = pe.matmul(PS[:, 4 + t, h * P:(h + 1) * P], g_at[t][:, h % 2, h // 2, :],
                                      g_v[t][:, h * P:(h + 1) * P], start=True, stop=True)
                    m.then_inc(S["g_o_ps"], 1)
                if more:
                    l_front(g + 1)
                for t in range(GT):
                    if more:
                        pe.wait_ge(S["xnT"], made(3 * NSEQ + (g + 1) * GT + t))
                    pe.wait_ge(S["g_y"], g * GT + t + 1)
                    for h in range(H1):
                        m = pe.transpose(PS[:, t, h * P:(h + 1) * P], g_gate[t][:, h * P:(h + 1) * P], ident[:, :])
                    m.then_inc(S["g_yT_ps"], 1)
                for t in range(GT):
                    pe.wait_ge(S["g_yT"], g * GT + t + 1)
                    product(PS[:, 4 + t, 0:D], lambda c: g_yT[t][:, c, :], lambda c: l_wo[:, c, :], DV // P)\
                        .then_inc(S["g_out_ps"], 1)

            pe.wait_ge(S["x_done"], made(3 * NSEQ - 1))
            pe.wait_ge(S["consts"], CONSTS)
            grouped(pe, l_front, l_body)

            def m_front(g):
                for t in range(GT):
                    pe.wait_ge(S["xn"], made(LAST + g * GT + t))
                    pe.wait_ge(S["m_cn"], g * GT + t + 1)
                    for n, src in enumerate((xn4[:, t], cn4[t])):
                        for c in range(DC):
                            m = pe.transpose(PS[:, t, n * D + c * P:n * D + (c + 1) * P], src[:, c * P:(c + 1) * P],
                                             ident[:, :])
                    m.then_inc(S["xnT_ps"], 1)

            def m_body(g, more):
                pe.wait_ge(S["x_done"], made(LAST + g * GT - 1))
                for t in range(GT):
                    pe.wait_ge(S["xnT"], made(LAST + g * GT + t))
                    pe.wait_ge(S["m_cT"], g * GT + t + 1)
                    for n, (w, src) in enumerate(((m_wq, xnT4[:, t]), (m_wk, m_cT[t]))):
                        for oc in range(DC):
                            m = product(PS[:, 4 + t, n * D + oc * P:n * D + (oc + 1) * P],
                                        lambda c: w[:, c, oc * P:(oc + 1) * P], lambda c: src[:, c, :])
                    m.then_inc(S["m_qk_ps"], 1)
                for t in range(GT):
                    pe.wait_ge(S["m_qk"], g * GT + t + 1)
                    product(PS[:, t, 0:P], lambda c: m_qk[t][:, c, :], lambda c: m_qk[t][:, DC + c, :])\
                        .then_inc(S["m_s_ps"], 1)
                for t in range(GT):
                    pe.wait_ge(S["m_exp"], g * GT + t + 1)
                    pe.transpose(PS[:, t, P:2 * P], m_e[t], ident[:, :]).then_inc(S["m_pT_ps"], 1)
                for t in range(GT):
                    pe.wait_ge(S["m_pT"], g * GT + t + 1)
                    pe.matmul(PS[:, t, D:2 * D], m_pT[t], cn4[t], start=True, stop=True).then_inc(S["m_o_ps"], 1)
                for t in range(GT):
                    pe.wait_ge(S["m_o"], g * GT + t + 1)
                    for c in range(DC):
                        m = pe.transpose(PS[:, 4 + t, c * P:(c + 1) * P], m_o[t][:, c * P:(c + 1) * P], ident[:, :])
                    m.then_inc(S["m_oT_ps"], 1)
                for t in range(GT):
                    pe.wait_ge(S["m_oT"], g * GT + t + 1)
                    product(PS[:, 4 + t, D:2 * D], lambda c: m_oT[t][:, c, :], lambda c: m_wo[:, c, :])\
                        .then_inc(S["m_out_ps"], 1)
                if more:
                    m_front(g + 1)
                for t in range(GT):
                    pe.wait_ge(S["f_xn"], g * GT + t + 1)
                    for c in range(DC):
                        m = pe.transpose(PS[:, 4 + t, c * P:(c + 1) * P], f_xn[t][:, c * P:(c + 1) * P], ident[:, :])
                    m.then_inc(S["f_xnT_ps"], 1)
                for t in range(GT):
                    pe.wait_ge(S["f_xnT"], g * GT + t + 1)
                    product(PS[:, 4 + t, D:2 * D], lambda c: f_xnT[t][:, c, :], lambda c: f_w[:, c, :])\
                        .then_inc(S["f_out_ps"], 1)

            pe.wait_ge(S["x_done"], made(4 * NSEQ - 1))
            grouped(pe, m_front, m_body)

        @block.vector
        def _(dv):
            def ln_stats(i, b):
                dv.wait_ge(S["rstd"], made(i - 1))
                dv.bn_stats(stats[:, :], tile(X, b)).then_inc(S["ln_stats"], 1)

            def ln_var(i):
                dv.wait_ge(S["consts"], CONSTS)
                dv.wait_ge(S["ln_stats"], i + 1)
                dv.bn_aggr(mv[:, :], stats[:, :]).then_inc(S["ln_aggr"], 1)
                dv.wait_ge(S["ln_aggr"], i + 1)
                dv.tensor_scalar(var[:, :], mv[:, 1:2], EPS, None, ALU.add).then_inc(S["ln_var"], 1)

            def ln(i, b):
                ln_stats(i, b)
                ln_var(i)

            def ln_apply(i, b):
                dv.wait_ge(S["rstd"], made(i))
                dv.wait_ge(S["xnT_ps"], made(i - 1))
                dv.tensor_scalar(xn[:, :], tile(X, b), mv[:, 0:1], rstd[:, 0:1], ALU.subtract,
                                 ALU.mult).then_inc(S["xn"], 1)

            def q_split(b):
                dv.wait_ge(S["q_ps"], made(b))
                for c in range(DC):
                    i = dv.tensor_tensor(q_heads[:, c * HC:(c + 1) * HC, :],
                                         over(PS[:, 5, c * P:(c + 1) * P], 1, HC), over(hmask[:, :], 2, P), ALU.mult)
                i.then_inc(S["q_heads"], 1)

            def scale(b, g):
                dv.wait_ge(S["s_ps"], made(b, g, 4))
                dv.wait_ge(S["expd"], made(b - 1, g, 4))
                dv.tensor_tensor(sc[:, 4 * g:4 * g + 4, :], PS[:, g, :].rearrange("p (h t) -> p h t", h=4),
                                 over(nA[:, :], 1, 4), ALU.mult).then_inc(S["scaled"], 1)

            def hide_max(b, g):
                dv.wait_ge(S["consts"], CONSTS)
                dv.wait_ge(S["scaled"], b * 4 + g + 1)
                for h in range(4 * g, 4 * g + 4):
                    i = dv.tensor_tensor_reduce(sc[:, h, :], sc[:, h, :], hide[:, :], 1.0, BIG, ALU.add, ALU.min,
                                                low[:, h:h + 1])
                i.then_inc(S["maxed"], 1)

            def norm(b):
                dv.wait_ge(S["o_ps"], made(b))
                o = PS[:, 7, 0:H0 * (HD + 1)].rearrange("p (h d) -> p h d", h=H0)
                dv.reciprocal(o_inv[:, :].unsqueeze(2), o[:, :, HD:HD + 1]).then_inc(S["o_inv"], 1)
                dv.wait_ge(S["o_inv"], b + 1)
                dv.tensor_tensor(cx[:, :].rearrange("p (h d) -> p h d", h=H0), o[:, :, 0:HD],
                                 over(o_inv[:, :], 2, HD), ALU.mult).then_inc(S["ctx"], 1)

            def add_x(b):
                dv.wait_ge(S["out_ps"], made(b))
                dv.wait_ge(S["x_biased"], made(b))
                dv.tensor_tensor(tile(X, b), PS[:, 5, D:2 * D], tile(X, b), ALU.add).then_inc(S["x_done"], 1)

            def relative(d):
                return part(work, d * P, P)

            def rel_bias():
                dv.wait_ge(S["dist"], 1)
                dv.wait_ge(S["ld_rel"], 16)
                dv.tensor_scalar(dist[:, :], dist[:, :], float(CLIP), None, ALU.min).then_inc(S["dist"], 1)
                dv.tensor_scalar(rel[:, :], rel[:, :], -float(HD) ** -0.5, None, ALU.mult).then_inc(S["dist"], 1)
                dv.wait_ge(S["dist"], 3)
                for d in range(CLIP + 1):
                    i = dv.tensor_scalar(relative(d), dist[:, :], float(d), None, ALU.is_equal)
                i.then_inc(S["rel_term"], 1)
                sums = nA, relT
                dv.wait_ge(S["rel_term"], 1)
                for d in range(2):
                    dv.tensor_scalar(sums[d][:, :], relative(d), rel[:, d:d + 1], None, ALU.mult)\
                        .then_inc(S["rel_sum"], 1)
                for d in range(2, CLIP + 1):
                    dv.wait_ge(S["rel_sum"], d - 1)
                    dv.scalar_tensor_tensor(out=sums[d % 2][:, :], in0=relative(d), scalar=rel[:, d:d + 1],
                                            in1=sums[d % 2][:, :], op0=ALU.mult, op1=ALU.add)\
                        .then_inc(S["rel_sum"], 1)
                dv.wait_ge(S["rel_sum"], CLIP + 1)
                dv.tensor_tensor(nA[:, :], nA[:, :], relT[:, :], ALU.add).then_inc(S["rel_sum"], 1)

            def front(b):
                ln(b, b)
                ln_apply(b, b)
                rel_bias()
                q_split(b)
                dv.wait_ge(S["rel_sum"], CLIP + 2)
                dv.wait_ge(S["ld_x_rest"], 16)
                scale(b, 0)
                scale(b, 1)
                hide_max(b, 0)
                hide_max(b, 1)
                scale(b, 2)
                hide_max(b, 2)

            def body(b, more):
                if more:
                    ln_stats(b + 1, b + 1)
                scale(b, 3)
                if more:
                    ln_var(b + 1)
                hide_max(b, 3)
                if more:
                    ln_apply(b + 1, b + 1)
                if more:
                    q_split(b + 1)
                norm(b)
                if more:
                    scale(b + 1, 0)
                    scale(b + 1, 1)
                    hide_max(b + 1, 0)
                    hide_max(b + 1, 1)
                    scale(b + 1, 2)
                    hide_max(b + 1, 2)
                add_x(b)

            dv.wait_ge(S["consts"], CONSTS)
            dv.wait_ge(S["ld_x"], 16)
            piped(dv, front, body)

            def x_ctx(b):
                dv.wait_ge(S["cT"], made(b - 1))
                dv.tensor_copy(cn[:, :], tile(C, b)).then_inc(S["x_cn"], 1)

            def x_q(b):
                dv.wait_ge(S["q_ps"], made(NSEQ + b))
                dv.wait_ge(S["s2_ps"], made(b - 1, 7, 8))
                for c in range(DC):
                    i = dv.scalar_tensor_tensor(out=q_heads[:, c * HC:(c + 1) * HC, :],
                                                in0=over(PS[:, 5, c * P:(c + 1) * P], 1, HC), scalar=x_bq[:, c:c + 1],
                                                in1=over(hmask[:, :], 2, P), op0=ALU.add, op1=ALU.mult)
                i.then_inc(S["qh"], 1)

            def levels(b, g):
                for lv, (o, n) in enumerate(zip((LOWK, 0, LV[1]), LV)):
                    yield (PS[:, g % 2, 0:2 * KEYS].rearrange("p (h k) -> p h k", h=2)[:, :, o:o + n],
                           sc2[:, 2 * g:2 * g + 2, o:o + n], mx[:, 2 * g:2 * g + 2, lv], n)

            def x_max(b, g):
                dv.wait_ge(S["s2_ps"], made(b, g, 8))
                for s_in, _, m, _ in levels(b, g):
                    i = dv.tensor_reduce(m, s_in, AX, ALU.max)
                i.then_inc(S["maxed2"], 1)

            def x_shift(b, g):
                dv.wait_ge(S["maxed2"], b * 8 + g + 1)
                dv.wait_ge(S["pt2_ps"], made(b - 1, g, 8))
                for s_in, s_out, m, n in levels(b, g):
                    i = dv.tensor_tensor(s_out, s_in, over(m, 2, n), ALU.subtract)
                i.then_inc(S["shifted"], 1)

            def x_norm(b):
                dv.wait_ge(S["o2_ps"], made(b))
                dv.wait_ge(S["ctx"], NSEQ + b)
                outs = [PS[:, 6 + half, 0:8 * 3 * VW].rearrange("p (h l d) -> p h l d", h=8, l=3)
                        for half in range(2)]
                for half in range(2):
                    dv.reciprocal(o2_inv[:, half, :, :].unsqueeze(3), outs[half][:, :, :, HD:VW]).then_inc(S["o2_inv"], 1)
                for half in range(2):
                    dv.wait_ge(S["o2_inv"], b * 2 + half + 1)
                    dv.tensor_tensor(o2_part[:, half], outs[half][:, :, :, 0:HD], over(o2_inv[:, half], 3, HD),
                                     ALU.mult).then_inc(S["o2_part"], 1)
                for half in range(2):
                    dv.wait_ge(S["o2_part"], b * 2 + half + 1)
                    i = dv.tensor_reduce(cx[:, half * P:(half + 1) * P].rearrange("p (h d) -> p h d", h=8),
                                         o2_part[:, half].rearrange("p h l d -> p h d l"), AX, ALU.add)
                i.then_inc(S["ctx"], 1)

            def x_add(b):
                dv.wait_ge(S["out_ps"], made(NSEQ + b))
                dv.wait_ge(S["x_biased"], made(NSEQ + b))
                dv.scalar_tensor_tensor(out=tile(X, b), in0=PS[:, 6, 0:D], scalar=x_sm[:, 0:1], in1=tile(X, b),
                                        op0=ALU.mult, op1=ALU.add).then_inc(S["x_done"], 1)

            def turn_weights():
                dv.wait_ge(S["w_mean"], 1)
                dv.tensor_scalar(f_stat[:, 1:2], PS[:, 6, 0:1], 1.0 / (D * D), 0.7, ALU.mult, ALU.mult)\
                    .then_inc(S["w_step"], 1)
                dv.wait_ge(S["w_step"], 1)
                dv.tensor_scalar(f_stat[:, 2:3], f_stat[:, 1:2], -1.0, None, ALU.mult).then_inc(S["w_step"], 1)
                dv.wait_ge(S["w_step"], 2)
                dv.tensor_scalar(fl, fw, f_stat[:, 2:3], None, ALU.is_lt).then_inc(S["w_step"], 1)
                dv.wait_ge(S["w_step"], 3)
                dv.scalar_tensor_tensor(out=fw, in0=fw, scalar=f_stat[:, 1:2], in1=fl, op0=ALU.is_gt,
                                        op1=ALU.subtract).then_inc(S["w_step"], 1)
                dv.wait_ge(S["w_step"], 4)
                dv.tensor_scalar(fw, fw, f_alpha[:, 0:1], None, ALU.mult).then_inc(S["w_step"], 1)
                for n in range(1, len(turns), 2):
                    dv.wait_ge(S["turn_ps"], n + 1)
                    dv.tensor_copy(turns[n][0], turned(n)).then_inc(S["turned_v"], 1)



            def x_front(b):
                ln(NSEQ + b, b)
                x_ctx(b)
                ln_apply(NSEQ + b, b)
                x_q(b)
                turn_weights()
                x_max(b, 0)
                x_shift(b, 0)
                x_max(b, 1)

            def x_body(b, more):
                for g in range(1, 8):
                    x_shift(b, g)
                    if g == 1 and more:
                        ln_stats(NSEQ + b + 1, b + 1)
                    if g < 7:
                        x_max(b, g + 1)
                    if g == 1 and more:
                        ln_var(NSEQ + b + 1)
                    if g == 2 and more:
                        x_ctx(b + 1)
                        ln_apply(NSEQ + b + 1, b + 1)
                if more:
                    x_q(b + 1)
                x_norm(b)
                if more:
                    x_max(b + 1, 0)
                    x_shift(b + 1, 0)
                    x_max(b + 1, 1)
                x_add(b)

            dv.wait_ge(S["ld_b"], LD_B)
            dv.wait_ge(S["ld_c"], LD_C)
            dv.wait_ge(S["x_done"], made(NSEQ - 1))
            dv.wait_ge(S["ld_w"], LD_W)
            dv.wait_ge(S["consts"], CONSTS)
            fw = t_fw.rearrange("p a b -> p (a b)")
            fl = t_fl.rearrange("p a b -> p (a b)")
            dv.tensor_reduce(f_stat[:, 0:1], fw, AX, ALU.add, apply_absolute_value=True).then_inc(S["w_tot"], 1)
            for c in range(DC):
                dv.tensor_scalar(x_bvb[:, c, :], ones[:, :], x_bv[:, c:c + 1], None, ALU.mult).then_inc(S["x_bv"], 1)
            dv.wait_ge(S["x_sig"], 1)
            dv.tensor_scalar(x_sm[:, :], x_sm[:, :], 1.0, None, ALU.add).then_inc(S["x_sigd"], 1)
            dv.wait_ge(S["x_sigd"], 1)
            dv.reciprocal(x_sm[:, :], x_sm[:, :]).then_inc(S["x_sigd"], 1)
            dv.wait_ge(S["x_bias_ps"], 1)
            dv.tensor_tensor(x_bo[:, :], x_bo[:, :], PS[:, 7, 0:D], ALU.add).then_inc(S["x_sigd"], 1)
            dv.wait_ge(S["x_sigd"], 3)
            dv.tensor_scalar(x_bo[:, :], x_bo[:, :], 2.0, x_sm[:, 0:1], ALU.mult, ALU.mult).then_inc(S["x_bias"], 1)
            piped(dv, x_front, x_body)

            def group_stats(n, g):
                dv.wait_ge(S["gl_rstd"], n + 1)
                for t in range(GT):
                    k = dv.bn_stats(gl_stats[:, t, :], tile(X, g * GT + t))
                k.then_inc(S["gl_stats"], 1)
                dv.wait_ge(S["consts"], CONSTS)
                dv.wait_ge(S["gl_stats"], n + 1)
                for t in range(GT):
                    k = dv.bn_aggr(gl_mv[:, t, :], gl_stats[:, t, :])
                k.then_inc(S["gl_aggr"], 1)
                dv.wait_ge(S["gl_aggr"], n + 1)
                dv.tensor_scalar(gl_var[:, :], gl_mv[:, :, 1], EPS, None, ALU.add).then_inc(S["gl_var"], 1)

            def group_apply(n, g, i):
                dv.wait_ge(S["gl_rstd"], n + 2)
                dv.wait_ge(S["xnT_ps"], made(i - 1))
                for t in range(GT):
                    dv.tensor_scalar(xn4[:, t, :], tile(X, g * GT + t), gl_mv[:, t, 0:1], gl_rstd[:, t:t + 1],
                                     ALU.subtract, ALU.mult).then_inc(S["xn"], 1)

            def logits(g):
                dv.wait_ge(S["r_ps"], made(g))
                dv.tensor_copy(lg[:, :, :], PS[:, 4, 0:GT * (NE + 1)].rearrange("p (t e) -> p t e", t=GT))\
                    .then_inc(S["logits"], 1)

            def compare(g):
                dv.wait_ge(S["logits"], g + 1)
                dv.tensor_reduce(l1[:, :], lg[:, :, 0:NE], AX, ALU.max).then_inc(S["top1"], 1)
                for t in range(GT):
                    li, lj = over(lg[:, t, 0:NE], 2, NE), over(lg[:, t, 0:NE], 1, NE)
                    dv.tensor_tensor(cmp[:, t], lj, li, ALU.is_gt)
                    i = dv.tensor_tensor(cmq[:, t], lj, li, ALU.is_equal)
                i.then_inc(S["gt"], 1)

            def ties(g):
                dv.wait_ge(S["top1"], g + 1)
                dv.wait_ge(S["gt"], g + 1)
                dv.tensor_tensor(lg[:, :, 0:NE], lg[:, :, 0:NE], over(l1[:, :], 2, NE), ALU.subtract)\
                    .then_inc(S["shift_l"], 1)
                for t in range(GT):
                    i = dv.tensor_tensor(cmq[:, t], cmq[:, t], tri16[:, :, :], ALU.mult)
                i.then_inc(S["eqt"], 1)
                dv.wait_ge(S["eqt"], g + 1)
                dv.tensor_tensor(cmp.rearrange("p a b c -> p (a b c)"), cmp.rearrange("p a b c -> p (a b c)"),
                                 cmq.rearrange("p a b c -> p (a b c)"), ALU.add).then_inc(S["beats"], 1)

            def ranks(g):
                dv.wait_ge(S["beats"], g + 1)
                dv.tensor_reduce(rank[:, :, :], cmp, AX, ALU.add).then_inc(S["rank"], 1)

            def weights(g):
                dv.wait_ge(S["rank"], g + 1)
                dv.wait_ge(S["exp_l"], g + 1)
                dv.scalar_tensor_tensor(out=combn[:, :, 0:NE], in0=rank[:, :, :], scalar=2.0, in1=lg[:, :, 0:NE],
                                        op0=ALU.is_lt, op1=ALU.mult).then_inc(S["sel"], 1)
                dv.wait_ge(S["sel"], g + 1)
                dv.tensor_reduce(wsum[:, :], combn[:, :, 0:NE], AX, ALU.add).then_inc(S["selsum"], 1)
                dv.wait_ge(S["selsum"], 2 * g + 1)
                dv.reciprocal(wsum[:, :], wsum[:, :]).then_inc(S["selsum"], 1)
                dv.wait_ge(S["selsum"], 2 * g + 2)
                dv.tensor_tensor(combn[:, :, 0:NE], combn[:, :, 0:NE], over(wsum[:, :], 2, NE), ALU.mult)
                dv.wait_ge(S["expg"], g + 1)
                dv.tensor_scalar(combn[:, :, NE:NE + 1], combn[:, :, NE:NE + 1], 1.0, None, ALU.add).then_inc(S["cgate"], 1)
                dv.wait_ge(S["cgate"], g + 1)
                dv.reciprocal(combn[:, :, NE:NE + 1], combn[:, :, NE:NE + 1]).then_inc(S["comb"], 1)

            def e_hidden(g, e):
                rows = F_OF(e)
                dv.wait_ge(S["sg"], made(g, e, NB))
                dv.wait_ge(S["h_ps"], made(g, e, NB))
                dv.wait_ge(S["d_ps"], made(g, e - 2, NB))
                dv.tensor_tensor(hh[0:rows, e % 2, :], PS[0:rows, 2 + e % 2, :], sg[0:rows, e % 2, :], ALU.mult)\
                    .then_inc(S["hh"], 1)

            def e_acc(g, e):
                r = e % 2
                dv.wait_ge(S["d_ps"], made(g, e, NB))
                if e == 0:
                    dv.wait_ge(S["comb_in"], g + 1)
                if e:
                    dv.wait_ge(S["acc"], made(g, e - 1, NB - 1))
                for t in range(GT):
                    x = tile(X, g * GT + t)
                    w = min(e, NE)
                    i = dv.scalar_tensor_tensor(out=x, in0=PS[:, 4 + 2 * r + t // 2, (t % 2) * D:(t % 2 + 1) * D],
                                                scalar=comb[:, t, w:w + 1], in1=x, op0=ALU.mult, op1=ALU.add)
                    if e == NB - 1:
                        i.then_inc(S["x_done"], 1)
                if e < NB - 1:
                    i.then_inc(S["acc"], 1)

            dv.wait_ge(S["consts"], CONSTS)

            def e_front(g):
                group_stats(g, g)
                group_apply(g, g, 2 * NSEQ + g * GT)
                for step in (logits, compare, ties, ranks, weights):
                    step(g)

            def e_body(g, more):
                e_hidden(g, 0)
                dv.wait_ge(S["comb"], made(g))
                dv.wait_ge(S["x_done"], made(2 * NSEQ + g * GT - 1))
                dv.tensor_copy(comb[:, :, :], combn).then_inc(S["comb_in"], 1)
                for e in range(NB):
                    if e == STEP and more:
                        logits(g + 1)
                    if e + 1 < NB:
                        e_hidden(g, e + 1)
                    e_acc(g, e)
                    if more and e == STEP - 8:
                        group_stats(g + 1, g + 1)
                    if more and e == STEP - 4:
                        group_apply(g + 1, g + 1, 2 * NSEQ + (g + 1) * GT)
                    if more and STEP <= e < STEP + 4:
                        (compare, ties, ranks, weights)[e - STEP](g + 1)

            grouped(dv, e_front, e_body)

            def l_front(g):
                group_stats(NG + g, g)
                group_apply(NG + g, g, 3 * NSEQ + g * GT)

            def l_body(g, more):
                for t in range(GT):
                    dv.wait_ge(S["g_ln"], g * GT + t + 1)
                    dv.scalar_tensor_tensor(out=g_zb[t], in0=g_zb[t], scalar=0.0, in1=g_t1[t], op0=ALU.min,
                                            op1=ALU.subtract).then_inc(S["g_log"], 1)
                for t in range(GT):
                    dv.wait_ge(S["g_log"], g * GT + t + 1)
                    for c in range(DC):
                        k = dv.tensor_tensor_scan(g_t1[t][:, c, :], ones[:, :], g_zb[t][:, c, :], 0.0,
                                                  ALU.mult, ALU.add)
                    k.then_inc(S["g_cum"], 1)
                for t in range(GT):
                    cum = g_t1[t].rearrange("p c (n t) -> p c n t", n=NCB)
                    mid = cum[:, :, :, CB // 2 - 1]
                    dv.wait_ge(S["g_cum"], g * GT + t + 1)
                    dv.tensor_tensor(g_zb[t].rearrange("p c (n t) -> p c n t", n=NCB), cum, over(mid, 3, CB),
                                     ALU.subtract).then_inc(S["g_dq"], 1)
                    for n in range(NCB):
                        w = CB * (n + 1)
                        k = dv.tensor_tensor(k_block(t, n), over(mid[:, :, n], 2, w), g_t1[t][:, :, 0:w], ALU.subtract)
                    k.then_inc(S["g_dk"], 1)
                for t in range(GT):
                    dv.wait_ge(S["g_eq"], g * GT + t + 1)
                    dv.wait_ge(S["g_qk"], g * GT + t + 1)
                    for par in range(2):
                        rows = slice(par * P // 2, (par + 1) * P // 2)
                        k = dv.scalar_tensor_tensor(
                            out=g_qx[t][rows, :, :, par, :],
                            in0=g_qk[t][rows, 0:DC, :].rearrange("p c (n t) -> p c n t", n=NCB),
                            scalar=float(D // H1) ** -0.5,
                            in1=g_zb[t][rows].rearrange("p c (n t) -> p c n t", n=NCB), op0=ALU.mult, op1=ALU.mult)
                    k.then_inc(S["g_qx"], 1)
                    dv.wait_ge(S["g_ek"], g * GT + t + 1)
                    for n in range(NCB):
                        k = dv.tensor_tensor(k_block(t, n), k_block(t, n), g_qk[t][:, DC:2 * DC, 0:CB * (n + 1)],
                                             ALU.mult)
                    k.then_inc(S["g_kx"], 1)
                if more:
                    group_stats(NG + g + 1, g + 1)
                for t in range(GT):
                    dv.wait_ge(S["consts"], CONSTS)
                    dv.wait_ge(S["g_a_ps"], g * GT + t + 1)
                    for n in range(NCB):
                        w, t0 = CB * (n + 1), CB * n
                        heads = PS[0:w, t, :].rearrange("p (c n r t) -> p c n r t", c=DC, n=NCB, r=2)
                        k = dv.copy_predicated(
                            g_at[t][0:w, :, :, t0:t0 + CB].rearrange("p r c t -> p c r t"),
                            over(over(trim[0:w, t0:t0 + CB], 1, 2), 1, DC).bitcast(mybir.dt.int32),
                            heads[:, :, n])
                    k.then_inc(S["g_at"], 1)
                if more:
                    group_apply(NG + g + 1, g + 1, 3 * NSEQ + (g + 1) * GT)
                dv.wait_ge(S["g_ss"], g * GT + GT)
                dv.tensor_scalar(g_ss, g_ss, 1.0 / P, EPS, ALU.mult, ALU.add).then_inc(S["g_ve"], 1)
                dv.wait_ge(S["g_rr"], g + 1)
                for t in range(GT):
                    dv.wait_ge(S["g_g2"], g * GT + t + 1)
                    for h in range(H1):
                        gate = g_gate[t][:, h * P:(h + 1) * P]
                        k = dv.scalar_tensor_tensor(out=gate, in0=PS[:, 4 + t, h * P:(h + 1) * P],
                                                    scalar=g_rr[:, t, h:h + 1], in1=gate, op0=ALU.mult, op1=ALU.mult)
                    k.then_inc(S["g_y"], 1)
                for t in range(GT):
                    x = tile(X, g * GT + t)
                    dv.wait_ge(S["g_out_ps"], g * GT + t + 1)
                    dv.tensor_tensor(x, PS[:, 4 + t, 0:D], x, ALU.add).then_inc(S["x_done"], 1)

            dv.wait_ge(S["atz"], GT + 1)
            dv.wait_ge(S["consts"], CONSTS)
            grouped(dv, l_front, l_body)

            def m_front(g):
                group_stats(2 * NG + g, g)
                for t in range(GT):
                    dv.tensor_copy(cn4[t], tile(C, g * GT + t)).then_inc(S["m_cn"], 1)
                    dv.tensor_scalar(m_hide[t], tile(pad4, g * GT + t).bitcast(U8), -BIG, None, ALU.mult)\
                        .then_inc(S["m_hide"], 1)
                group_apply(2 * NG + g, g, LAST + g * GT)
                dv.wait_ge(S["xn"], made(LAST + g * GT + GT - 1))
                dv.tensor_tensor(tiles(X, g), tiles(X, g), over(m_bo[:, :], 1, GT), ALU.add).then_inc(S["m_biased"], 1)

            def m_body(g, more):
                for t in range(GT):
                    dv.wait_ge(S["m_hide"], g * GT + t + 1)
                    dv.wait_ge(S["m_s_ps"], g * GT + t + 1)
                    dv.tensor_tensor(m_s[t], PS[:, t, 0:P], m_hide[t], ALU.add).then_inc(S["m_masked"], 1)
                for t in range(GT):
                    dv.wait_ge(S["m_masked"], g * GT + t + 1)
                    dv.tensor_scalar(m_s[t], m_s[t], -1.0, None, ALU.mult).then_inc(S["m_neg"], 1)
                for t in range(GT):
                    dv.wait_ge(S["m_neg"], g * GT + t + 1)
                    dv.tensor_reduce(m_low[t], m_s[t], AX, ALU.min).then_inc(S["m_low"], 1)
                for t in range(GT):
                    dv.wait_ge(S["m_exp"], g * GT + t + 1)
                    dv.reciprocal(m_inv[t], m_sum[t]).then_inc(S["m_inv"], 1)
                for t in range(GT):
                    dv.wait_ge(S["m_inv"], g * GT + t + 1)
                    dv.wait_ge(S["m_o_ps"], g * GT + t + 1)
                    dv.tensor_scalar(m_o[t], PS[:, t, D:2 * D], m_inv[t], None, ALU.mult).then_inc(S["m_o"], 1)
                if more:
                    m_front(g + 1)
                dv.wait_ge(S["m_biased"], g + 1)
                for t in range(GT):
                    x = tile(X, g * GT + t)
                    dv.wait_ge(S["m_out_ps"], g * GT + t + 1)
                    dv.tensor_tensor(x, PS[:, 4 + t, D:2 * D], x, ALU.add).then_inc(S["m_done"], 1)
                for t in range(GT):
                    dv.wait_ge(S["consts"], CONSTS)
                    dv.wait_ge(S["m_done"], g * GT + t + 1)
                    k = dv.bn_stats(f_stats[:, t, :], tile(X, g * GT + t))
                k.then_inc(S["f_stats"], 1)
                dv.wait_ge(S["consts"], CONSTS)
                dv.wait_ge(S["f_stats"], g + 1)
                for t in range(GT):
                    k = dv.bn_aggr(f_mv[:, t, :], f_stats[:, t, :])
                k.then_inc(S["f_aggr"], 1)
                dv.wait_ge(S["f_aggr"], g + 1)
                dv.tensor_scalar(f_var[:, :], f_mv[:, :, 1], EPS, None, ALU.add).then_inc(S["f_var"], 1)
                dv.wait_ge(S["f_rstd"], g + 1)
                for t in range(GT):
                    dv.tensor_scalar(f_xn[t], tile(X, g * GT + t), f_mv[:, t, 0:1], f_rstd[:, t:t + 1],
                                     ALU.subtract, ALU.mult).then_inc(S["f_xn"], 1)
                dv.wait_ge(S["f_xn"], g * GT + GT)
                dv.tensor_tensor(tiles(X, g), tiles(X, g), over(f_b[:, :], 1, GT), ALU.add).then_inc(S["f_biased"], 1)
                dv.wait_ge(S["f_biased"], g + 1)
                for t in range(GT):
                    x = tile(X, g * GT + t)
                    dv.wait_ge(S["f_out_ps"], g * GT + t + 1)
                    dv.tensor_tensor(x, PS[:, 4 + t, D:2 * D], x, ALU.add).then_inc(S["x_done"], 1)

            dv.wait_ge(S["x_done"], made(4 * NSEQ - 1))
            grouped(dv, m_front, m_body)


_INS = ["x", "ctx_1024", "mask_S2_ff1", "mask_BxS2_bk0",
        "L0_attn_Wq", "L0_attn_Wk", "L0_attn_Wv", "L0_attn_Wo", "L0_attn_bo", "L0_attn_rel_emb",
        "L0_xattn_Wq", "L0_xattn_bq", "L0_xattn_Wk", "L0_xattn_bk", "L0_xattn_Wv", "L0_xattn_bv", "L0_xattn_Wo",
        "L0_xattn_bo",
        "L0_ffn_gate_w", "L0_ffn_w_gate_up", "L0_ffn_w_down", "L0_ffn_shared_w_gate", "L0_ffn_shared_w_up",
        "L0_ffn_shared_w_down", "L0_ffn_shared_gate_w",
        "L1_attn_Wq", "L1_attn_Wk", "L1_attn_Wv", "L1_attn_Wg", "L1_attn_Wgk1", "L1_attn_Wgk2", "L1_attn_bgk2",
        "L1_attn_Wout", "L1_attn_rms_w",
        "L1_xattn_Wq", "L1_xattn_bq", "L1_xattn_Wk", "L1_xattn_bk", "L1_xattn_Wo", "L1_xattn_bo",
        "L1_ffn_weight", "L1_ffn_alpha", "L1_ffn_bias"]


def kernel(**inputs):
    import numpy as _np
    import concourse.bacc as _bacc
    from concourse import mybir as _mybir
    from concourse.bass_utils import run_bass_kernel_spmd as _run

    nc = _bacc.Bacc("TRN2", target_bir_lowering=False, num_devices=1)
    arrays, aps = {}, {}
    for name in _INS:
        a = _np.ascontiguousarray(inputs[name])
        if a.dtype == _np.bool_:
            a = a.view(_np.int32)
        arrays[f"in_{name}"] = a
        aps[name] = nc.dram_tensor(f"in_{name}", a.shape, _mybir.dt.from_np(a.dtype), kind="ExternalInput").ap()
    out = nc.dram_tensor("out_0", (NSEQ, P, D), _mybir.dt.from_np(_np.dtype("float32")), kind="ExternalOutput").ap()
    build(nc, aps, out)
    r = _run(nc, [arrays], core_ids=[0])
    return r.results[0]["out_0"]
```

```python
from contextlib import ExitStack

import concourse.bass as bass
from concourse import mybir

F32 = mybir.dt.float32
U8 = mybir.dt.uint8
ALU = mybir.AluOpType
ACT = mybir.ActivationFunctionType
AX = mybir.AxisListType.X

P = 128
NSEQ = 16
D = 256
DC = D // P
H0 = 16
HD = D // H0
HC = P // HD
CLIP = 16
BIG = 1e30
EPS = 1e-5
LV = (P, P // 2, P // 4)
KEYS = sum(LV)
LOWK = KEYS - P
VW = HD + 1
NE = 16
FE = 128
FS = 704
NB = NE + -(-FS // FE)
GT = 4
STEP = 14
NG = NSEQ // GT
H1 = 4
DV = 512
CB = 32
NCB = P // CB
GATE_NORM = 32.0
LR = 32

SEMS = """
ld_x ld_x_rest ld_rel ld_a ld_c
consts dist rel_term rel_sum
ln_stats ln_aggr ln_var rstd xn xnT_ps xnT x_biased x_done
q_ps kv_ps kT q_heads v s_ps scaled maxed expd pt_ps pt o_ps o_inv ctx ctxT_ps ctxT out_ps
ld_b ld_e ld_w ld_m stored
x_cn x_bv x_bias_ps x_sig x_sigd x_bias
cT mean_sum means k_ps kx qh v2_ps v2 s2_ps maxed2 shifted expd2 pt2_ps pt2 o2_ps o2_inv o2_part
turn_ps turned_a turned_v w_tot w_mean w_step
gl_stats gl_aggr gl_var gl_rstd
r_ps logits top1 gt eqt beats rank shift_l exp_l sel selsum cgate expg comb xT_in comb_in
g_ps h_ps sg hh d_ps acc
g_qk_ps g_qk g_gk_ps g_gk g_z_ps g_z g_v_ps g_v g_g_ps g_gate g_abs g_exp g_ln g_log g_cum g_dq g_dk g_eq g_ek
g_qx g_kx g_a_ps g_at g_o_ps g_ss g_ve g_rr g_wo g_y g_yT_ps g_yT g_out_ps atz
m_cn m_hide m_cT m_qk_ps m_qk m_s_ps m_masked m_neg m_low m_exp m_pT_ps m_pT m_o_ps m_inv m_o m_oT_ps m_oT m_out_ps
m_biased m_done f_stats f_aggr f_var f_rstd f_xn f_xnT_ps f_xnT f_biased f_out_ps
""".split()
CREDITED = {"rstd": 1, "xn": 1, "xnT_ps": 1, "xnT": 1, "x_biased": 1, "x_done": 1, "q_ps": 1, "kv_ps": 1, "kT": 1,
            "q_heads": 1, "v": 1, "s_ps": 4, "expd": 4, "pt_ps": 4, "pt": 4, "o_ps": 1, "out_ps": 1,
            "cT": 1, "means": 2, "x_cn": 1, "k_ps": 1, "kx": 1, "qh": 1, "v2_ps": 1, "v2": 1, "s2_ps": 8, "shifted": 8,
            "expd2": 8, "pt2_ps": 8, "pt2": 8, "o2_ps": 1,
            "r_ps": 1, "comb": 1, "g_ps": NB, "h_ps": NB, "sg": NB, "hh": NB, "d_ps": NB, "acc": NB - 1,
            "gl_rstd": 1}

def made(tile, part=0, parts=1):
    return (tile + 1) * parts + part + 1

def over(ap, at, n):
    ap = ap.unsqueeze(at)
    shape = list(ap.shape)
    shape[at] = n
    return ap.broadcast_to(shape)

def build(nc, A, out):
    with ExitStack() as ctx:
        def sb(name, shape, dt=F32):
            return ctx.enter_context(nc.sbuf_tensor(name, shape, dt))

        S = {n: ctx.enter_context(nc.semaphore(n)) for n in SEMS}
        PS = ctx.enter_context(nc.psum_tensor("PS", [P, 8, 512], F32))

        X = sb("X", [P, NSEQ, D])
        C = sb("C", [P, NSEQ, D])
        ident = sb("ident_sb", [P, P])
        hmask = sb("hmask_sb", [P, HC])
        mhalf = sb("mhalf_sb", [P, 1])
        half = sb("half", [P, 1])
        stats = sb("stats", [P, 6])
        mv = sb("mv", [P, 2])
        var = sb("var", [P, 1])
        rstd = sb("rstd_sb", [P, 1])
        xn = sb("xn_sb", [P, D])
        xnT = sb("xnT_sb", [P, DC, P])
        first = sb("first", [P, 4 * DC * D])
        a_bo = sb("a_bo", [P, D])
        rel = sb("rel", [P, CLIP + 1])
        dist = sb("dist_sb", [P, P])
        relT = sb("relT", [P, P])
        csum = dist[:, :].rearrange("p (c t) -> p c t", c=DC)
        nA = sb("nA", [P, P])
        hide = sb("hide", [P, P])
        kT = sb("kT_sb", [P, DC, P])
        q_heads = sb("q_heads_sb", [P, H0, P])
        va = sb("va", [P, H0, HD + 1])
        low = sb("low", [P, H0])
        o_inv = sb("o_inv_sb", [P, H0])
        cx = sb("cx", [P, D])
        cxT = sb("cxT", [P, DC, P])

        x_wq, x_wk, x_wv, x_wo = (sb(f"x_{n}", [P, DC, D]) for n in ("wq", "wk", "wv", "wo"))
        x_bq, x_bk, x_bv = (sb(f"x_{n}", [P, DC]) for n in ("bq", "bk", "bv"))
        x_bo = sb("x_bo", [P, D])
        x_sm = sb("x_sm", [P, 1])
        x_bvb = sb("x_bvb", [P, DC, P])
        cT = sb("cT_sb", [P, DC, KEYS])
        kx = sb("kx_sb", [P, DC, KEYS])
        vx = sb("vx", [P, H0, VW])
        vlow = sb("vlow", [P, H0, 2 * VW])
        mx = sb("mx", [P, H0, 3])
        o2_inv = sb("o2_inv_sb", [P, 2, 8, 3])
        o2_part = sb("o2_part_sb", [P, 2, 8, 3, HD])
        s_g = sb("s_g", [P, DC, FS])
        s_u = sb("s_u", [P, DC, FS])
        s_dn = sb("s_dn", [P, NB - NE, D])
        gwT = sb("gwT", [P, DC, NE + 1])
        lg = sb("lg", [P, GT, NE + 1])
        l1 = sb("l1", [P, GT])
        tri16 = sb("tri16", [P, NE, NE])
        rank = sb("rank_sb", [P, GT, NE])
        wsum = sb("wsum", [P, GT])
        comb = sb("comb_sb", [P, GT, NE + 1])
        l_wq, l_wk = (sb(f"l_{n}", [P, DC, D]) for n in ("wq", "wk"))
        l_wv, l_wg = (sb(f"l_{n}", [P, DC, DV]) for n in ("wv", "wg"))
        l_gk1 = sb("l_gk1", [P, DC, LR])
        l_gk2 = sb("l_gk2", [LR, D])
        l_bgk = sb("l_bgk", [P, DC])
        l_wo = sb("l_wo", [P, DV // P, D])
        l_rms = sb("l_rms", [P, 1])
        trim = sb("trim_sb", [P, P])
        ones = sb("ones", [P, P])
        m_wq, m_wk, m_wo, f_w = (sb(f"m_{n}", [P, DC, D]) for n in ("wq", "wk", "wo", "wf"))
        m_bq, m_bk = (sb(f"m_{n}", [P, DC]) for n in ("bq", "bk"))
        m_bo, f_b = (sb(f"m_{n}", [P, D]) for n in ("bo", "bf"))
        f_alpha = sb("f_alpha", [P, 1])
        f_stat = sb("f_stat", [P, 4])
        pad4 = sb("pad4", [P, NSEQ, P // 4], mybir.dt.int32)

        cn = sb("cn", [P, D])
        work = sb("work", [P, 7760])
        wide = sb("wide", [P, NE * (DC * 2 * FE + D)])

        def part(region, base, *shape):
            n = 1
            for x in shape:
                n *= x
            view = region[:, base:base + n]
            if len(shape) == 1:
                return view
            letters = "abcd"[:len(shape)]
            return view.rearrange(f"p ({' '.join(letters)}) -> p {' '.join(letters)}", **dict(zip(letters, shape)))

        a_wq, a_wk, a_wv, a_wo = (part(first, n * DC * D, DC, D) for n in range(4))
        sc = part(work, 0, H0, P)
        ex = part(work, 2048, H0, P)
        pT = part(work, 4096, H0, P)
        sc2 = part(work, 0, H0, KEYS)
        pT2 = part(work, 3584, 8, 512)
        sg = part(work, 0, 2, 512)
        hh = part(work, 1024, 2, 512)
        xT3 = part(work, 2048, DC, GT * P)
        cmp = part(work, 3072, GT, NE, NE)
        cmq = part(work, 4096, GT, NE, NE)
        xTn = part(first, GT * D, DC, GT * P)
        combn = part(work, 7168, GT, NE + 1)
        gl_stats, gl_mv = sb("gl_stats_sb", [P, GT, 6]), sb("gl_mv", [P, GT, 2])
        gl_var, gl_rstd = sb("gl_var_sb", [P, GT]), sb("gl_rstd_sb", [P, GT])
        f_stats, f_mv = sb("f_stats_sb", [P, GT, 6]), sb("f_mv", [P, GT, 2])
        f_var, f_rstd = sb("f_var_sb", [P, GT]), sb("f_rstd_sb", [P, GT])
        xn4 = part(first, 0, GT, D)
        xnT4 = part(work, 6656, GT, DC, P)
        def slots(base, *shape):
            return [part(wide, t * 3072 + base, *shape) for t in range(GT)]

        g_qk = slots(0, 2 * DC, P)
        g_zb = slots(512, DC, P)
        g_t1 = slots(768, DC, P)
        g_v = slots(1024, DV)
        g_gate = slots(1536, DV)
        g_at = slots(2048, 2, 2, P)
        g_yT = slots(2560, DV // P, P)
        g_sq = slots(2560, H1, P)
        KX = CB * NCB * (NCB + 1)
        g_qx = [part(work, t * 2 * D, DC, NCB, 2, CB) for t in range(GT)]
        g_kx = [part(work, GT * 2 * D + t * KX, KX) for t in range(GT)]
        g_gk = [part(work, 6144 + t * P, P) for t in range(GT)]
        g_ss = part(work, 7680, GT, H1)
        g_rr = part(work, 7680 + GT * H1, GT, H1)
        m_qk = slots(0, 2 * DC, P)
        m_s = slots(512, P)
        m_e = slots(640, P)
        m_pT = slots(768, P)
        m_o = slots(896, D)
        m_oT = slots(1152, DC, P)
        m_cT = slots(1408, DC, P)
        m_hide = slots(1664, P)
        cn4 = slots(1792, D)
        f_xn = slots(2048, D)
        f_xnT = slots(2304, DC, P)
        m_low = slots(2560, 1)
        m_sum = slots(2561, 1)
        m_inv = slots(2562, 1)

        e_gu = part(wide, 0, NE, DC, 2 * FE)
        e_dn = part(wide, NE * DC * 2 * FE, NE, D)
        SR = -(-FS // P)
        t_sg = part(wide, 0, SR, D)
        t_su = part(wide, 1536, SR, D)
        t_sd = part(wide, 3072, DC, FS)
        t_gw = part(wide, 4480, D)[0:NE + 1]
        t_lq = part(wide, 4736, DC, D)
        t_lk = part(wide, 5248, DC, D)
        t_lv = part(wide, 5760, DV // P, D)
        t_lg = part(wide, 6784, DV // P, D)
        t_g1 = part(wide, 7808, D)[0:LR]
        t_g2 = part(wide, 8064, DC, LR)
        t_lo = part(wide, 8128, DC, DV)
        t_mq = part(wide, 9152, DC, D)
        t_mk = part(wide, 9664, DC, D)
        t_mo = part(wide, 10176, DC, D)
        t_fw = part(wide, 10688, DC, D)
        t_fl = part(wide, 11200, DC, D)

        turns = []

        def turn(dst, blocks):
            turns.append((dst, blocks))

        def blocks_of(src, rows, c, width=P):
            return [(src[:, r, c * P:(c + 1) * P], n * width) for n, r in enumerate(rows)]

        for src, dst in ((t_sg, s_g), (t_su, s_u)):
            for c in range(DC):
                turn(dst[:, c, 0:4 * P], blocks_of(src, range(4), c))
                turn(dst[:, c, 4 * P:FS], [(src[:, 4, c * P:(c + 1) * P], 0),
                                           (src[0:FS - 5 * P, 5, c * P:(c + 1) * P], P)])
        for k in (0, 2):
            turn(s_dn[:, k:k + 2, :], [(t_sd[:, r, (k + j) * P:(k + j + 1) * P], j * D + r * P)
                                       for j in range(2) for r in range(DC)])
        turn(s_dn[:, 4, :], [(t_sd[:, r, 4 * P:5 * P], r * P) for r in range(DC)])
        turn(s_dn[0:FS - 5 * P, 5, :], [(t_sd[:, r, 5 * P:FS], r * P) for r in range(DC)])
        turn(gwT[:, :, :], [(t_gw[:, c * P:(c + 1) * P], c * (NE + 1)) for c in range(DC)])
        for src, dst in ((t_lq, l_wq), (t_lk, l_wk), (t_mq, m_wq), (t_mk, m_wk), (t_mo, m_wo)):
            turn(dst[:, :, :], [(src[:, r, c * P:(c + 1) * P], c * D + r * P) for c in range(DC) for r in range(DC)])
        for src, dst in ((t_lv, l_wv), (t_lg, l_wg)):
            for c in range(DC):
                turn(dst[:, c, :], blocks_of(src, range(4), c))
        turn(l_gk1[:, :, :], [(t_g1[:, c * P:(c + 1) * P], c * LR) for c in range(DC)])
        turn(l_gk2[:, :], [(t_g2[:, r, :], r * P) for r in range(DC)])
        for k in (0, 2):
            turn(l_wo[:, k:k + 2, :], [(t_lo[:, r, (k + j) * P:(k + j + 1) * P], j * D + r * P)
                                       for j in range(2) for r in range(DC)])
        turn(f_w[:, :, :], [(t_fw[:, r, c * P:(c + 1) * P], c * D + r * P) for c in range(DC) for r in range(DC)])

        def turned(n):
            dst, _ = turns[n]
            ps = PS[0:dst.shape[0], n % 4, 0:dst.free_size()]
            return ps if len(dst.shape) == 2 else ps.rearrange("p (a b) -> p a b", a=dst.shape[1])

        def tile(T, b):
            return T[:, bass.ds(b, 1), :].rearrange("p a d -> p (a d)")

        CONSTS = 19
        LD_A, LD_W, LD_C, LD_B, LD_M, LD_E = (16 * n for n in (5, 19, 1, 9, 7, 8))
        LAST = 4 * NSEQ
        block = ctx.enter_context(nc.Block())

        def piped(eng, front, body):
            front(0)
            with eng.Fori(0, NSEQ - 1) as b:
                body(b, True)
            body(NSEQ - 1, False)

        def piped_by_two(eng, front, body):
            front(0)
            with eng.Fori(0, NSEQ - 2) as b:
                body(b, 2)
            body(NSEQ - 2, 1)
            body(NSEQ - 1, 0)

        def k_block(t, n):
            w = CB * (n + 1)
            base = GT * 2 * D + t * KX + DC * CB * (n * (n + 1) // 2)
            return part(work, base, DC, w)

        def tiles(T, g):
            return T[:, bass.ds(g * GT, GT), :]

        def grouped(eng, front, body):
            if front:
                front(0)
            with eng.Fori(0, NG - 1) as g:
                body(g, True)
            body(NG - 1, False)

        def grouped_by_two(eng, body):
            with eng.Fori(0, NG - 2) as g:
                body(g, 2)
            body(NG - 2, 1)
            body(NG - 1, 0)

        def F_OF(e):
            return min(FE, FS - (e - NE) * FE) if e >= NE else FE

        def w_in(ap):
            return ap.rearrange("(c p) n -> p c n", p=P)

        @block.sync
        def _(sp):
            xv = A["x"].rearrange("b t d -> t b d")

            def load(dst, src, done, slow=False):
                sp.dma_start(dst, src, allow_slow_non_contiguous=slow).then_inc(done, 16)

            def all_rows(name):
                return A[name].partition_broadcast(P)

            def column(name):
                return A[name].rearrange("(c p) -> p c", p=P)

            load(rel[:, :], all_rows("L0_attn_rel_emb"), S["ld_rel"])
            load(X[:, 0:4, :], xv[:, 0:4, :], S["ld_x"])
            for t, n in ((a_wq, "L0_attn_Wq"), (a_wk, "L0_attn_Wk"), (a_wv, "L0_attn_Wv"), (a_wo, "L0_attn_Wo")):
                load(t[:, :, :], w_in(A[n]), S["ld_a"])
            load(a_bo[:, :], all_rows("L0_attn_bo"), S["ld_a"])
            load(X[:, 4:NSEQ, :], xv[:, 4:NSEQ, :], S["ld_x_rest"])
            for t, n in ((t_sg, "L0_ffn_shared_w_gate"), (t_su, "L0_ffn_shared_w_up")):
                load(t[:, 0:5, :], A[n][0:5 * P, :].rearrange("(r p) d -> p r d", p=P), S["ld_w"])
                load(t[0:FS - 5 * P, 5, :], A[n][5 * P:FS, :], S["ld_w"])
            load(t_gw[0:NE, :], A["L0_ffn_gate_w"], S["ld_w"])
            load(t_gw[NE:NE + 1, :], A["L0_ffn_shared_gate_w"], S["ld_w"])
            load(t_g1[:, :], A["L1_attn_Wgk1"], S["ld_w"])
            for t, n in ((t_sd, "L0_ffn_shared_w_down"), (t_lq, "L1_attn_Wq"), (t_lk, "L1_attn_Wk"),
                         (t_lv, "L1_attn_Wv"), (t_lg, "L1_attn_Wg"), (t_g2, "L1_attn_Wgk2"),
                         (t_lo, "L1_attn_Wout"), (t_mq, "L1_xattn_Wq"), (t_mk, "L1_xattn_Wk"),
                         (t_mo, "L1_xattn_Wo"), (t_fw, "L1_ffn_weight")):
                load(t[:, :, :], A[n].rearrange("(r p) d -> p r d", p=P), S["ld_w"])
            load(f_alpha[:, :], all_rows("L1_ffn_alpha"), S["ld_w"])
            load(C[:, :, :], A["ctx_1024"].rearrange("b t d -> t b d"), S["ld_c"])
            for t, n in ((x_wq, "Wq"), (x_wk, "Wk"), (x_wv, "Wv"), (x_wo, "Wo")):
                load(t[:, :, :], w_in(A["L0_xattn_" + n]), S["ld_b"])
            for t, n in ((x_bq, "bq"), (x_bk, "bk"), (x_bv, "bv")):
                load(t[:, :], column("L0_xattn_" + n), S["ld_b"], slow=True)
            load(x_bo[:, :], all_rows("L0_xattn_bo"), S["ld_b"])
            load(x_sm[:, :], A["mask_S2_ff1"].rearrange("(p a) -> p a", a=1), S["ld_b"], slow=True)
            load(l_bgk[:, :], column("L1_attn_bgk2"), S["ld_m"], slow=True)
            load(l_rms[:, :], A["L1_attn_rms_w"].rearrange("(p a) -> p a", a=1), S["ld_m"], slow=True)
            for t, n in ((m_bq, "L1_xattn_bq"), (m_bk, "L1_xattn_bk")):
                load(t[:, :], column(n), S["ld_m"], slow=True)
            load(m_bo[:, :], all_rows("L1_xattn_bo"), S["ld_m"])
            load(f_b[:, :], all_rows("L1_ffn_bias"), S["ld_m"])
            load(pad4.rearrange("p b t -> p (b t)"), A["mask_BxS2_bk0"].rearrange("b t -> (b t)").partition_broadcast(P), S["ld_m"])
            sp.wait_ge(S["turn_ps"], len(turns))
            for e in range(0, NE, 4):
                load(e_gu[:, e:e + 4, :, :].rearrange("p e c n -> p (e c) n"),
                     A["L0_ffn_w_gate_up"][e:e + 4].rearrange("e (c p) n -> p (e c) n", p=P), S["ld_e"])
                load(e_dn[:, e:e + 4, :], A["L0_ffn_w_down"][e:e + 4].rearrange("e f n -> f e n"), S["ld_e"])
            for done, n in ((S["ld_c"], LD_C), (S["ld_b"], LD_B), (S["ld_m"], LD_M), (S["ld_w"], LD_W), (S["ld_e"], LD_E)):
                sp.wait_ge(done, n)
            with sp.Fori(0, NSEQ) as b:
                sp.wait_ge(S["x_done"], made(LAST + b))
                load(out[bass.ds(b, 1)].rearrange("b t d -> t (b d)"), tile(X, b), S["stored"])
            sp.wait_ge(S["stored"], 16 * NSEQ)

        @block.gpsimd
        def _(gp):
            for name, n in CREDITED.items():
                gp.sem_inc(S[name], n)
            for buf, value in ((mhalf[:, :], -0.5), (half[:, :], 0.5), (ident[:, :], 0.0), (hmask[:, :], 1.0),
                               (hide[:, :], 0.0), (va[:, :, HD:VW], 1.0), (tri16[:, :, :], 1.0), (trim[:, :], 1.0),
                               (ones[:, :], 1.0), (vlow[:, :, :], 0.0),
                               (vx[:, :, HD:VW], 0.75)):
                gp.memset(buf, value).then_inc(S["consts"], 1)
            gp.wait_ge(S["consts"], 11)
            gp.memset(vlow[0:LV[1], :, HD:VW], 3.0).then_inc(S["consts"], 1)
            gp.wait_ge(S["consts"], 12)
            gp.memset(vlow[LV[1]:LOWK, :, VW + HD:2 * VW], 3.0).then_inc(S["consts"], 1)
            gp.wait_ge(S["consts"], 13)
            gp.affine_select(out=tri16[:, :, :], in_=tri16[:, :, :], compare_op=ALU.is_gt, fill=0.0, base=0,
                             pattern=[[1, NE], [-1, NE]], channel_multiplier=0).then_inc(S["consts"], 1)
            gp.affine_select(out=trim[:, :], in_=trim[:, :], compare_op=ALU.is_ge, fill=0.0, base=0,
                             pattern=[[1, P]], channel_multiplier=-1).then_inc(S["consts"], 1)
            gp.affine_select(out=ident[:, :], in_=ident[:, :], compare_op=ALU.not_equal, fill=1.0,
                             base=0, pattern=[[-1, P]], channel_multiplier=1).then_inc(S["consts"], 1)
            gp.affine_select(out=hide[:, :], in_=hide[:, :], compare_op=ALU.is_ge, fill=BIG,
                             base=0, pattern=[[-1, P]], channel_multiplier=1).then_inc(S["consts"], 1)
            gp.affine_select(out=hmask[:, :], in_=hmask[:, :], compare_op=ALU.is_ge, fill=0.0,
                             base=0, pattern=[[-HD, HC]], channel_multiplier=1).then_inc(S["consts"], 1)
            gp.wait_ge(S["consts"], 18)
            gp.affine_select(out=hmask[:, :], in_=hmask[:, :], compare_op=ALU.is_ge, fill=0.0,
                             base=HD - 1, pattern=[[HD, HC]], channel_multiplier=-1).then_inc(S["consts"], 1)
            gp.iota(dist[:, :], pattern=[[-1, P]], base=0, channel_multiplier=1,
                    allow_small_or_imprecise_dtypes=True).then_inc(S["dist"], 1)

            def ln(i):
                gp.wait_ge(S["ln_var"], i + 1)
                gp.wait_ge(S["xn"], made(i - 1))
                gp.tensor_tensor(rstd[:, :], var[:, :], mhalf[:, :], ALU.pow).then_inc(S["rstd"], 1)

            def bias_x(i, b, bias):
                gp.wait_ge(S["xn"], made(i))
                gp.tensor_tensor(tile(X, b), tile(X, b), bias[:, :], ALU.add).then_inc(S["x_biased"], 1)

            gp.wait_ge(S["consts"], CONSTS)
            gp.wait_ge(S["ld_a"], LD_A)

            def front(b):
                ln(b)
                bias_x(b, b, a_bo)

            piped(gp, front, lambda b, more: front(b + 1) if more else None)

            def x_front(b, first=False):
                i = NSEQ + b
                if not first:
                    ln(i)
                    bias_x(i, b, x_bo)
                for lv, (src, dst, n) in enumerate(((LOWK, 0, P), (0, LV[1], LV[1]))):
                    if lv == 0:
                        gp.wait_ge(S["cT"], made(b))
                    else:
                        gp.wait_ge(S["means"], made(b, 0, 2))
                    pair = cT[:, :, src:src + n].rearrange("p c (t a) -> p c t a", a=2)
                    gp.tensor_tensor(csum[:, :, 0:n // 2], pair[:, :, :, 0], pair[:, :, :, 1], ALU.add)\
                        .then_inc(S["mean_sum"], 1)
                    gp.wait_ge(S["mean_sum"], 2 * b + lv + 1)
                    gp.tensor_tensor(cT[:, :, dst:dst + n // 2], csum[:, :, 0:n // 2],
                                     half[:, 0:1].unsqueeze(2).broadcast_to([P, DC, n // 2]), ALU.mult)\
                        .then_inc(S["means"], 1)

            ln(NSEQ)
            gp.wait_ge(S["x_done"], made(NSEQ - 1))
            x_front(0, first=True)
            gp.wait_ge(S["x_bias"], 1)
            bias_x(NSEQ, 0, x_bo)
            with gp.Fori(0, NSEQ - 1) as b:
                x_front(b + 1)

            def group_ln(n, i):
                gp.wait_ge(S["gl_var"], n + 1)
                gp.wait_ge(S["xn"], made(i - 1))
                gp.tensor_tensor(gl_rstd[:, :], gl_var[:, :], mhalf[:, 0:1].broadcast_to([P, GT]), ALU.pow)\
                    .then_inc(S["gl_rstd"], 1)

            with gp.Fori(0, NG) as g:
                group_ln(g, 2 * NSEQ + g * GT)

            def l_front(g):
                group_ln(NG + g, 3 * NSEQ + g * GT)

            def l_body(g, more):
                if more:
                    l_front(g + 1)
                else:
                    group_ln(2 * NG, LAST)
                for t in range(GT):
                    mid = g_t1[t].rearrange("p c (n t) -> p c n t", n=NCB)[:, :, :, CB // 2 - 1]
                    gp.wait_ge(S["g_cum"], g * GT + t + 1)
                    for n in range(NCB):
                        w = CB * (n + 1)
                        k = gp.tensor_tensor(k_block(t, n), over(mid[:, :, n], 2, w), g_t1[t][:, :, 0:w],
                                             ALU.subtract)
                    k.then_inc(S["g_dk"], 1)
                for t in range(GT):
                    gp.wait_ge(S["g_ve"], g * GT + t + 1)
                    gp.tensor_tensor(g_rr[:, t], g_ss[:, t], mhalf[:, 0:1].broadcast_to([P, H1]), ALU.pow)\
                        .then_inc(S["g_rr"], 1)

            l_front(0)
            gp.wait_ge(S["x_done"], made(3 * NSEQ - 1))
            for t in range(GT):
                gp.memset(part(wide, t * 3072 + 2048, 2 * 2 * P), 0.0).then_inc(S["atz"], 1)
            gp.memset(part(work, 0, GT * 2 * D), 0.0).then_inc(S["atz"], 1)
            grouped(gp, None, l_body)

            def m_front(g):
                group_ln(2 * NG + g, LAST + g * GT)

            def m_body(g, more):
                gp.wait_ge(S["f_var"], g + 1)
                gp.tensor_tensor(f_rstd[:, :], f_var[:, :], mhalf[:, 0:1].broadcast_to([P, GT]), ALU.pow)\
                    .then_inc(S["f_rstd"], 1)
                if more > 1:
                    m_front(g + 2)

            m_front(1)
            grouped_by_two(gp, m_body)

        @block.scalar
        def _(act):
            def ln_xnT(i):
                act.wait_ge(S["xnT_ps"], made(i))
                act.activation(xnT[:, :, :], PS[:, 4, 0:D].rearrange("p (c t) -> p c t", c=DC),
                               ACT.Copy).then_inc(S["xnT"], 1)

            def front_k(b):
                act.wait_ge(S["kv_ps"], made(b))
                act.activation(kT[:, :, :], PS[:, 6, 0:D].rearrange("p (c t) -> p c t", c=DC),
                               ACT.Copy).then_inc(S["kT"], 1)

            def front_v(b):
                act.wait_ge(S["o_ps"], made(b - 1))
                act.activation(va[:, :, 0:HD], PS[:, 6, D:2 * D].rearrange("p (h d) -> p h d", h=H0),
                               ACT.Copy).then_inc(S["v"], 1)

            def exps(b, g):
                act.wait_ge(S["maxed"], b * 4 + g + 1)
                act.wait_ge(S["pt_ps"], made(b - 1, g, 4))
                for h in range(4 * g, 4 * g + 4):
                    i = act.activation(ex[:, h, :], sc[:, h, :], ACT.Exp, bias=low[:, h:h + 1], scale=-1.0)
                i.then_inc(S["expd"], 1)

            def pts(b, g):
                act.wait_ge(S["pt_ps"], made(b, g, 4))
                act.wait_ge(S["o_ps"], made(b - 1))
                act.activation(pT[:, 4 * g:4 * g + 4, :], PS[:, g, :].rearrange("p (h t) -> p h t", h=4),
                               ACT.Copy).then_inc(S["pt"], 1)

            def ctxT(b):
                act.wait_ge(S["ctxT_ps"], b + 1)
                act.activation(cxT[:, :, :], PS[:, 7, 0:D].rearrange("p (c t) -> p c t", c=DC),
                               ACT.Copy).then_inc(S["ctxT"], 1)

            def front(b):
                ln_xnT(b)
                front_k(b)
                front_v(b)
                ln_xnT(b + 1)
                exps(b, 0)
                exps(b, 1)

            def body(b, more):
                pts(b, 0)
                exps(b, 2)
                pts(b, 1)
                exps(b, 3)
                pts(b, 2)
                pts(b, 3)
                if more:
                    front_k(b + 1)
                    front_v(b + 1)
                ctxT(b)
                if more > 1:
                    ln_xnT(b + 2)
                if more:
                    exps(b + 1, 0)
                    exps(b + 1, 1)

            act.wait_ge(S["consts"], CONSTS)
            piped_by_two(act, front, body)

            def two(ap):
                return ap.rearrange("p (c t) -> p c t", c=DC)

            def x_T(b):
                act.wait_ge(S["xnT_ps"], made(NSEQ + b))
                act.activation(xnT[:, :, :], two(PS[:, 4, 0:D]), ACT.Copy).then_inc(S["xnT"], 1)
                act.activation(cT[:, :, LOWK:KEYS], two(PS[:, 4, D:2 * D]), ACT.Copy).then_inc(S["cT"], 1)

            def x_k(b):
                act.wait_ge(S["k_ps"], made(b))
                for c in range(DC):
                    i = act.activation(kx[:, c, :], PS[:, 4, c * KEYS:(c + 1) * KEYS], ACT.Identity,
                                       bias=x_bk[:, c:c + 1], scale=1.0)
                i.then_inc(S["kx"], 1)

            def x_v(b):
                act.wait_ge(S["v2_ps"], made(b))
                act.wait_ge(S["o2_ps"], made(b - 1))
                heads = PS[:, 4, :].rearrange("p (a h d) -> p a h d", a=2, h=H0)
                act.activation(vx[:, :, 0:HD], heads[:, 0], ACT.Copy)
                act.activation(vlow[0:LV[1], :, 0:HD], heads[0:LV[1], 1], ACT.Copy)
                act.activation(vlow[LV[1]:LOWK, :, VW:VW + HD], heads[LV[1]:LOWK, 1], ACT.Copy).then_inc(S["v2"], 1)

            def x_exp(b, g):
                act.wait_ge(S["shifted"], made(b, g, 8))
                act.activation(sc2[:, 2 * g:2 * g + 2, :], sc2[:, 2 * g:2 * g + 2, :], ACT.Exp,
                               scale=float(HD) ** -0.5).then_inc(S["expd2"], 1)

            def x_pT(b, g):
                act.wait_ge(S["pt2_ps"], made(b, g, 8))
                act.wait_ge(S["o2_ps"], made(b - 1))
                act.activation(pT2[:, g, :], PS[:, 2 + g % 2, :], ACT.Copy).then_inc(S["pt2"], 1)

            def x_ctxT(b):
                act.wait_ge(S["ctxT_ps"], NSEQ + b + 1)
                act.activation(cxT[:, :, :], two(PS[:, 7, 0:D]), ACT.Copy).then_inc(S["ctxT"], 1)

            def turn_weights():
                for n in range(0, len(turns), 2):
                    act.wait_ge(S["turn_ps"], n + 1)
                    act.activation(turns[n][0], turned(n), ACT.Copy).then_inc(S["turned_a"], 1)

            def x_front(b):
                x_T(b)
                x_k(b)
                x_v(b)
                turn_weights()
                x_exp(b, 0)

            def x_body(b, more):
                for g in range(8):
                    if g:
                        x_exp(b, g)
                        x_pT(b, g - 1)
                    if g == 4 and more:
                        x_T(b + 1)
                    if g == 5 and not more:
                        e_xT(0)
                x_pT(b, 7)
                if more:
                    x_k(b + 1)
                else:
                    e_take(0)
                x_ctxT(b)
                if more:
                    x_exp(b + 1, 0)
                    x_v(b + 1)
                else:
                    e_silu(0, 0)

            act.wait_ge(S["ld_b"], LD_B)
            act.activation(x_sm[:, :], x_sm[:, :], ACT.Exp, scale=-1.0).then_inc(S["x_sig"], 1)
            act.wait_ge(S["consts"], CONSTS)
            act.wait_ge(S["x_done"], made(NSEQ - 1))
            def e_silu(g, e):
                rows = F_OF(e)
                act.wait_ge(S["g_ps"], made(g, e, NB))
                act.wait_ge(S["hh"], made(g, e - 2, NB))
                act.activation(sg[0:rows, e % 2, :], PS[0:rows, e % 2, :], ACT.Silu).then_inc(S["sg"], 1)

            def e_xT(g, dst=lambda t: xTn[:, :, t * P:(t + 1) * P]):
                for t in range(GT):
                    act.wait_ge(S["xnT_ps"], made(2 * NSEQ + g * GT + (t | 1)))
                    act.activation(dst(t), two(PS[:, 4 + t // 2, (t % 2) * D:(t % 2 + 1) * D]),
                                   ACT.Copy).then_inc(S["xnT"], 1)

            def e_exps(g):
                act.wait_ge(S["shift_l"], g + 1)
                act.activation(lg[:, :, 0:NE], lg[:, :, 0:NE], ACT.Exp).then_inc(S["exp_l"], 1)
                act.activation(combn[:, :, NE:NE + 1], lg[:, :, NE:NE + 1], ACT.Exp, scale=-1.0)\
                    .then_inc(S["expg"], 1)

            def e_take(g):
                act.wait_ge(S["h_ps"], made(g - 1, NB - 1, NB))
                act.wait_ge(S["xnT"], made(2 * NSEQ + g * GT + GT - 1))
                act.activation(xT3, xTn, ACT.Copy).then_inc(S["xT_in"], 1)

            def e_body(g, more):
                for e in range(NB):
                    if e:
                        e_silu(g, e)
                    if e == STEP and more:
                        e_xT(g + 1)
                    if e == STEP and not more:
                        e_xT(g + 1, lambda t: xnT4[:, t])
                    if e == STEP + 2 and more:
                        e_exps(g + 1)
                if more:
                    e_take(g + 1)
                    e_silu(g + 1, 0)

            piped(act, x_front, x_body)

            act.wait_ge(S["x_done"], made(2 * NSEQ - 1))
            e_exps(0)
            grouped(act, None, e_body)

            def l_xnT(g, t):
                act.wait_ge(S["xnT_ps"], made(3 * NSEQ + g * GT + t))
                act.activation(xnT4[:, t], two(PS[:, 4 + t, 0:D]), ACT.Copy).then_inc(S["xnT"], 1)

            def l_body(g, more):
                for t in range(GT):
                    act.wait_ge(S["g_gk_ps"], g * GT + t + 1)
                    act.activation(g_gk[t][0:LR, :], PS[0:LR, t, D:D + P], ACT.Copy).then_inc(S["g_gk"], 1)
                for t in range(GT):
                    act.wait_ge(S["g_qk_ps"], g * GT + t + 1)
                    act.activation(g_qk[t], PS[:, 4 + t, :].rearrange("p (c t) -> p c t", c=2 * DC), ACT.Copy)\
                        .then_inc(S["g_qk"], 1)
                for t in range(GT):
                    act.wait_ge(S["g_z_ps"], g * GT + t + 1)
                    for c in range(DC):
                        i = act.activation(g_zb[t][:, c, :], PS[:, t, c * P:(c + 1) * P], ACT.Identity,
                                           bias=l_bgk[:, c:c + 1], scale=1.0)
                    i.then_inc(S["g_z"], 1)
                for t in range(GT):
                    act.wait_ge(S["g_z"], g * GT + t + 1)
                    act.activation(g_t1[t], g_zb[t], ACT.Abs).then_inc(S["g_abs"], 1)
                for t in range(GT):
                    act.wait_ge(S["g_abs"], g * GT + t + 1)
                    act.activation(g_t1[t], g_t1[t], ACT.Exp, scale=-1.0).then_inc(S["g_exp"], 1)
                for t in range(GT):
                    act.wait_ge(S["g_exp"], g * GT + t + 1)
                    act.activation(g_t1[t], g_t1[t], ACT.Ln, bias=1.0).then_inc(S["g_ln"], 1)
                for t in range(GT):
                    act.wait_ge(S["g_v_ps"], g * GT + t + 1)
                    act.activation(g_v[t], PS[:, t, :], ACT.Copy).then_inc(S["g_v"], 1)
                for t in range(GT):
                    act.wait_ge(S["g_dq"], g * GT + t + 1)
                    act.activation(g_zb[t], g_zb[t], ACT.Exp, scale=1.0 / GATE_NORM).then_inc(S["g_eq"], 1)
                    act.wait_ge(S["g_dk"], g * GT + t + 1)
                    act.activation(g_kx[t], g_kx[t], ACT.Exp, scale=1.0 / GATE_NORM).then_inc(S["g_ek"], 1)
                for t in range(GT):
                    act.wait_ge(S["g_g_ps"], g * GT + t + 1)
                    act.activation(g_gate[t], PS[:, 4 + t, :], ACT.Silu).then_inc(S["g_gate"], 1)
                for t in range(GT):
                    act.wait_ge(S["g_o_ps"], g * GT + t + 1)
                    for h in range(H1):
                        i = act.activation(g_sq[t][:, h, :], PS[:, t, h * P:(h + 1) * P], ACT.Square,
                                           accum_out=g_ss[:, t, h:h + 1])
                    i.then_inc(S["g_ss"], 1)
                for t in range(GT):
                    if more:
                        l_xnT(g + 1, t)
                    act.wait_ge(S["g_yT_ps"], g * GT + t + 1)
                    act.activation(g_yT[t], PS[:, t, :].rearrange("p (h t) -> p h t", h=H1), ACT.Copy)\
                        .then_inc(S["g_yT"], 1)

            act.wait_ge(S["x_done"], made(3 * NSEQ - 1))
            act.wait_ge(S["ld_m"], LD_M)
            grouped(act, None, l_body)

            def m_front(g):
                for t in range(GT):
                    act.wait_ge(S["xnT_ps"], made(LAST + g * GT + t))
                    act.activation(xnT4[:, t], two(PS[:, t, 0:D]), ACT.Copy).then_inc(S["xnT"], 1)
                    act.activation(m_cT[t], two(PS[:, t, D:2 * D]), ACT.Copy).then_inc(S["m_cT"], 1)
                for t in range(GT - 1):
                    m_bias(g, t)

            def m_bias(g, t):
                act.wait_ge(S["m_qk_ps"], g * GT + t + 1)
                for c in range(DC):
                    act.activation(m_qk[t][:, c, :], PS[:, 4 + t, c * P:(c + 1) * P], ACT.Identity,
                                   bias=m_bq[:, c:c + 1], scale=1.0)
                    i = act.activation(m_qk[t][:, DC + c, :], PS[:, 4 + t, D + c * P:D + (c + 1) * P],
                                       ACT.Identity, bias=m_bk[:, c:c + 1], scale=1.0)
                i.then_inc(S["m_qk"], 1)

            def m_body(g, more):
                for t in range(GT):
                    act.wait_ge(S["m_low"], g * GT + t + 1)
                    act.activation(m_e[t], m_s[t], ACT.Exp, bias=m_low[t], scale=-1.0, accum_out=m_sum[t])\
                        .then_inc(S["m_exp"], 1)
                for t in range(GT):
                    act.wait_ge(S["m_pT_ps"], g * GT + t + 1)
                    act.activation(m_pT[t], PS[:, t, P:2 * P], ACT.Copy).then_inc(S["m_pT"], 1)
                for t in range(GT):
                    act.wait_ge(S["m_oT_ps"], g * GT + t + 1)
                    act.activation(m_oT[t], two(PS[:, 4 + t, 0:D]), ACT.Copy).then_inc(S["m_oT"], 1)
                if more:
                    m_front(g + 1)
                for t in range(GT):
                    act.wait_ge(S["f_xnT_ps"], g * GT + t + 1)
                    act.activation(f_xnT[t], two(PS[:, t, 0:D]), ACT.Copy).then_inc(S["f_xnT"], 1)
                if more:
                    m_bias(g + 1, GT - 1)

            act.wait_ge(S["x_done"], made(4 * NSEQ - 1))
            m_front(0)
            m_bias(0, GT - 1)
            grouped(act, None, m_body)

        @block.tensor
        def _(pe):
            def ln_T(i):
                pe.wait_ge(S["xn"], made(i))
                pe.wait_ge(S["xnT"], made(i - 1))
                for c in range(DC):
                    m = pe.transpose(PS[:, 4, c * P:(c + 1) * P], xn[:, c * P:(c + 1) * P], ident[:, :])
                m.then_inc(S["xnT_ps"], 1)

            def q_or_k(b, w, bank):
                for oc in range(DC):
                    for c in range(DC):
                        m = pe.matmul(PS[:, bank, oc * P:(oc + 1) * P], w[:, c, oc * P:(oc + 1) * P],
                                      xnT[:, c, :], start=(c == 0), stop=(c == DC - 1))
                return m

            def qs(b, first=False):
                pe.wait_ge(S["xnT"], made(b))
                if not first:
                    pe.wait_ge(S["x_done"], made(b - 2))
                q_or_k(b, a_wq, 5).then_inc(S["q_ps"], 1)

            def ks(b, first=False):
                pe.wait_ge(S["xnT"], made(b))
                if not first:
                    pe.wait_ge(S["v"], made(b - 1))
                q_or_k(b, a_wk, 6)

            def vs(b):
                for c in range(DC):
                    m = pe.matmul(PS[:, 6, D:2 * D], xnT[:, c, :], a_wv[:, c, :], start=(c == 0), stop=(c == DC - 1))
                m.then_inc(S["kv_ps"], 1)

            def scores(b, groups):
                if 0 in groups:
                    pe.wait_ge(S["q_heads"], made(b))
                    pe.wait_ge(S["kT"], made(b))
                    pe.wait_ge(S["pt"], made(b - 1, 3, 4))
                for g in groups:
                    for h in range(4 * g, 4 * g + 4):
                        m = pe.matmul(PS[:, g, (h % 4) * P:(h % 4 + 1) * P], q_heads[:, h, :], kT[:, h // HC, :],
                                      start=True, stop=True)
                    m.then_inc(S["s_ps"], 1)

            def p_T(b, g):
                pe.wait_ge(S["expd"], made(b, g, 4))
                for h in range(4 * g, 4 * g + 4):
                    m = pe.transpose(PS[:, g, (h % 4) * P:(h % 4 + 1) * P], ex[:, h, :], ident[:, :])
                m.then_inc(S["pt_ps"], 1)

            def av(b, g):
                if g == 0:
                    pe.wait_ge(S["v"], made(b))
                pe.wait_ge(S["pt"], made(b, g, 4))
                for h in range(4 * g, 4 * g + 4):
                    m = pe.matmul(PS[:, 7, h * (HD + 1):(h + 1) * (HD + 1)], pT[:, h, :], va[:, h, :],
                                  start=True, stop=True)
                if g == 3:
                    m.then_inc(S["o_ps"], 1)

            def ctx_T(b):
                pe.wait_ge(S["ctx"], b + 1)
                for c in range(DC):
                    m = pe.transpose(PS[:, 7, c * P:(c + 1) * P], cx[:, c * P:(c + 1) * P], ident[:, :])
                m.then_inc(S["ctxT_ps"], 1)

            def ctx_out(b):
                pe.wait_ge(S["ctxT"], b + 1)
                for c in range(DC):
                    m = pe.matmul(PS[:, 5, D:2 * D], cxT[:, c, :], a_wo[:, c, :], start=(c == 0), stop=(c == DC - 1))
                m.then_inc(S["out_ps"], 1)

            def front(b):
                ln_T(b)
                qs(b, first=True)
                ks(b, first=True)
                vs(b)
                scores(b, range(4))
                ln_T(b + 1)

            def body(b, more):
                if more:
                    ks(b + 1)
                p_T(b, 0)
                p_T(b, 1)
                if more:
                    qs(b + 1)
                av(b, 0)
                p_T(b, 2)
                av(b, 1)
                if more:
                    vs(b + 1)
                p_T(b, 3)
                av(b, 2)
                av(b, 3)
                if more:
                    scores(b + 1, range(3))
                if more > 1:
                    ln_T(b + 2)
                ctx_T(b)
                if more:
                    scores(b + 1, (3,))
                ctx_out(b)

            pe.wait_ge(S["consts"], CONSTS)
            pe.wait_ge(S["ld_a"], LD_A)
            piped_by_two(pe, front, body)

            def product(ps, lhsT, rhs, chunks=DC):
                for c in range(chunks):
                    m = pe.matmul(ps, lhsT(c), rhs(c), start=(c == 0), stop=(c == chunks - 1))
                return m

            def x_T(b):
                pe.wait_ge(S["xn"], made(NSEQ + b))
                pe.wait_ge(S["v2"], made(b - 1))
                for c in range(DC):
                    pe.transpose(PS[:, 4, c * P:(c + 1) * P], xn[:, c * P:(c + 1) * P], ident[:, :])
                copy_wait(b)
                for c in range(DC):
                    m = pe.transpose(PS[:, 4, D + c * P:D + (c + 1) * P], cn[:, c * P:(c + 1) * P], ident[:, :])
                m.then_inc(S["xnT_ps"], 1)

            def copy_wait(b):
                pe.wait_ge(S["x_cn"], made(b))

            def x_q(b):
                pe.wait_ge(S["xnT"], made(NSEQ + b))
                for oc in range(DC):
                    m = product(PS[:, 5, oc * P:(oc + 1) * P], lambda c: x_wq[:, c, oc * P:(oc + 1) * P],
                                lambda c: xnT[:, c, :])
                m.then_inc(S["q_ps"], 1)

            def x_k(b):
                pe.wait_ge(S["means"], made(b, 1, 2))
                for oc in range(DC):
                    m = product(PS[:, 4, oc * KEYS:(oc + 1) * KEYS], lambda c: x_wk[:, c, oc * P:(oc + 1) * P],
                                lambda c: cT[:, c, :])
                m.then_inc(S["k_ps"], 1)

            def x_v(b):
                pe.wait_ge(S["kx"], made(b))
                product(PS[:, 4, 0:D], lambda c: cT[:, c, LOWK:KEYS], lambda c: x_wv[:, c, :])

            def x_v_low(b):
                product(PS[:, 4, D:2 * D], lambda c: cT[:, c, 0:P], lambda c: x_wv[:, c, :])\
                    .then_inc(S["v2_ps"], 1)

            def x_scores(b, g):
                if g == 0:
                    pe.wait_ge(S["qh"], made(b))
                    pe.wait_ge(S["kx"], made(b))
                pe.wait_ge(S["shifted"], made(b, g - 2, 8))
                for j in range(2):
                    h = 2 * g + j
                    m = pe.matmul(PS[:, g % 2, j * KEYS:(j + 1) * KEYS], q_heads[:, h, :], kx[:, h // HC, :],
                                  start=True, stop=True)
                m.then_inc(S["s2_ps"], 1)

            def x_pT(b, g):
                pe.wait_ge(S["expd2"], made(b, g, 8))
                pe.wait_ge(S["pt2"], made(b, g - 2, 8))
                for j in range(2):
                    h = 2 * g + j
                    pe.transpose(PS[:, 2 + g % 2, j * P:(j + 1) * P], sc2[:, h, LOWK:KEYS], ident[:, :])
                    m = pe.transpose(PS[:, 2 + g % 2, D + j * P:D + (j + 1) * P], sc2[:, h, 0:P], ident[:, :])
                m.then_inc(S["pt2_ps"], 1)

            def x_av(b, g):
                if g == 0:
                    pe.wait_ge(S["v2"], made(b))
                    pe.wait_ge(S["x_done"], made(NSEQ + b - 1))
                pe.wait_ge(S["pt2"], made(b, g, 8))
                for j in range(2):
                    h = 2 * g + j
                    o = 3 * VW * (h % 8)
                    pe.matmul(PS[:, 6 + g // 4, o:o + VW], pT2[:, g, j * P:(j + 1) * P], vx[:, h, :],
                              start=True, stop=True)
                    m = pe.matmul(PS[:, 6 + g // 4, o + VW:o + 3 * VW], pT2[:, g, D + j * P:D + (j + 1) * P],
                                  vlow[:, h, :], start=True, stop=True)
                if g == 7:
                    m.then_inc(S["o2_ps"], 1)

            def x_ctx_T(b):
                pe.wait_ge(S["ctx"], NSEQ + b + 1)
                for c in range(DC):
                    m = pe.transpose(PS[:, 7, c * P:(c + 1) * P], cx[:, c * P:(c + 1) * P], ident[:, :])
                m.then_inc(S["ctxT_ps"], 1)

            def x_out(b):
                pe.wait_ge(S["ctxT"], NSEQ + b + 1)
                product(PS[:, 6, 0:D], lambda c: cxT[:, c, :], lambda c: x_wo[:, c, :]).then_inc(S["out_ps"], 1)

            def turn_weights():
                pe.wait_ge(S["ld_w"], LD_W)
                for n, (dst, blocks) in enumerate(turns):
                    if n == len(turns) - 1:
                        pe.wait_ge(S["w_step"], 5)
                    if n >= 4:
                        if n % 2:
                            pe.wait_ge(S["turned_v"], (n - 3) // 2)
                        else:
                            pe.wait_ge(S["turned_a"], (n - 2) // 2)
                    for src, col in blocks:
                        m = pe.transpose(PS[0:src.shape[1], n % 4, col:col + src.shape[0]], src,
                                         ident[0:src.shape[0], 0:src.shape[0]])
                    m.then_inc(S["turn_ps"], 1)
                pe.wait_ge(S["turned_a"], (len(turns) + 1) // 2)
                pe.wait_ge(S["turned_v"], len(turns) // 2)

            def x_front(b):
                x_T(b)
                pe.wait_ge(S["x_done"], made(NSEQ - 1))
                x_q(b)
                pe.wait_ge(S["w_tot"], 1)
                pe.matmul(PS[:, 6, 0:1], ones[:, :], f_stat[:, 0:1], start=True, stop=True).then_inc(S["w_mean"], 1)
                x_k(b)
                pe.wait_ge(S["x_bv"], DC)
                product(PS[:, 7, 0:D], lambda c: x_bvb[:, c, :], lambda c: x_wo[:, c, :]).then_inc(S["x_bias_ps"], 1)
                x_v(b)
                x_v_low(b)
                turn_weights()
                x_scores(b, 0)
                x_scores(b, 1)

            def x_body(b, more):
                for g in range(8):
                    if g + 2 < 8:
                        x_scores(b, g + 2)
                    x_pT(b, g)
                    if g:
                        x_av(b, g - 1)
                    if g == 3 and more:
                        x_T(b + 1)
                    if g == 4 and more:
                        x_q(b + 1)
                    if g == 6 and more:
                        x_k(b + 1)
                    if g == 4 and not more:
                        pe.wait_ge(S["qh"], made(NSEQ - 1))
                        e_T(0)
                    if g == 6 and not more:
                        e_router(0)
                x_av(b, 7)
                if more:
                    x_scores(b + 1, 0)
                    x_scores(b + 1, 1)
                    x_v(b + 1)
                if not more:
                    pe.wait_ge(S["ld_e"], LD_E)
                    e_up(0, 0, ("gate",))
                x_ctx_T(b)
                if more:
                    x_v_low(b + 1)
                else:
                    e_up(0, 0, ("up",))
                x_out(b)

            pe.wait_ge(S["ld_c"], LD_C)
            pe.wait_ge(S["ld_b"], LD_B)
            def e_up(g, e, which=("gate", "up")):
                rows = F_OF(e)
                if e < NE:
                    wg, wu = (lambda c: e_gu[:, e, c, 0:FE]), (lambda c: e_gu[:, e, c, FE:2 * FE])
                else:
                    o = (e - NE) * FE
                    wg, wu = (lambda c: s_g[:, c, o:o + rows]), (lambda c: s_u[:, c, o:o + rows])
                if "gate" in which:
                    if e == 0:
                        pe.wait_ge(S["xT_in"], g + 1)
                    pe.wait_ge(S["sg"], made(g, e - 2, NB))
                    product(PS[0:rows, e % 2, :], wg, lambda c: xT3[:, c, :]).then_inc(S["g_ps"], 1)
                if "up" in which:
                    pe.wait_ge(S["hh"], made(g, e - 2, NB))
                    product(PS[0:rows, 2 + e % 2, :], wu, lambda c: xT3[:, c, :]).then_inc(S["h_ps"], 1)

            def e_down(g, e):
                rows, r = F_OF(e), e % 2
                w = e_dn[:, e, :] if e < NE else s_dn[0:rows, e - NE, :]
                pe.wait_ge(S["hh"], made(g, e, NB))
                if e == 0:
                    pe.wait_ge(S["acc"], made(g - 1, NB - 2, NB - 1))
                elif e == 1:
                    pe.wait_ge(S["x_done"], made(2 * NSEQ + g * GT - 1))
                else:
                    pe.wait_ge(S["acc"], made(g, e - 2, NB - 1))
                for t in range(GT):
                    m = pe.matmul(PS[:, 4 + 2 * r + t // 2, (t % 2) * D:(t % 2 + 1) * D],
                                  hh[0:rows, r, t * P:(t + 1) * P], w, start=True, stop=True)
                m.then_inc(S["d_ps"], 1)

            def e_T(g):
                for t in range(GT):
                    pe.wait_ge(S["xn"], made(2 * NSEQ + g * GT + t))
                    for c in range(DC):
                        o = (t % 2) * D + c * P
                        m = pe.transpose(PS[:, 4 + t // 2, o:o + P], xn4[:, t, c * P:(c + 1) * P], ident[:, :])
                    m.then_inc(S["xnT_ps"], 1)

            def e_router(g):
                pe.wait_ge(S["xnT"], made(2 * NSEQ + g * GT + GT - 1))
                for t in range(GT):
                    m = product(PS[:, 4, t * (NE + 1):(t + 1) * (NE + 1)],
                                lambda c: xTn[:, c, t * P:(t + 1) * P], lambda c: gwT[:, c, :])
                m.then_inc(S["r_ps"], 1)

            def e_body(g, more):
                for e in range(NB):
                    if e + 1 < NB:
                        e_up(g, e + 1)
                    if e == STEP and more:
                        e_router(g + 1)
                        pe.wait_ge(S["logits"], g + 2)
                    if e == STEP and not more:
                        pe.wait_ge(S["xnT"], made(3 * NSEQ + GT - 1))
                    e_down(g, e)
                    if e == STEP - 1:
                        pe.wait_ge(S["acc"], made(g, STEP - 2, NB - 1))
                        e_T(g + 1)
                if more:
                    e_up(g + 1, 0)

            piped(pe, x_front, x_body)

            pe.wait_ge(S["logits"], 1)
            pe.wait_ge(S["x_done"], made(2 * NSEQ - 1))
            grouped(pe, None, e_body)

            def l_front(g):
                for t in range(GT):
                    pe.wait_ge(S["xn"], made(3 * NSEQ + g * GT + t))
                    for c in range(DC):
                        m = pe.transpose(PS[:, 4 + t, c * P:(c + 1) * P], xn4[:, t, c * P:(c + 1) * P], ident[:, :])
                    m.then_inc(S["xnT_ps"], 1)

            def gates(g, t):
                pe.wait_ge(S["g_qk"], g * GT + t + 1)
                product(PS[:, 4 + t, :], lambda c: xnT4[:, t, c, :], lambda c: l_wg[:, c, :])\
                    .then_inc(S["g_g_ps"], 1)

            def scores(g, t):
                pe.wait_ge(S["consts"], CONSTS)
                pe.wait_ge(S["g_v"], g * GT + t + 1)
                pe.wait_ge(S["g_kx"], g * GT + t + 1)
                pe.wait_ge(S["g_qx"], g * GT + t + 1)
                for n in range(NCB):
                    w = CB * (n + 1)
                    for c in range(DC):
                        o = (c * NCB + n) * 2 * CB
                        m = pe.matmul(PS[0:w, t, o:o + 2 * CB], k_block(t, n)[:, c, :],
                                      g_qx[t][:, c, n].rearrange("p r t -> p (r t)"), start=True, stop=True)
                m.then_inc(S["g_a_ps"], 1)

            def y_T(g, t):
                pe.wait_ge(S["g_y"], g * GT + t + 1)
                for h in range(H1):
                    m = pe.transpose(PS[:, t, h * P:(h + 1) * P], g_gate[t][:, h * P:(h + 1) * P], ident[:, :])
                m.then_inc(S["g_yT_ps"], 1)

            def l_body(g, more):
                for t in range(GT):
                    pe.wait_ge(S["xnT"], made(3 * NSEQ + g * GT + t))
                    product(PS[0:LR, t, D:D + P], lambda c: l_gk1[:, c, :], lambda c: xnT4[:, t, c, :])\
                        .then_inc(S["g_gk_ps"], 1)
                pe.wait_ge(S["x_done"], made(3 * NSEQ + g * GT - 1))
                for t in range(GT):
                    for n, w in enumerate((l_wq, l_wk)):
                        for oc in range(DC):
                            m = product(PS[:, 4 + t, n * D + oc * P:n * D + (oc + 1) * P],
                                        lambda c: w[:, c, oc * P:(oc + 1) * P], lambda c: xnT4[:, t, c, :])
                    m.then_inc(S["g_qk_ps"], 1)
                for t in range(GT):
                    pe.wait_ge(S["g_gk"], g * GT + t + 1)
                    for oc in range(DC):
                        m = pe.matmul(PS[:, t, oc * P:(oc + 1) * P], l_gk2[:, oc * P:(oc + 1) * P],
                                      g_gk[t][0:LR, :], start=True, stop=True)
                    m.then_inc(S["g_z_ps"], 1)
                for t in range(GT):
                    pe.wait_ge(S["g_z"], g * GT + t + 1)
                    product(PS[:, t, :], lambda c: xnT4[:, t, c, :], lambda c: l_wv[:, c, :]).then_inc(S["g_v_ps"], 1)
                for t in range(GT):
                    gates(g, t)
                for t in range(GT):
                    scores(g, t)
                for t in range(GT):
                    pe.wait_ge(S["g_at"], g * GT + t + 1)
                    for h in range(H1):
                        m = pe.matmul(PS[:, t, h * P:(h + 1) * P], g_at[t][:, h % 2, h // 2, :],
                                      g_v[t][:, h * P:(h + 1) * P], start=True, stop=True)
                    m.then_inc(S["g_o_ps"], 1)
                if more:
                    pe.wait_ge(S["g_gate"], g * GT + GT)
                    l_front(g + 1)
                y_T(g, 0)
                pe.wait_ge(S["consts"], CONSTS)
                pe.wait_ge(S["g_wo"], 1)
                for t in range(GT):
                    if t + 1 < GT:
                        y_T(g, t + 1)
                    if more:
                        pe.wait_ge(S["xnT"], made(3 * NSEQ + (g + 1) * GT + t))
                    else:
                        pe.wait_ge(S["g_gate"], g * GT + t + 1)
                    pe.wait_ge(S["g_yT"], g * GT + t + 1)
                    product(PS[:, 4 + t, 0:D], lambda c: g_yT[t][:, c, :], lambda c: l_wo[:, c, :], DV // P)\
                        .then_inc(S["g_out_ps"], 1)

            grouped(pe, None, l_body)

            def m_front(g):
                for t in range(GT):
                    pe.wait_ge(S["xn"], made(LAST + g * GT + t))
                    pe.wait_ge(S["m_cn"], g * GT + t + 1)
                    for n, src in enumerate((xn4[:, t], cn4[t])):
                        for c in range(DC):
                            m = pe.transpose(PS[:, t, n * D + c * P:n * D + (c + 1) * P], src[:, c * P:(c + 1) * P],
                                             ident[:, :])
                    m.then_inc(S["xnT_ps"], 1)

            def m_project(g, tiles, first=False):
                for t in tiles:
                    pe.wait_ge(S["xnT"], made(LAST + g * GT + t))
                    if not first:
                        pe.wait_ge(S["m_done"], (g - 1) * GT + t + 1)
                    pe.wait_ge(S["m_cT"], g * GT + t + 1)
                    for n, (w, src) in enumerate(((m_wq, xnT4[:, t]), (m_wk, m_cT[t]))):
                        for oc in range(DC):
                            m = product(PS[:, 4 + t, n * D + oc * P:n * D + (oc + 1) * P],
                                        lambda c: w[:, c, oc * P:(oc + 1) * P], lambda c: src[:, c, :])
                    m.then_inc(S["m_qk_ps"], 1)

            def m_body(g, more):
                for t in range(GT):
                    pe.wait_ge(S["x_done"], made(LAST + (g - 1) * GT + t))
                    pe.wait_ge(S["m_qk"], g * GT + t + 1)
                    product(PS[:, t, 0:P], lambda c: m_qk[t][:, c, :], lambda c: m_qk[t][:, DC + c, :])\
                        .then_inc(S["m_s_ps"], 1)
                for t in range(GT):
                    pe.wait_ge(S["m_exp"], g * GT + t + 1)
                    pe.transpose(PS[:, t, P:2 * P], m_e[t], ident[:, :]).then_inc(S["m_pT_ps"], 1)
                for t in range(GT):
                    pe.wait_ge(S["m_pT"], g * GT + t + 1)
                    pe.matmul(PS[:, t, D:2 * D], m_pT[t], cn4[t], start=True, stop=True).then_inc(S["m_o_ps"], 1)
                for t in range(GT):
                    pe.wait_ge(S["m_o"], g * GT + t + 1)
                    for c in range(DC):
                        m = pe.transpose(PS[:, 4 + t, c * P:(c + 1) * P], m_o[t][:, c * P:(c + 1) * P], ident[:, :])
                    m.then_inc(S["m_oT_ps"], 1)
                for t in range(GT):
                    if t == GT // 2 and more:
                        m_front(g + 1)
                    pe.wait_ge(S["m_oT"], g * GT + t + 1)
                    product(PS[:, 4 + t, D:2 * D], lambda c: m_oT[t][:, c, :], lambda c: m_wo[:, c, :])\
                        .then_inc(S["m_out_ps"], 1)
                if more:
                    m_project(g + 1, range(GT - 1))
                    pe.wait_ge(S["m_cT"], (g + 1) * GT + GT)
                for t in range(GT):
                    pe.wait_ge(S["f_xn"], g * GT + t + 1)
                    for c in range(DC):
                        m = pe.transpose(PS[:, t, c * P:(c + 1) * P], f_xn[t][:, c * P:(c + 1) * P], ident[:, :])
                    m.then_inc(S["f_xnT_ps"], 1)
                if more:
                    m_project(g + 1, (GT - 1,))
                for t in range(GT):
                    pe.wait_ge(S["f_xnT"], g * GT + t + 1)
                    product(PS[:, t, D:2 * D], lambda c: f_xnT[t][:, c, :], lambda c: f_w[:, c, :])\
                        .then_inc(S["f_out_ps"], 1)

            pe.wait_ge(S["x_done"], made(4 * NSEQ - 1))
            m_front(0)
            m_project(0, range(GT), first=True)
            grouped(pe, None, m_body)

        @block.vector
        def _(dv):
            def ln_stats(i, b):
                dv.wait_ge(S["rstd"], made(i - 1))
                dv.bn_stats(stats[:, :], tile(X, b)).then_inc(S["ln_stats"], 1)

            def ln_var(i):
                dv.wait_ge(S["consts"], CONSTS)
                dv.wait_ge(S["ln_stats"], i + 1)
                dv.bn_aggr(mv[:, :], stats[:, :]).then_inc(S["ln_aggr"], 1)
                dv.wait_ge(S["ln_aggr"], i + 1)
                dv.tensor_scalar(var[:, :], mv[:, 1:2], EPS, None, ALU.add).then_inc(S["ln_var"], 1)

            def ln(i, b):
                ln_stats(i, b)
                ln_var(i)

            def ln_apply(i, b):
                dv.wait_ge(S["rstd"], made(i))
                dv.wait_ge(S["xnT_ps"], made(i - 1))
                dv.tensor_scalar(xn[:, :], tile(X, b), mv[:, 0:1], rstd[:, 0:1], ALU.subtract,
                                 ALU.mult).then_inc(S["xn"], 1)

            def q_split(b):
                dv.wait_ge(S["q_ps"], made(b))
                for c in range(DC):
                    i = dv.tensor_tensor(q_heads[:, c * HC:(c + 1) * HC, :],
                                         over(PS[:, 5, c * P:(c + 1) * P], 1, HC), over(hmask[:, :], 2, P), ALU.mult)
                i.then_inc(S["q_heads"], 1)

            def scale(b, g):
                dv.wait_ge(S["s_ps"], made(b, g, 4))
                dv.wait_ge(S["expd"], made(b - 1, g, 4))
                dv.tensor_tensor(sc[:, 4 * g:4 * g + 4, :], PS[:, g, :].rearrange("p (h t) -> p h t", h=4),
                                 over(nA[:, :], 1, 4), ALU.mult).then_inc(S["scaled"], 1)

            def hide_max(b, g):
                dv.wait_ge(S["consts"], CONSTS)
                dv.wait_ge(S["scaled"], b * 4 + g + 1)
                for h in range(4 * g, 4 * g + 4):
                    i = dv.tensor_tensor_reduce(sc[:, h, :], sc[:, h, :], hide[:, :], 1.0, BIG, ALU.add, ALU.min,
                                                low[:, h:h + 1])
                i.then_inc(S["maxed"], 1)

            def norm(b):
                dv.wait_ge(S["o_ps"], made(b))
                o = PS[:, 7, 0:H0 * (HD + 1)].rearrange("p (h d) -> p h d", h=H0)
                dv.reciprocal(o_inv[:, :].unsqueeze(2), o[:, :, HD:HD + 1]).then_inc(S["o_inv"], 1)
                dv.wait_ge(S["o_inv"], b + 1)
                dv.tensor_tensor(cx[:, :].rearrange("p (h d) -> p h d", h=H0), o[:, :, 0:HD],
                                 over(o_inv[:, :], 2, HD), ALU.mult).then_inc(S["ctx"], 1)

            def add_x(b):
                dv.wait_ge(S["out_ps"], made(b))
                dv.wait_ge(S["x_biased"], made(b))
                dv.tensor_tensor(tile(X, b), PS[:, 5, D:2 * D], tile(X, b), ALU.add).then_inc(S["x_done"], 1)

            def relative(d):
                return part(work, d * P, P)

            def rel_bias():
                dv.wait_ge(S["dist"], 1)
                dv.wait_ge(S["ld_rel"], 16)
                dv.tensor_scalar(dist[:, :], dist[:, :], float(CLIP), None, ALU.min).then_inc(S["dist"], 1)
                dv.tensor_scalar(rel[:, :], rel[:, :], -float(HD) ** -0.5, None, ALU.mult).then_inc(S["dist"], 1)
                dv.wait_ge(S["dist"], 3)
                for d in range(CLIP + 1):
                    i = dv.tensor_scalar(relative(d), dist[:, :], float(d), None, ALU.is_equal)
                i.then_inc(S["rel_term"], 1)
                sums = nA, relT
                dv.wait_ge(S["rel_term"], 1)
                for d in range(2):
                    dv.tensor_scalar(sums[d][:, :], relative(d), rel[:, d:d + 1], None, ALU.mult)\
                        .then_inc(S["rel_sum"], 1)
                for d in range(2, CLIP + 1):
                    if d == CLIP * 2 // 3:
                        q_split(0)
                    dv.wait_ge(S["rel_sum"], d - 1)
                    dv.scalar_tensor_tensor(out=sums[d % 2][:, :], in0=relative(d), scalar=rel[:, d:d + 1],
                                            in1=sums[d % 2][:, :], op0=ALU.mult, op1=ALU.add)\
                        .then_inc(S["rel_sum"], 1)
                dv.wait_ge(S["rel_sum"], CLIP + 1)
                dv.tensor_tensor(nA[:, :], nA[:, :], relT[:, :], ALU.add).then_inc(S["rel_sum"], 1)

            def front(b):
                ln(b, b)
                ln_apply(b, b)
                ln(b + 1, b + 1)
                rel_bias()
                ln_apply(b + 1, b + 1)
                dv.wait_ge(S["rel_sum"], CLIP + 2)
                dv.wait_ge(S["ld_x_rest"], 16)
                scale(b, 0)
                scale(b, 1)
                hide_max(b, 0)
                hide_max(b, 1)
                scale(b, 2)
                hide_max(b, 2)

            def body(b, more):
                scale(b, 3)
                hide_max(b, 3)
                if more:
                    q_split(b + 1)
                if more > 1:
                    ln(b + 2, b + 2)
                    ln_apply(b + 2, b + 2)
                if not more:
                    dv.wait_ge(S["ld_c"], LD_C)
                    x_ln(0)
                norm(b)
                if more:
                    scale(b + 1, 0)
                    scale(b + 1, 1)
                    hide_max(b + 1, 0)
                    hide_max(b + 1, 1)
                add_x(b)
                if more:
                    scale(b + 1, 2)
                    hide_max(b + 1, 2)

            def x_ctx(b):
                dv.wait_ge(S["cT"], made(b - 1))
                dv.tensor_copy(cn[:, :], tile(C, b)).then_inc(S["x_cn"], 1)

            def x_ln(b):
                ln(NSEQ + b, b)
                x_ctx(b)
                ln_apply(NSEQ + b, b)

            dv.wait_ge(S["consts"], CONSTS)
            dv.wait_ge(S["ld_x"], 16)
            front(0)
            with dv.Fori(0, NSEQ - 2) as b:
                body(b, 2)
            body(NSEQ - 2, 1)
            body(NSEQ - 1, 0)

            def x_q(b):
                dv.wait_ge(S["q_ps"], made(NSEQ + b))
                dv.wait_ge(S["s2_ps"], made(b - 1, 7, 8))
                for c in range(DC):
                    i = dv.scalar_tensor_tensor(out=q_heads[:, c * HC:(c + 1) * HC, :],
                                                in0=over(PS[:, 5, c * P:(c + 1) * P], 1, HC), scalar=x_bq[:, c:c + 1],
                                                in1=over(hmask[:, :], 2, P), op0=ALU.add, op1=ALU.mult)
                i.then_inc(S["qh"], 1)

            def levels(b, g):
                for lv, (o, n) in enumerate(zip((LOWK, 0, LV[1]), LV)):
                    yield (PS[:, g % 2, 0:2 * KEYS].rearrange("p (h k) -> p h k", h=2)[:, :, o:o + n],
                           sc2[:, 2 * g:2 * g + 2, o:o + n], mx[:, 2 * g:2 * g + 2, lv], n)

            def x_max(b, g):
                dv.wait_ge(S["s2_ps"], made(b, g, 8))
                for s_in, _, m, _ in levels(b, g):
                    i = dv.tensor_reduce(m, s_in, AX, ALU.max)
                i.then_inc(S["maxed2"], 1)

            def x_shift(b, g):
                dv.wait_ge(S["maxed2"], b * 8 + g + 1)
                dv.wait_ge(S["pt2_ps"], made(b - 1, g, 8))
                for s_in, s_out, m, n in levels(b, g):
                    i = dv.tensor_tensor(s_out, s_in, over(m, 2, n), ALU.subtract)
                i.then_inc(S["shifted"], 1)

            def x_norm(b):
                dv.wait_ge(S["o2_ps"], made(b))
                dv.wait_ge(S["ctx"], NSEQ + b)
                outs = [PS[:, 6 + half, 0:8 * 3 * VW].rearrange("p (h l d) -> p h l d", h=8, l=3)
                        for half in range(2)]
                for half in range(2):
                    dv.reciprocal(o2_inv[:, half, :, :].unsqueeze(3), outs[half][:, :, :, HD:VW]).then_inc(S["o2_inv"], 1)
                for half in range(2):
                    dv.wait_ge(S["o2_inv"], b * 2 + half + 1)
                    dv.tensor_tensor(o2_part[:, half], outs[half][:, :, :, 0:HD], over(o2_inv[:, half], 3, HD),
                                     ALU.mult).then_inc(S["o2_part"], 1)
                for half in range(2):
                    dv.wait_ge(S["o2_part"], b * 2 + half + 1)
                    i = dv.tensor_reduce(cx[:, half * P:(half + 1) * P].rearrange("p (h d) -> p h d", h=8),
                                         o2_part[:, half].rearrange("p h l d -> p h d l"), AX, ALU.add)
                i.then_inc(S["ctx"], 1)

            def x_add(b):
                dv.wait_ge(S["out_ps"], made(NSEQ + b))
                dv.wait_ge(S["x_biased"], made(NSEQ + b))
                dv.scalar_tensor_tensor(out=tile(X, b), in0=PS[:, 6, 0:D], scalar=x_sm[:, 0:1], in1=tile(X, b),
                                        op0=ALU.mult, op1=ALU.add).then_inc(S["x_done"], 1)

            def turn_weights():
                dv.wait_ge(S["w_mean"], 1)
                dv.tensor_scalar(f_stat[:, 1:2], PS[:, 6, 0:1], 1.0 / (D * D), 0.7, ALU.mult, ALU.mult)\
                    .then_inc(S["w_step"], 1)
                dv.wait_ge(S["w_step"], 1)
                dv.tensor_scalar(f_stat[:, 2:3], f_stat[:, 1:2], -1.0, None, ALU.mult).then_inc(S["w_step"], 1)
                dv.wait_ge(S["w_step"], 2)
                dv.tensor_scalar(fl, fw, f_stat[:, 2:3], None, ALU.is_lt).then_inc(S["w_step"], 1)
                dv.wait_ge(S["w_step"], 3)
                dv.scalar_tensor_tensor(out=fw, in0=fw, scalar=f_stat[:, 1:2], in1=fl, op0=ALU.is_gt,
                                        op1=ALU.subtract).then_inc(S["w_step"], 1)
                dv.wait_ge(S["w_step"], 4)
                dv.tensor_scalar(fw, fw, f_alpha[:, 0:1], None, ALU.mult).then_inc(S["w_step"], 1)
                for n in range(1, len(turns), 2):
                    dv.wait_ge(S["turn_ps"], n + 1)
                    dv.tensor_copy(turns[n][0], turned(n)).then_inc(S["turned_v"], 1)

            def x_front(b):
                x_q(b)
                dv.wait_ge(S["x_sig"], 1)
                dv.tensor_scalar(x_sm[:, :], x_sm[:, :], 1.0, None, ALU.add).then_inc(S["x_sigd"], 1)
                dv.wait_ge(S["x_sigd"], 1)
                dv.reciprocal(x_sm[:, :], x_sm[:, :]).then_inc(S["x_sigd"], 1)
                dv.wait_ge(S["x_bias_ps"], 1)
                dv.tensor_tensor(x_bo[:, :], x_bo[:, :], PS[:, 7, 0:D], ALU.add).then_inc(S["x_sigd"], 1)
                dv.wait_ge(S["x_sigd"], 3)
                dv.tensor_scalar(x_bo[:, :], x_bo[:, :], 2.0, x_sm[:, 0:1], ALU.mult, ALU.mult).then_inc(S["x_bias"], 1)
                x_ln(b + 1)
                turn_weights()
                x_max(b, 0)
                x_shift(b, 0)
                x_max(b, 1)
                x_shift(b, 1)

            def x_body(b, more):
                for g in range(1, 8):
                    if g > 1:
                        x_shift(b, g)
                    if g < 7:
                        x_max(b, g + 1)
                    if g == 1 and not more:
                        dv.wait_ge(S["x_done"], made(NSEQ + GT - 1))
                        group_stats(0, 0)
                    if g == 3 and not more:
                        group_apply(0, 0, 2 * NSEQ)
                    if g == 7 and not more:
                        logits(0)
                if more:
                    x_q(b + 1)
                if more > 1:
                    x_ln(b + 2)
                x_norm(b)
                if more:
                    x_max(b + 1, 0)
                    x_shift(b + 1, 0)
                    x_max(b + 1, 1)
                    x_shift(b + 1, 1)
                x_add(b)

            dv.wait_ge(S["ld_b"], LD_B)
            dv.wait_ge(S["ld_c"], LD_C)
            dv.wait_ge(S["x_done"], made(NSEQ - 1))
            dv.wait_ge(S["ld_w"], LD_W)
            dv.wait_ge(S["consts"], CONSTS)
            fw = t_fw.rearrange("p a b -> p (a b)")
            fl = t_fl.rearrange("p a b -> p (a b)")
            dv.tensor_reduce(f_stat[:, 0:1], fw, AX, ALU.add, apply_absolute_value=True).then_inc(S["w_tot"], 1)
            for c in range(DC):
                dv.tensor_scalar(x_bvb[:, c, :], ones[:, :], x_bv[:, c:c + 1], None, ALU.mult).then_inc(S["x_bv"], 1)
            def group_stats(n, g):
                dv.wait_ge(S["gl_rstd"], n + 1)
                for t in range(GT):
                    k = dv.bn_stats(gl_stats[:, t, :], tile(X, g * GT + t))
                k.then_inc(S["gl_stats"], 1)
                dv.wait_ge(S["consts"], CONSTS)
                dv.wait_ge(S["gl_stats"], n + 1)
                for t in range(GT):
                    k = dv.bn_aggr(gl_mv[:, t, :], gl_stats[:, t, :])
                k.then_inc(S["gl_aggr"], 1)
                dv.wait_ge(S["gl_aggr"], n + 1)
                dv.tensor_scalar(gl_var[:, :], gl_mv[:, :, 1], EPS, None, ALU.add).then_inc(S["gl_var"], 1)

            def group_apply(n, g, i):
                dv.wait_ge(S["gl_rstd"], n + 2)
                dv.wait_ge(S["xnT_ps"], made(i - 1))
                for t in range(GT):
                    dv.tensor_scalar(xn4[:, t, :], tile(X, g * GT + t), gl_mv[:, t, 0:1], gl_rstd[:, t:t + 1],
                                     ALU.subtract, ALU.mult).then_inc(S["xn"], 1)

            def logits(g):
                dv.wait_ge(S["r_ps"], made(g))
                dv.tensor_copy(lg[:, :, :], PS[:, 4, 0:GT * (NE + 1)].rearrange("p (t e) -> p t e", t=GT))\
                    .then_inc(S["logits"], 1)

            def compare(g):
                dv.wait_ge(S["logits"], g + 1)
                dv.tensor_reduce(l1[:, :], lg[:, :, 0:NE], AX, ALU.max).then_inc(S["top1"], 1)
                for t in range(GT):
                    li, lj = over(lg[:, t, 0:NE], 2, NE), over(lg[:, t, 0:NE], 1, NE)
                    dv.tensor_tensor(cmp[:, t], lj, li, ALU.is_gt)
                    i = dv.tensor_tensor(cmq[:, t], lj, li, ALU.is_equal)
                i.then_inc(S["gt"], 1)

            def ties(g):
                dv.wait_ge(S["top1"], g + 1)
                dv.wait_ge(S["gt"], g + 1)
                dv.tensor_tensor(lg[:, :, 0:NE], lg[:, :, 0:NE], over(l1[:, :], 2, NE), ALU.subtract)\
                    .then_inc(S["shift_l"], 1)
                for t in range(GT):
                    i = dv.tensor_tensor(cmq[:, t], cmq[:, t], tri16[:, :, :], ALU.mult)
                i.then_inc(S["eqt"], 1)
                dv.wait_ge(S["eqt"], g + 1)
                dv.tensor_tensor(cmp.rearrange("p a b c -> p (a b c)"), cmp.rearrange("p a b c -> p (a b c)"),
                                 cmq.rearrange("p a b c -> p (a b c)"), ALU.add).then_inc(S["beats"], 1)

            def ranks(g):
                dv.wait_ge(S["beats"], g + 1)
                dv.tensor_reduce(rank[:, :, :], cmp, AX, ALU.add).then_inc(S["rank"], 1)

            def weights(g):
                dv.wait_ge(S["rank"], g + 1)
                dv.wait_ge(S["exp_l"], g + 1)
                dv.scalar_tensor_tensor(out=combn[:, :, 0:NE], in0=rank[:, :, :], scalar=2.0, in1=lg[:, :, 0:NE],
                                        op0=ALU.is_lt, op1=ALU.mult).then_inc(S["sel"], 1)
                dv.wait_ge(S["sel"], g + 1)
                dv.tensor_reduce(wsum[:, :], combn[:, :, 0:NE], AX, ALU.add).then_inc(S["selsum"], 1)
                dv.wait_ge(S["selsum"], 2 * g + 1)
                dv.reciprocal(wsum[:, :], wsum[:, :]).then_inc(S["selsum"], 1)
                dv.wait_ge(S["selsum"], 2 * g + 2)
                dv.tensor_tensor(combn[:, :, 0:NE], combn[:, :, 0:NE], over(wsum[:, :], 2, NE), ALU.mult)
                dv.wait_ge(S["expg"], g + 1)
                dv.tensor_scalar(combn[:, :, NE:NE + 1], combn[:, :, NE:NE + 1], 1.0, None, ALU.add).then_inc(S["cgate"], 1)
                dv.wait_ge(S["cgate"], g + 1)
                dv.reciprocal(combn[:, :, NE:NE + 1], combn[:, :, NE:NE + 1]).then_inc(S["comb"], 1)

            def e_hidden(g, e):
                rows = F_OF(e)
                dv.wait_ge(S["sg"], made(g, e, NB))
                dv.wait_ge(S["h_ps"], made(g, e, NB))
                dv.wait_ge(S["d_ps"], made(g, e - 2, NB))
                dv.tensor_tensor(hh[0:rows, e % 2, :], PS[0:rows, 2 + e % 2, :], sg[0:rows, e % 2, :], ALU.mult)\
                    .then_inc(S["hh"], 1)

            def e_acc(g, e):
                r = e % 2
                dv.wait_ge(S["d_ps"], made(g, e, NB))
                if e == 0:
                    dv.wait_ge(S["comb_in"], g + 1)
                if e:
                    dv.wait_ge(S["acc"], made(g, e - 1, NB - 1))
                for t in range(GT):
                    x = tile(X, g * GT + t)
                    w = min(e, NE)
                    i = dv.scalar_tensor_tensor(out=x, in0=PS[:, 4 + 2 * r + t // 2, (t % 2) * D:(t % 2 + 1) * D],
                                                scalar=comb[:, t, w:w + 1], in1=x, op0=ALU.mult, op1=ALU.add)
                    if e == NB - 1:
                        i.then_inc(S["x_done"], 1)
                if e < NB - 1:
                    i.then_inc(S["acc"], 1)

            dv.wait_ge(S["consts"], CONSTS)

            def e_body(g, more):
                dv.wait_ge(S["comb"], made(g))
                dv.wait_ge(S["x_done"], made(2 * NSEQ + g * GT - 1))
                dv.tensor_copy(comb[:, :, :], combn).then_inc(S["comb_in"], 1)
                for e in range(NB):
                    if e == STEP and more:
                        logits(g + 1)
                    if e + 1 < NB:
                        e_hidden(g, e + 1)
                    e_acc(g, e)
                    if more and e == STEP - 8:
                        group_stats(g + 1, g + 1)
                    if more and e == STEP - 4:
                        group_apply(g + 1, g + 1, 2 * NSEQ + (g + 1) * GT)
                    if not more and e == STEP - 8:
                        dv.wait_ge(S["x_done"], made(2 * NSEQ + GT - 1))
                        group_stats(NG, 0)
                    if not more and e == STEP - 4:
                        group_apply(NG, 0, 3 * NSEQ)
                    if more and STEP <= e < STEP + 4:
                        (compare, ties, ranks, weights)[e - STEP](g + 1)
                if more:
                    e_hidden(g + 1, 0)

            piped_by_two(dv, x_front, x_body)

            compare(0)
            e_hidden(0, 0)
            for step in (ties, ranks, weights):
                step(0)
            grouped(dv, None, e_body)

            def decays(g, t):
                cum = g_t1[t].rearrange("p c (n t) -> p c n t", n=NCB)
                mid = cum[:, :, :, CB // 2 - 1]
                dv.wait_ge(S["g_cum"], g * GT + t + 1)
                dv.tensor_tensor(g_zb[t].rearrange("p c (n t) -> p c n t", n=NCB), cum, over(mid, 3, CB),
                                 ALU.subtract).then_inc(S["g_dq"], 1)

            def scaled(g, t):
                dv.wait_ge(S["g_eq"], g * GT + t + 1)
                dv.wait_ge(S["g_qk"], g * GT + t + 1)
                for par in range(2):
                    rows = slice(par * P // 2, (par + 1) * P // 2)
                    k = dv.scalar_tensor_tensor(
                        out=g_qx[t][rows, :, :, par, :],
                        in0=g_qk[t][rows, 0:DC, :].rearrange("p c (n t) -> p c n t", n=NCB),
                        scalar=float(D // H1) ** -0.5,
                        in1=g_zb[t][rows].rearrange("p c (n t) -> p c n t", n=NCB), op0=ALU.mult, op1=ALU.mult)
                k.then_inc(S["g_qx"], 1)
                dv.wait_ge(S["g_ek"], g * GT + t + 1)
                for n in range(NCB):
                    k = dv.tensor_tensor(k_block(t, n), k_block(t, n), g_qk[t][:, DC:2 * DC, 0:CB * (n + 1)],
                                         ALU.mult)
                k.then_inc(S["g_kx"], 1)

            def log_decay(g, t):
                dv.wait_ge(S["g_ln"], g * GT + t + 1)
                dv.scalar_tensor_tensor(out=g_zb[t], in0=g_zb[t], scalar=0.0, in1=g_t1[t], op0=ALU.min,
                                        op1=ALU.subtract).then_inc(S["g_log"], 1)

            def summed(g, t):
                dv.wait_ge(S["g_log"], g * GT + t + 1)
                for c in range(DC):
                    k = dv.tensor_tensor_scan(g_t1[t][:, c, :], ones[:, :], g_zb[t][:, c, :], 0.0, ALU.mult, ALU.add)
                k.then_inc(S["g_cum"], 1)

            def attended(g, t):
                dv.wait_ge(S["consts"], CONSTS)
                dv.wait_ge(S["g_a_ps"], g * GT + t + 1)
                for n in range(NCB):
                    w, t0 = CB * (n + 1), CB * n
                    heads = PS[0:w, t, :].rearrange("p (c n r t) -> p c n r t", c=DC, n=NCB, r=2)
                    k = dv.copy_predicated(
                        g_at[t][0:w, :, :, t0:t0 + CB].rearrange("p r c t -> p c r t"),
                        over(over(trim[0:w, t0:t0 + CB], 1, 2), 1, DC).bitcast(mybir.dt.int32),
                        heads[:, :, n])
                k.then_inc(S["g_at"], 1)

            def mean_square(g, t):
                dv.wait_ge(S["g_ss"], g * GT + t + 1)
                dv.tensor_scalar(g_ss[:, t], g_ss[:, t], 1.0 / P, EPS, ALU.mult, ALU.add).then_inc(S["g_ve"], 1)

            def gated(g, t):
                dv.wait_ge(S["g_rr"], g * GT + t + 1)
                dv.wait_ge(S["g_gate"], g * GT + t + 1)
                for h in range(H1):
                    gate = g_gate[t][:, h * P:(h + 1) * P]
                    k = dv.scalar_tensor_tensor(out=gate, in0=PS[:, t, h * P:(h + 1) * P],
                                                scalar=g_rr[:, t, h:h + 1], in1=gate, op0=ALU.mult, op1=ALU.mult)
                k.then_inc(S["g_y"], 1)

            def l_body(g, more):
                if more:
                    group_stats(NG + g + 1, g + 1)
                    group_apply(NG + g + 1, g + 1, 3 * NSEQ + (g + 1) * GT)
                else:
                    dv.wait_ge(S["x_done"], made(3 * NSEQ + GT - 1))
                    group_stats(2 * NG, 0)
                    group_apply(2 * NG, 0, LAST)
                steps = (log_decay, summed, decays)
                for step_no in range(GT + len(steps) - 1):
                    for n, step in enumerate(steps):
                        if 0 <= step_no - n < GT:
                            step(g, step_no - n)
                for t in range(GT):
                    scaled(g, t)
                for t in range(GT):
                    attended(g, t)
                for t in range(GT + 1):
                    if t < GT:
                        mean_square(g, t)
                    if t:
                        gated(g, t - 1)
                for t in range(GT):
                    x = tile(X, g * GT + t)
                    dv.wait_ge(S["g_out_ps"], g * GT + t + 1)
                    dv.tensor_tensor(x, PS[:, 4 + t, 0:D], x, ALU.add).then_inc(S["x_done"], 1)

            dv.wait_ge(S["ld_m"], LD_M)
            dv.tensor_scalar(l_wo[:, :, :], l_wo[:, :, :], l_rms[:, 0:1], None, ALU.mult).then_inc(S["g_wo"], 1)
            dv.wait_ge(S["atz"], GT + 1)
            dv.wait_ge(S["consts"], CONSTS)
            grouped(dv, None, l_body)

            def m_context(g):
                for t in range(GT):
                    dv.tensor_copy(cn4[t], tile(C, g * GT + t)).then_inc(S["m_cn"], 1)
                    dv.tensor_scalar(m_hide[t], tile(pad4, g * GT + t).bitcast(U8), -BIG, None, ALU.mult)\
                        .then_inc(S["m_hide"], 1)

            def m_bias(g):
                dv.wait_ge(S["xn"], made(LAST + g * GT + GT - 1))
                dv.tensor_tensor(tiles(X, g), tiles(X, g), over(m_bo[:, :], 1, GT), ALU.add).then_inc(S["m_biased"], 1)

            def masked(g, t):
                dv.wait_ge(S["m_hide"], g * GT + t + 1)
                dv.wait_ge(S["m_s_ps"], g * GT + t + 1)
                dv.tensor_tensor(m_s[t], PS[:, t, 0:P], m_hide[t], ALU.add).then_inc(S["m_masked"], 1)

            def negated(g, t):
                dv.wait_ge(S["m_masked"], g * GT + t + 1)
                dv.tensor_scalar(m_s[t], m_s[t], -1.0, None, ALU.mult).then_inc(S["m_neg"], 1)

            def lowest(g, t):
                dv.wait_ge(S["m_neg"], g * GT + t + 1)
                dv.tensor_reduce(m_low[t], m_s[t], AX, ALU.min).then_inc(S["m_low"], 1)

            def m_body(g, more):
                steps = (masked, negated, lowest)
                for step_no in range(GT + len(steps) - 1):
                    for n, step in enumerate(steps):
                        if 0 <= step_no - n < GT:
                            step(g, step_no - n)
                if more:
                    group_apply(2 * NG + g + 1, g + 1, LAST + (g + 1) * GT)
                for t in range(GT):
                    dv.wait_ge(S["m_exp"], g * GT + t + 1)
                    dv.reciprocal(m_inv[t], m_sum[t]).then_inc(S["m_inv"], 1)
                for t in range(GT):
                    dv.wait_ge(S["m_inv"], g * GT + t + 1)
                    dv.wait_ge(S["m_o_ps"], g * GT + t + 1)
                    dv.tensor_scalar(m_o[t], PS[:, t, D:2 * D], m_inv[t], None, ALU.mult).then_inc(S["m_o"], 1)
                if more:
                    m_context(g + 1)
                    m_bias(g + 1)
                dv.wait_ge(S["m_biased"], g + 1)
                for t in range(GT + 1):
                    if t < GT:
                        x = tile(X, g * GT + t)
                        dv.wait_ge(S["m_out_ps"], g * GT + t + 1)
                        dv.tensor_tensor(x, PS[:, 4 + t, D:2 * D], x, ALU.add).then_inc(S["m_done"], 1)
                    if t:
                        dv.wait_ge(S["consts"], CONSTS)
                        dv.wait_ge(S["m_done"], g * GT + t)
                        k = dv.bn_stats(f_stats[:, t - 1, :], tile(X, g * GT + t - 1))
                k.then_inc(S["f_stats"], 1)
                dv.wait_ge(S["consts"], CONSTS)
                dv.wait_ge(S["f_stats"], g + 1)
                for t in range(GT):
                    k = dv.bn_aggr(f_mv[:, t, :], f_stats[:, t, :])
                k.then_inc(S["f_aggr"], 1)
                dv.wait_ge(S["f_aggr"], g + 1)
                dv.tensor_scalar(f_var[:, :], f_mv[:, :, 1], EPS, None, ALU.add).then_inc(S["f_var"], 1)
                dv.wait_ge(S["f_rstd"], g + 1)
                for t in range(GT):
                    dv.tensor_scalar(f_xn[t], tile(X, g * GT + t), f_mv[:, t, 0:1], f_rstd[:, t:t + 1],
                                     ALU.subtract, ALU.mult).then_inc(S["f_xn"], 1)
                dv.wait_ge(S["f_xn"], g * GT + GT)
                dv.tensor_tensor(tiles(X, g), tiles(X, g), over(f_b[:, :], 1, GT), ALU.add).then_inc(S["f_biased"], 1)
                if more > 1:
                    group_stats(2 * NG + g + 2, g + 2)
                dv.wait_ge(S["f_biased"], g + 1)
                for t in range(GT):
                    x = tile(X, g * GT + t)
                    dv.wait_ge(S["f_out_ps"], g * GT + t + 1)
                    dv.tensor_tensor(x, PS[:, t, D:2 * D], x, ALU.add).then_inc(S["x_done"], 1)

            dv.wait_ge(S["x_done"], made(4 * NSEQ - 1))
            m_context(0)
            m_bias(0)
            group_stats(2 * NG + 1, 1)
            grouped_by_two(dv, m_body)

_INS = ["x", "ctx_1024", "mask_S2_ff1", "mask_BxS2_bk0",
        "L0_attn_Wq", "L0_attn_Wk", "L0_attn_Wv", "L0_attn_Wo", "L0_attn_bo", "L0_attn_rel_emb",
        "L0_xattn_Wq", "L0_xattn_bq", "L0_xattn_Wk", "L0_xattn_bk", "L0_xattn_Wv", "L0_xattn_bv", "L0_xattn_Wo",
        "L0_xattn_bo",
        "L0_ffn_gate_w", "L0_ffn_w_gate_up", "L0_ffn_w_down", "L0_ffn_shared_w_gate", "L0_ffn_shared_w_up",
        "L0_ffn_shared_w_down", "L0_ffn_shared_gate_w",
        "L1_attn_Wq", "L1_attn_Wk", "L1_attn_Wv", "L1_attn_Wg", "L1_attn_Wgk1", "L1_attn_Wgk2", "L1_attn_bgk2",
        "L1_attn_Wout", "L1_attn_rms_w",
        "L1_xattn_Wq", "L1_xattn_bq", "L1_xattn_Wk", "L1_xattn_bk", "L1_xattn_Wo", "L1_xattn_bo",
        "L1_ffn_weight", "L1_ffn_alpha", "L1_ffn_bias"]

def kernel(**inputs):
    import numpy as _np
    import concourse.bacc as _bacc
    from concourse import mybir as _mybir
    from concourse.bass_utils import run_bass_kernel_spmd as _run

    nc = _bacc.Bacc("TRN2", target_bir_lowering=False, num_devices=1)
    arrays, aps = {}, {}
    for name in _INS:
        a = _np.ascontiguousarray(inputs[name])
        if a.dtype == _np.bool_:
            a = a.view(_np.int32)
        arrays[f"in_{name}"] = a
        aps[name] = nc.dram_tensor(f"in_{name}", a.shape, _mybir.dt.from_np(a.dtype), kind="ExternalInput").ap()
    out = nc.dram_tensor("out_0", (NSEQ, P, D), _mybir.dt.from_np(_np.dtype("float32")), kind="ExternalOutput").ap()
    build(nc, aps, out)
    r = _run(nc, [arrays], core_ids=[0])
    return r.results[0]["out_0"]
```
